# Optimizing a Trainium2 kernel written in Bass

```python
import numpy as np
import jax
import jax.numpy as jnp

def _softmax(x, axis=-1):
    return jax.nn.softmax(x, axis=axis)

def _gelu(x):
    return jax.nn.gelu(x, approximate=True)

def _silu(x):
    return jax.nn.silu(x)

def _sigmoid(x):
    return jax.nn.sigmoid(x)

def _layernorm(x, axis=-1, eps=1e-05):
    m = jnp.mean(x, axis=axis, keepdims=True)
    v = jnp.var(x, axis=axis, keepdims=True)
    return (x - m) / jnp.sqrt(v + eps)

def _scatter_add(tgt, idx, src, axis=0):
    return tgt.at[idx].add(src)

def _segment_sum(src, seg, n):
    return jax.ops.segment_sum(src, seg, n)
kernel_name = 'mk_adaln_attn_ffn_d1_seqx_r4_d80714'

def setup_inputs(seed: int=0):
    np.random.seed(seed)
    _w = jnp.asarray

    def _rec_inputs():
        import jax
        import jax.numpy as jnp
        _rk = jax.random.key(seed)
        x = -0.0003929 + 0.9999 * jax.random.normal(jax.random.fold_in(_rk, 1), (64, 64, 256), jnp.float32)
        _lenS = 64 - jax.random.randint(jax.random.fold_in(_rk, 7), (64,), 0, max(1, 64 // 4) + 1, jnp.int32)
        _lenS2 = 64 - jax.random.randint(jax.random.fold_in(_rk, 8), (64,), 0, max(1, 64 // 4) + 1, jnp.int32)
        itok_B_0_2 = jax.random.randint(jax.random.fold_in(_rk, 11), (64,), 0, 3, jnp.int32)
        itok_B_0_6 = jax.random.randint(jax.random.fold_in(_rk, 12), (64,), 0, 7, jnp.int32)
        return (x, itok_B_0_2, itok_B_0_6)
    x, itok_B_0_2, itok_B_0_6 = _rec_inputs()

    def _L0_cond_setup():
        import jax, jax.numpy as jnp
        import numpy as np
        NEG_INF = -1e+30
        key = jax.random.key(seed)
        k1, k2, k3, k4, k5 = jax.random.split(key, 5)
        B, S, D, A = (16, 256, 256, 64)
        hidden = jax.random.normal(k1, (B, S, D), dtype=jnp.float32)
        W1 = jax.random.normal(k2, (D, A), dtype=jnp.float32) / np.sqrt(D)
        b1 = jax.random.normal(k3, (A,), dtype=jnp.float32) * 0.01
        v = jax.random.normal(k4, (A,), dtype=jnp.float32) / np.sqrt(A)
        prompt_type_ids = jax.random.randint(k5, (B,), 0, 3, dtype=jnp.int32)
        return {'hidden': hidden, 'W1': W1, 'b1': b1, 'v': v, 'prompt_type_ids': prompt_type_ids}
    _L0_cond_all = _L0_cond_setup()
    _L0_cond_in = {k: v for k, v in _L0_cond_all.items() if k in ('W1', 'b1', 'v')}
    del _L0_cond_all

    def _L0_attn_setup():
        import jax, jax.numpy as jnp
        import numpy as np
        D_MODEL = 256
        N_HEADS = 16
        HEAD_DIM = D_MODEL // N_HEADS
        D_LATENT = 64
        LAMBDA_DECAY = 0.01
        TIME_STEP = 0.01
        CLAMP = 10000.0

        def _reference_tuple_inner(x, Wq, Wk, Wv, Wo, W_down_kv, W_up_k, W_up_v):
            B, S, _ = x.shape
            q = x @ Wq
            k = x @ Wk
            v = x @ Wv
            latent_kv = (k + v) @ W_down_kv
            k_rec = latent_kv @ W_up_k
            v_rec = latent_kv @ W_up_v

            def heads(t):
                return t.reshape(B, S, N_HEADS, HEAD_DIM).transpose(0, 2, 1, 3)
            qh, kh, vh = (heads(q), heads(k_rec), heads(v_rec))
            scale = 1.0 / (jnp.sqrt(jnp.float32(D_MODEL)) + 1e-08)
            scores = jnp.einsum('bhqd,bhkd->bhqk', qh, kh) * scale
            scores = jnp.clip(jnp.nan_to_num(scores, nan=-1000000000.0), -CLAMP, CLAMP)
            idx = jnp.arange(S, dtype=jnp.float32)
            decay = jnp.exp(-LAMBDA_DECAY * TIME_STEP * jnp.abs(idx[:, None] - idx[None, :]))
            scores = scores * decay[None, None, :, :]
            scores = jnp.clip(jnp.nan_to_num(scores, nan=-1000000000.0), -CLAMP, CLAMP)
            attn = jax.nn.softmax(scores, axis=-1)
            out = jnp.einsum('bhqk,bhkd->bhqd', attn, vh)
            out = out.transpose(0, 2, 1, 3).reshape(B, S, D_MODEL)
            return (out @ Wo, latent_kv)
        key = jax.random.key(seed)
        ks = jax.random.split(key, 8)
        B, S = (2, 512)

        def w(k, i, o):
            return jax.random.normal(k, (i, o), dtype=jnp.float32) * 0.02
        return {'x': jax.random.normal(ks[0], (B, S, D_MODEL), dtype=jnp.float32), 'Wq': w(ks[1], D_MODEL, D_MODEL), 'Wk': w(ks[2], D_MODEL, D_MODEL), 'Wv': w(ks[3], D_MODEL, D_MODEL), 'Wo': w(ks[4], D_MODEL, D_MODEL), 'W_down_kv': w(ks[5], D_MODEL, D_LATENT), 'W_up_k': w(ks[6], D_LATENT, D_MODEL), 'W_up_v': w(ks[7], D_LATENT, D_MODEL)}
    _L0_attn_all = _L0_attn_setup()
    _L0_attn_in = {k: v for k, v in _L0_attn_all.items() if k in ('Wq', 'Wk', 'Wv', 'Wo', 'W_down_kv', 'W_up_k', 'W_up_v')}
    del _L0_attn_all

    def _L0_cond2_setup():
        import jax, jax.numpy as jnp
        import numpy as np
        N_PROFILES = 8
        HIDDEN = 256
        BOTTLENECK = 128
        EPS = 1e-05
        key = jax.random.key(seed)
        ks = jax.random.split(key, 8)
        B, S, H, K, P = (16, 512, HIDDEN, BOTTLENECK, N_PROFILES)
        down_w = jax.random.normal(ks[0], (P, H, K), dtype=jnp.float32) * (1.0 / np.sqrt(H))
        down_b = jax.random.normal(ks[1], (P, K), dtype=jnp.float32) * 0.01
        up_w = jax.random.normal(ks[2], (P, K, H), dtype=jnp.float32) * (1.0 / np.sqrt(K))
        up_b = jax.random.normal(ks[3], (P, H), dtype=jnp.float32) * 0.01
        ln_g = jnp.ones((P, H), dtype=jnp.float32)
        ln_b = jnp.zeros((P, H), dtype=jnp.float32)
        hidden = jax.random.normal(ks[4], (B, S, H), dtype=jnp.float32)
        profile_ids = jax.random.randint(ks[5], (B,), 0, P)
        return {'hidden': hidden, 'profile_ids': profile_ids, 'down_w': down_w, 'down_b': down_b, 'up_w': up_w, 'up_b': up_b, 'ln_g': ln_g, 'ln_b': ln_b}
    _L0_cond2_all = _L0_cond2_setup()
    _L0_cond2_in = {k: v for k, v in _L0_cond2_all.items() if k in ('down_w', 'down_b', 'up_w', 'up_b', 'ln_g', 'ln_b')}
    del _L0_cond2_all

    def _L0_ffn_setup():
        import jax, jax.numpy as jnp
        import numpy as np
        E = 8
        K = 2
        D = 256
        H = 684
        B, S = (2, 512)

        def _moe_forward(x, centroid, Wg, bg, W1, b1, W2, b2):
            T = x.shape[0] * x.shape[1]
            xs = x.reshape(T, D)
            d2 = jnp.sum(xs * xs, axis=-1, keepdims=True) + jnp.sum(centroid * centroid, axis=-1)[None, :] - 2.0 * (xs @ centroid.T)
            dist = jnp.sqrt(jnp.maximum(d2, 1e-12))
            w, sel = jax.lax.top_k(dist, K)
            w = jax.nn.softmax(w.astype(jnp.float32), axis=1).astype(x.dtype)
            we = jnp.zeros((T, E), dtype=x.dtype).at[jnp.arange(T)[:, None], sel].add(w)
            out = jnp.zeros_like(xs)
            for e in range(E):
                h = jax.nn.silu(xs @ Wg[e] + bg[e]) * (xs @ W1[e] + b1[e])
                out = out + we[:, e:e + 1] * (h @ W2[e] + b2[e])
            return out.reshape(x.shape)
        key = jax.random.key(seed)
        ks = jax.random.split(key, 9)
        scale = 0.02
        return {'x': jax.random.normal(ks[0], (B, S, D), dtype=jnp.float32), 'centroid': jax.random.normal(ks[1], (E, D), dtype=jnp.float32), 'Wg': jax.random.normal(ks[2], (E, D, H), dtype=jnp.float32) * scale, 'bg': jnp.zeros((E, H), dtype=jnp.float32), 'W1': jax.random.normal(ks[3], (E, D, H), dtype=jnp.float32) * scale, 'b1': jnp.zeros((E, H), dtype=jnp.float32), 'W2': jax.random.normal(ks[4], (E, H, D), dtype=jnp.float32) * scale, 'b2': jnp.zeros((E, D), dtype=jnp.float32)}
    _L0_ffn_all = _L0_ffn_setup()
    _L0_ffn_in = {k: v for k, v in _L0_ffn_all.items() if k in ('centroid', 'Wg', 'bg', 'W1', 'b1', 'W2', 'b2')}
    del _L0_ffn_all
    return {'x': x, 'itok_B_0_2': itok_B_0_2, 'itok_B_0_6': itok_B_0_6, 'L0_cond_W1': _L0_cond_in['W1'], 'L0_cond_b1': _L0_cond_in['b1'], 'L0_cond_v': _L0_cond_in['v'], 'L0_attn_Wq': _L0_attn_in['Wq'], 'L0_attn_Wk': _L0_attn_in['Wk'], 'L0_attn_Wv': _L0_attn_in['Wv'], 'L0_attn_Wo': _L0_attn_in['Wo'], 'L0_attn_W_down_kv': _L0_attn_in['W_down_kv'], 'L0_attn_W_up_k': _L0_attn_in['W_up_k'], 'L0_attn_W_up_v': _L0_attn_in['W_up_v'], 'L0_cond2_down_w': _L0_cond2_in['down_w'], 'L0_cond2_down_b': _L0_cond2_in['down_b'], 'L0_cond2_up_w': _L0_cond2_in['up_w'], 'L0_cond2_up_b': _L0_cond2_in['up_b'], 'L0_cond2_ln_g': _L0_cond2_in['ln_g'], 'L0_cond2_ln_b': _L0_cond2_in['ln_b'], 'L0_ffn_centroid': _L0_ffn_in['centroid'], 'L0_ffn_Wg': _L0_ffn_in['Wg'], 'L0_ffn_bg': _L0_ffn_in['bg'], 'L0_ffn_W1': _L0_ffn_in['W1'], 'L0_ffn_b1': _L0_ffn_in['b1'], 'L0_ffn_W2': _L0_ffn_in['W2'], 'L0_ffn_b2': _L0_ffn_in['b2']}

def reference(x, itok_B_0_2, itok_B_0_6, L0_cond_W1, L0_cond_b1, L0_cond_v, L0_attn_Wq, L0_attn_Wk, L0_attn_Wv, L0_attn_Wo, L0_attn_W_down_kv, L0_attn_W_up_k, L0_attn_W_up_v, L0_cond2_down_w, L0_cond2_down_b, L0_cond2_up_w, L0_cond2_up_b, L0_cond2_ln_g, L0_cond2_ln_b, L0_ffn_centroid, L0_ffn_Wg, L0_ffn_bg, L0_ffn_W1, L0_ffn_b1, L0_ffn_W2, L0_ffn_b2):
    import jax
    import jax.numpy as jnp

    def _L0_cond_ref(hidden, W1, b1, v, prompt_type_ids):
        import jax, jax.numpy as jnp
        import numpy as np
        NEG_INF = -1e+30
        B, S, D = hidden.shape
        attn_in = jnp.tanh(jnp.einsum('bsd,da->bsa', hidden, W1) + b1)
        scores = jnp.einsum('bsa,a->bs', attn_in, v)
        idx = jnp.arange(S)
        j = idx[:, None]
        l = idx[None, :]
        prefix_m = l <= j
        postfix_m = l >= j
        cloze_m = l != j
        pt = prompt_type_ids[:, None, None]
        mask = jnp.where(pt == 0, prefix_m[None], jnp.where(pt == 1, postfix_m[None], cloze_m[None]))
        masked_scores = jnp.where(mask, scores[:, None, :], NEG_INF)
        p = jax.nn.softmax(masked_scores, axis=-1)
        cnt = jnp.sum(mask, axis=-1).astype(hidden.dtype)
        pooled = jnp.einsum('bjl,bld->bjd', p, hidden) / cnt[..., None]
        return pooled

    def _L0_attn_ref(x, Wq, Wk, Wv, Wo, W_down_kv, W_up_k, W_up_v):
        import jax, jax.numpy as jnp
        import numpy as np
        D_MODEL = 256
        N_HEADS = 16
        HEAD_DIM = D_MODEL // N_HEADS
        D_LATENT = 64
        LAMBDA_DECAY = 0.01
        TIME_STEP = 0.01
        CLAMP = 10000.0

        def _reference_tuple_inner(x, Wq, Wk, Wv, Wo, W_down_kv, W_up_k, W_up_v):
            B, S, _ = x.shape
            q = x @ Wq
            k = x @ Wk
            v = x @ Wv
            latent_kv = (k + v) @ W_down_kv
            k_rec = latent_kv @ W_up_k
            v_rec = latent_kv @ W_up_v

            def heads(t):
                return t.reshape(B, S, N_HEADS, HEAD_DIM).transpose(0, 2, 1, 3)
            qh, kh, vh = (heads(q), heads(k_rec), heads(v_rec))
            scale = 1.0 / (jnp.sqrt(jnp.float32(D_MODEL)) + 1e-08)
            scores = jnp.einsum('bhqd,bhkd->bhqk', qh, kh) * scale
            scores = jnp.clip(jnp.nan_to_num(scores, nan=-1000000000.0), -CLAMP, CLAMP)
            idx = jnp.arange(S, dtype=jnp.float32)
            decay = jnp.exp(-LAMBDA_DECAY * TIME_STEP * jnp.abs(idx[:, None] - idx[None, :]))
            scores = scores * decay[None, None, :, :]
            scores = jnp.clip(jnp.nan_to_num(scores, nan=-1000000000.0), -CLAMP, CLAMP)
            attn = jax.nn.softmax(scores, axis=-1)
            out = jnp.einsum('bhqk,bhkd->bhqd', attn, vh)
            out = out.transpose(0, 2, 1, 3).reshape(B, S, D_MODEL)
            return (out @ Wo, latent_kv)
        return _reference_tuple_inner(x, Wq, Wk, Wv, Wo, W_down_kv, W_up_k, W_up_v)[0]

    def _L0_cond2_ref(hidden, profile_ids, down_w, down_b, up_w, up_b, ln_g, ln_b):
        import jax, jax.numpy as jnp
        import numpy as np
        N_PROFILES = 8
        HIDDEN = 256
        BOTTLENECK = 128
        EPS = 1e-05
        Wd = down_w[profile_ids]
        bd = down_b[profile_ids][:, None]
        Wu = up_w[profile_ids]
        bu = up_b[profile_ids][:, None]
        g = ln_g[profile_ids][:, None]
        b = ln_b[profile_ids][:, None]
        z = jax.nn.relu(jnp.einsum('bsh,bhk->bsk', hidden, Wd) + bd)
        y = hidden + jnp.einsum('bsk,bkh->bsh', z, Wu) + bu
        mu = jnp.mean(y, axis=-1, keepdims=True)
        var = jnp.mean(jnp.square(y - mu), axis=-1, keepdims=True)
        return (y - mu) * jax.lax.rsqrt(var + EPS) * g + b

    def _L0_ffn_ref(x, centroid, Wg, bg, W1, b1, W2, b2):
        import jax, jax.numpy as jnp
        import numpy as np
        E = 8
        K = 2
        D = 256
        H = 684
        B, S = (2, 512)

        def _moe_forward(x, centroid, Wg, bg, W1, b1, W2, b2):
            T = x.shape[0] * x.shape[1]
            xs = x.reshape(T, D)
            d2 = jnp.sum(xs * xs, axis=-1, keepdims=True) + jnp.sum(centroid * centroid, axis=-1)[None, :] - 2.0 * (xs @ centroid.T)
            dist = jnp.sqrt(jnp.maximum(d2, 1e-12))
            w, sel = jax.lax.top_k(dist, K)
            w = jax.nn.softmax(w.astype(jnp.float32), axis=1).astype(x.dtype)
            we = jnp.zeros((T, E), dtype=x.dtype).at[jnp.arange(T)[:, None], sel].add(w)
            out = jnp.zeros_like(xs)
            for e in range(E):
                h = jax.nn.silu(xs @ Wg[e] + bg[e]) * (xs @ W1[e] + b1[e])
                out = out + we[:, e:e + 1] * (h @ W2[e] + b2[e])
            return out.reshape(x.shape)
        return _moe_forward(x, centroid, Wg, bg, W1, b1, W2, b2)
    x = x + _L0_attn_ref(_L0_cond_ref(x, L0_cond_W1, L0_cond_b1, L0_cond_v, itok_B_0_2), L0_attn_Wq, L0_attn_Wk, L0_attn_Wv, L0_attn_Wo, L0_attn_W_down_kv, L0_attn_W_up_k, L0_attn_W_up_v)
    x = x + _L0_ffn_ref(_L0_cond2_ref(x, itok_B_0_6, L0_cond2_down_w, L0_cond2_down_b, L0_cond2_up_w, L0_cond2_up_b, L0_cond2_ln_g, L0_cond2_ln_b), L0_ffn_centroid, L0_ffn_Wg, L0_ffn_bg, L0_ffn_W1, L0_ffn_b1, L0_ffn_W2, L0_ffn_b2)
    return x

_drawn_inputs = setup_inputs


def setup_inputs(seed=0):
    import zlib

    import numpy as np

    out = dict(_drawn_inputs(seed))
    spreads = {'L0_cond2_ln_g': (1.0, 0.558),
     'L0_cond2_ln_b': (0.0, 0.436),
     'L0_ffn_bg': (0.0, 0.8),
     'L0_ffn_b1': (0.0, 0.8),
     'L0_ffn_b2': (0.0, 0.275)}
    factors = {'L0_cond_W1': 8.0,
     'L0_cond_b1': 8.0,
     'L0_cond_v': 8.0,
     'L0_attn_Wq': 8.0,
     'L0_attn_Wk': 8.0,
     'L0_attn_Wv': 8.0,
     'L0_attn_Wo': 8.0,
     'L0_attn_W_down_kv': 8.0,
     'L0_attn_W_up_k': 8.0,
     'L0_attn_W_up_v': 8.0,
     'L0_cond2_down_b': 40.563,
     'L0_cond2_up_b': 38.981}
    for name, (base, spread) in spreads.items():
        noise = np.random.default_rng([zlib.crc32(name.encode()), seed]).standard_normal(out[name].shape)
        drawn = base * np.exp(spread * noise) if base else spread * noise
        out[name] = jnp.asarray(drawn.astype(out[name].dtype))
    for name, factor in factors.items():
        out[name] = (out[name] * factor).astype(out[name].dtype)
    return out
```

```python
import numpy as np
from contextlib import ExitStack

import concourse.bass as bass
from concourse import mybir

F32 = mybir.dt.float32
BF16 = mybir.dt.bfloat16
I32 = mybir.dt.int32
ALU = mybir.AluOpType
ACT = mybir.ActivationFunctionType
AX = mybir.AxisListType.X

P = 128
B, S, D = 64, 64, 256
T = B * S
KD = D // P
A = 64
L = 64
NH, DH = 16, 16
HP = NH // 2
NPAIR = T // P
UT = 2 * P
NUNIT = T // UT
VW = 2 * DH + 2
QSCALE = 1.0 / 16.0
CLAMP = 10000.0
DECAY = -0.01 * 0.01
FAR = 1.0e30


class Made:

    def __init__(self, sem, step=1):
        self.sem, self.step = sem, step

    def by(self, instruction):
        return instruction.then_inc(self.sem, self.step)

    def wait(self, eng, value):
        if isinstance(value, int) and value <= 0:
            return
        eng.wait_ge(self.sem, value)


def carry(pool, spare, carried, n):
    carried.wait(pool, n)
    carried.by(pool.tensor_tensor(spare[:, 1:2], spare[:, 0:1], spare[:, 0:1], ALU.add))


def setup_and_attention(nc, io, sb, made, dram, ps, ident, x1_dram, beside_pool=None):
    F0, F1, G, O, Spair, Tpair = (ps[k] for k in ("F0", "F1", "G", "O", "Spair", "Tpair"))
    qk_dram = dram("qk_dram", [2, 4, D, UT], BF16)

    w1 = sb("w1", [P, KD, A])
    b1 = sb("b1", [A, 1])
    v = sb("v", [A, 1])
    vrep = sb("vrep", [A, S])
    wq = sb("wq", [P, KD, D])
    wk = sb("wk", [P, KD, D])
    wv = sb("wv", [P, KD, D])
    wkvT = sb("wkvT", [P, KD, D])
    wdown = sb("wdown", [P, KD, L])
    wkvd = sb("wkvd", [P, KD, L])
    wuk = sb("wuk", [L, D])
    wuv = sb("wuv", [L, D])
    wo = sb("wo", [P, KD, D])
    types_i = sb("types_i", [P, B], I32)
    types = sb("types", [P, NPAIR])
    is_t = sb("is_t", [P, 3, NPAIR])
    diff = sb("diff", [P, S])
    shut = sb("shut", [P, 3, S])
    cap = sb("cap", [P, NPAIR, S])
    capt = sb("capt", [P, NPAIR, S])
    count = sb("count", [P, NPAIR])
    decay = sb("decay", [P, S])
    XU = sb("XU", [P, 2, 2, D])
    XT = sb("XT", [P, KD, UT])
    AT = sb("AT", [A, UT])
    SM = sb("SM", [P, 2, S])
    smx = sb("smx", [P, 2])
    ssum = sb("ssum", [P, 2])
    PB = sb("PB", [P, 2, P])
    PT = sb("PT", [P, 2, P])
    PO = sb("PO", [P, KD, UT])
    QK = sb("QK", [P, 4, KD, UT], BF16)
    LT = sb("LT", [L, 2, UT])
    QS = sb("QS", [3 * 32, 2, HP, UT], BF16)
    KS = sb("KS", [3 * 32, 2, HP, 2, UT], BF16)
    VB = sb("VB", [P, 2, 2, 2, HP, VW])
    W = sb("W", [P, 2, NH, S])
    rowmax = sb("rowmax", [P, 2, NH])
    PX = sb("PX", [P, 2, HP, P])
    rec = sb("rec", [P, HP, 2])
    ON = sb("ON", [P, HP, 2, DH])
    OT = sb("OT", [P, KD, P])
    XR = sb("XR", [P, 2, D])

    s_w = made("s_w", 16)
    s_c = made("s_c")
    s_v = made("s_v")
    s_a = made("s_a")
    s_p = made("s_p")

    loads = [
        (w1[:, :, :], io["L0_cond_W1"].rearrange("(k p) a -> p k a", p=P)),
        (b1[:, :], io["L0_cond_b1"].rearrange("(a o) -> a o", o=1)),
        (v[:, :], io["L0_cond_v"].rearrange("(a o) -> a o", o=1)),
        (types_i[:, :], io["itok_B_0_2"].rearrange("(o b) -> o b", o=1).partition_broadcast(P)
         if False else io["itok_B_0_2"].rearrange("(o b) -> o b", o=1).broadcast_to([P, B])),
        (wk[:, :, :], io["L0_attn_Wk"].rearrange("(k p) n -> p k n", p=P)),
        (wv[:, :, :], io["L0_attn_Wv"].rearrange("(k p) n -> p k n", p=P)),
        (wdown[:, :, :], io["L0_attn_W_down_kv"].rearrange("(k p) n -> p k n", p=P)),
        (wq[:, :, :], io["L0_attn_Wq"].rearrange("(k p) n -> p k n", p=P)),
        (wuk[:, :], io["L0_attn_W_up_k"]),
        (wuv[:, :], io["L0_attn_W_up_v"]),
        (wo[:, :, :], io["L0_attn_Wo"].rearrange("(k p) n -> p k n", p=P)),
    ]

    with nc.Block() as block:
        @block.sync
        def _(sp):
            for out, in_ in loads:
                s_w.by(sp.dma_start(out, in_))
            s_w.wait(sp, 16 * len(loads))

        @block.gpsimd
        def _(pool):
            n = [0]

            def step(instruction):
                s_c.by(instruction)
                n[0] += 1
                s_c.wait(pool, n[0])

            step(pool.memset(ident[:, :], 0.0))
            step(pool.affine_select(out=ident[:, :], in_=ident[:, :], compare_op=ALU.not_equal, fill=1.0,
                                    base=0, pattern=[[-1, P]], channel_multiplier=1))
            for h in range(2):
                step(pool.iota(diff[S * h:S * h + S, :], pattern=[[1, S]], base=0, channel_multiplier=-1,
                               allow_small_or_imprecise_dtypes=True))
            step(pool.memset(PB[:, :, :], 0.0))
            step(pool.memset(KS[:, :, :, :, :], 0.0))
            step(pool.memset(VB[:, :, :, :, :, :], 0.0))
            for half in range(2):
                col = 2 * DH + half
                step(pool.memset(VB[S * half:S * half + S, :, :, :, :, :].rearrange(
                    "p u s b h c -> p (u s b h) c")[:, :, col], 1.0))

        @block.vector
        def _(dve):
            n = [0]

            def step(instruction):
                s_v.by(instruction)
                n[0] += 1
                s_v.wait(dve, n[0])

            s_w.wait(dve, 16 * len(loads))
            s_c.wait(dve, 4)
            step(dve.memset(vrep[:, :], 1.0))
            step(dve.tensor_scalar(vrep[:, :], vrep[:, :], v[:, 0:1], None, ALU.mult))
            step(dve.tensor_tensor(wk[:, :, :], wk[:, :, :], wv[:, :, :], ALU.add))
            for h in range(2):
                rows = slice(S * h, S * h + S)
                step(dve.tensor_copy(types[rows, :], types_i[rows, :].rearrange("p (n b) -> p n b", b=2)[:, :, h]))
            step(dve.tensor_scalar(is_t[:, 0, :], types[:, :], 0.0, None, ALU.is_equal))
            step(dve.tensor_scalar(is_t[:, 1, :], types[:, :], 1.0, None, ALU.is_equal))
            step(dve.tensor_tensor(is_t[:, 2, :], is_t[:, 0, :], is_t[:, 1, :], ALU.add))
            step(dve.tensor_scalar(is_t[:, 2, :], is_t[:, 2, :], -1.0, 1.0, ALU.mult, ALU.add))
            for k, op in enumerate((ALU.is_gt, ALU.is_lt, ALU.is_equal)):
                step(dve.tensor_scalar(shut[:, k, :], diff[:, :], 0.0, None, op))
            wide = [P, NPAIR, S]
            for k in range(3):
                to = cap if k == 0 else capt
                step(dve.tensor_tensor(to[:, :, :], is_t[:, k, :].unsqueeze(2).broadcast_to(wide),
                                       shut[:, k, :].unsqueeze(1).broadcast_to(wide), ALU.mult))
                if k:
                    step(dve.tensor_tensor(cap[:, :, :], cap[:, :, :], capt[:, :, :], ALU.add))
            step(dve.tensor_reduce(count[:, :], cap[:, :, :], AX, ALU.add))
            step(dve.tensor_scalar(count[:, :], count[:, :], -1.0, float(S), ALU.mult, ALU.add))
            step(dve.tensor_scalar(cap[:, :, :], cap[:, :, :], -2.0 * FAR, FAR, ALU.mult, ALU.add))

        @block.scalar
        def _(act):
            s_c.wait(act, 4)
            s_a.by(act.activation(decay[:, :], diff[:, :], ACT.Abs))
            s_a.wait(act, 1)
            s_a.by(act.activation(decay[:, :], decay[:, :], ACT.Exp, scale=DECAY))
            for k in range(KD):
                s_p.wait(act, k + 1)
                s_a.by(act.activation(wkvT[:, k, :], F0[:, 0:D], ACT.Copy))
            s_p.wait(act, KD + 1)
            s_a.by(act.activation(wkvd[:, :, :], F1[:, 0:KD * L].rearrange("p (k l) -> p k l", k=KD), ACT.Copy))

        @block.tensor
        def _(pe):
            s_c.wait(pe, 2)
            s_v.wait(pe, 3)
            for k in range(KD):
                if k:
                    s_a.wait(pe, 2 + k)
                for m in range(KD):
                    last = pe.transpose(F0[:, m * P:(m + 1) * P], wk[:, m, k * P:(k + 1) * P], ident[:, :])
                s_p.by(last)
            s_a.wait(pe, 2 + KD)
            for m in range(KD):
                for k in range(KD):
                    last = pe.matmul(F1[:, m * L:(m + 1) * L], wkvT[:, k, m * P:(m + 1) * P], wdown[:, k, :],
                                     start=(k == 0), stop=(k == KD - 1))
            s_p.by(last)

    u_x = made("u_x", 16)
    names_u = ["xt_ps", "xt", "at_ps", "at", "sc_ps", "sc_a", "sc_b", "sc_c", "sc_e", "sc_f", "sc_g", "sc_h", "pb",
               "pt_ps", "pt", "po_ps", "po", "q_ps", "qhi", "qlo", "lt_ps", "lt", "k_ps", "khi", "klo",
               "v_ps", "vb0", "vb1"]
    U = {k: made("u_" + k, 2) for k in names_u}
    names_p = ["s_ps", "clip", "dec", "max", "sub", "t_ps0", "t_ps1", "px0", "px1", "o_ps", "rec", "on",
               "ot_ps", "ot", "g_ps", "x1"]
    R = {k: made("p_" + k) for k in names_p}
    u_qk_out = made("u_qk_out", 16)
    u_qs = made("u_qs", 16)
    p_xr = made("p_xr", 16)
    p_out = made("p_out", 16)

    LS, LT_, LV, LG = 2, 3, 4, 5

    def has_pair(n):
        return not isinstance(n, int) or 0 <= n < NPAIR

    def run(eng, body):
        first, last = 8, 28
        for t in range(-2, first):
            body(t, t % 4)
        with eng.Fori(first, last - 3, 4) as t:
            cache = {}
            for j in range(4):
                body(Slot(t, cache, eng) + j, j)
        for t in range(last, NPAIR + LG):
            body(t, t % 4)

    class Slot:

        def __init__(self, t, cache, eng, c=0):
            self.t, self.cache, self.eng, self.c = t, cache, eng, c

        def __add__(self, c):
            return Slot(self.t, self.cache, self.eng, self.c + c)

        def __sub__(self, c):
            return self + (-c)

        def reg(self):
            return self.t + self.c

    def val(x, mul=1):
        if isinstance(x, int):
            return x * mul
        return x.reg() * mul if mul != 1 else x.reg()

    def ge(eng, m, x, mul=1):
        if isinstance(x, int):
            if x > 0:
                eng.wait_ge(m.sem, x * mul)
            return
        eng.wait_ge(m.sem, val(x, mul))

    def on_unit(t, j, start):
        if (j - start) % 2:
            return None
        u2 = t - start
        if isinstance(u2, int) and not 0 <= u2 < 2 * NUNIT:
            return None
        return u2, ((j - start) // 2) % 2

    def pe_slot(pe, t, j):
        n = t - LG
        if has_pair(n):
            ge(pe, R["on"], n + 1)
            ge(pe, R["x1"], n)
            for m in range(KD):
                last = pe.transpose(G[:, m * P:(m + 1) * P],
                                    ON[:, :, :, :].rearrange("p h e d -> p (h e d)")[:, m * P:(m + 1) * P], ident[:, :])
            R["ot_ps"].by(last)
        n = t - LS
        if has_pair(n):
            up, h = (((j - LS) % 4) // 2), (j - LS) % 2
            if h == 0:
                ge(pe, u_qs, n + 2, 72)
            ge(pe, R["clip"], n)
            for b in range(2):
                c0 = h * P + b * S
                for hp in range(HP):
                    last = pe.matmul(Spair[S * b:S * b + S, hp * P:(hp + 1) * P], QS[:, up, hp, c0:c0 + S],
                                     KS[:, up, hp, :, c0:c0 + S], start=True, stop=True)
            R["s_ps"].by(last)
        n = t - LG
        if has_pair(n):
            ge(pe, R["ot"], n + 1)
            for m in range(KD):
                last = pe.matmul(G[:, D:2 * D], OT[:, m, :], wo[:, m, :], start=(m == 0), stop=(m == KD - 1))
            R["g_ps"].by(last)
        f = on_unit(t, j, 0)
        if f:
            u2, up = f
            ge(pe, U["po"], u2 + 2)
            ge(pe, U["pt"], u2 + 2)
            ge(pe, U["vb1"], u2 - 2)
            for m in range(KD):
                for k in range(KD):
                    last = pe.matmul(F0[:, m * UT:(m + 1) * UT], wq[:, k, m * P:(m + 1) * P], PO[:, k, :],
                                     start=(k == 0), stop=(k == KD - 1))
            U["q_ps"].by(last)
            for k in range(KD):
                last = pe.matmul(F1[0:L, 0:UT], wkvd[:, k, :], PO[:, k, :], start=(k == 0), stop=(k == KD - 1))
            U["lt_ps"].by(last)
        n = t - LT_
        if has_pair(n):
            w = W[:, (j - LT_) % 2, :, :].rearrange("p h s -> p (h s)")
            ge(pe, R["sub"], n + 1)
            for half in range(2):
                ge(pe, R[f"px{half}"], n)
                for hp in range(4 * half, 4 * half + 4):
                    last = pe.transpose(Tpair[:, hp * P:(hp + 1) * P], w[:, hp * P:(hp + 1) * P], ident[:, :])
                R[f"t_ps{half}"].by(last)
        f = on_unit(t, j, 0)
        if f:
            u2, up = f
            ge(pe, U["lt"], u2 + 2)
            ge(pe, U["qlo"], u2 + 2)
            for m in range(KD):
                last = pe.matmul(F0[:, m * UT:(m + 1) * UT], wuk[:, m * P:(m + 1) * P], LT[:, up, :],
                                 start=True, stop=True)
            U["k_ps"].by(last)
        f = on_unit(t, j, -2)
        if f:
            u2, up = f
            ge(pe, U["klo"], u2)
            ge(pe, u_x, u2 + 2, 8)
            for k in range(KD):
                for s in range(2):
                    last = pe.transpose(F0[:, k * UT + s * P:k * UT + (s + 1) * P], XU[:, up, s, k * P:(k + 1) * P],
                                        ident[:, :])
            U["xt_ps"].by(last)
        f = on_unit(t, j, -1)
        if f:
            u2, up = f
            ge(pe, U["pb"], u2 + 2)
            ge(pe, U["klo"], u2)
            for s in range(2):
                last = pe.transpose(F0[:, s * P:(s + 1) * P], PB[:, s, :], ident[:, :])
            U["pt_ps"].by(last)
        f = on_unit(t, j, -2)
        if f:
            u2, up = f
            ge(pe, U["xt"], u2 + 2)
            ge(pe, U["lt"], u2)
            for k in range(KD):
                last = pe.matmul(F1[0:A, 0:UT], w1[:, k, :], XT[:, k, :], start=(k == 0), stop=(k == KD - 1))
            U["at_ps"].by(last)
        n = t - LV
        if has_pair(n):
            up, h = (((j - LV) % 4) // 2), (j - LV) % 2
            ge(pe, R["px0"], n + 1)
            ge(pe, R["px1"], n + 1)
            if h == 0:
                ge(pe, U["vb0"], n + 2)
                ge(pe, U["vb1"], n + 2)
            ge(pe, R["on"], n)
            for b in range(2):
                if b and f:
                    ge(pe, U["at"], f[0] + 2)
                for hp in range(HP):
                    last = pe.matmul(O[S * b:S * b + S, hp * VW:(hp + 1) * VW], PX[:, h, hp, S * b:S * b + S],
                                     VB[:, up, h, b, hp, :], start=True, stop=True)
            R["o_ps"].by(last)
        f = on_unit(t, j, -2)
        if f:
            if not has_pair(n):
                ge(pe, U["at"], f[0] + 2)
            for b in range(2):
                last = pe.matmul(F1[S * b:S * b + S, UT:UT + P].rearrange("p (s l) -> p s l", s=2), vrep[:, :],
                                 AT[:, :].rearrange("a (s b l) -> a s b l", s=2, b=2)[:, :, b, :],
                                 start=True, stop=True)
            U["sc_ps"].by(last)
        f = on_unit(t, j, -1)
        if f:
            u2, up = f
            ge(pe, U["pt"], u2 + 2)
            ge(pe, U["sc_a"], u2 + 2)
            for k in range(KD):
                for s in range(2):
                    last = pe.matmul(F1[:, k * UT + s * P:k * UT + (s + 1) * P], XU[:, up, s, k * P:(k + 1) * P],
                                     PT[:, s, :], start=True, stop=True)
            U["po_ps"].by(last)
        f = on_unit(t, j, 3)
        if f:
            u2, up = f
            ge(pe, U["po"], min(u2 + 6, 2 * NUNIT) if isinstance(u2, int) else u2 + 6)
            for s in range(2):
                last = pe.matmul(F1[:, s * D:(s + 1) * D], LT[:, up, s * P:(s + 1) * P], wuv[:, :],
                                 start=True, stop=True)
            U["v_ps"].by(last)

    def act_slot(act, t, j):
        n = t - LG
        if has_pair(n):
            ge(act, R["ot_ps"], n + 1)
            R["ot"].by(act.activation(OT[:, :, :], G[:, 0:KD * P].rearrange("p (k t) -> p k t", k=KD), ACT.Copy))
        f = on_unit(t, j, 0)
        if f:
            u2, up = f
            ge(act, U["q_ps"], u2 + 2)
            ge(act, u_qk_out, u2, 32)
            U["qhi"].by(act.activation(QK[:, 0, :, :], F0[:, :].rearrange("p (k t) -> p k t", k=KD), ACT.Copy,
                                       scale=QSCALE))
            ge(act, U["lt_ps"], u2 + 2)
            ge(act, U["v_ps"], u2 - 2)
            U["lt"].by(act.activation(LT[:, up, :], F1[0:L, 0:UT], ACT.Copy))
        n = t - LT_
        if has_pair(n):
            for half in range(2):
                ge(act, R[f"t_ps{half}"], n + 1)
                ge(act, R["o_ps"], n - 1)
                R[f"px{half}"].by(act.activation(
                    PX[:, (j - LT_) % 2, 4 * half:4 * half + 4, :],
                    Tpair[:, 512 * half:512 * half + 512].rearrange("p (h t) -> p h t", h=4), ACT.Exp))
        f = on_unit(t, j, 0)
        if f:
            u2, up = f
            ge(act, U["k_ps"], u2 + 2)
            U["khi"].by(act.activation(QK[:, 2, :, :], F0[:, :].rearrange("p (k t) -> p k t", k=KD), ACT.Copy))
        f = on_unit(t, j, -2)
        if f:
            u2, up = f
            ge(act, U["xt_ps"], u2 + 2)
            U["xt"].by(act.activation(XT[:, :, :], F0[:, :].rearrange("p (k t) -> p k t", k=KD), ACT.Copy))
            ge(act, U["at_ps"], u2 + 2)
            U["at"].by(act.activation(AT[:, :], F1[0:A, 0:UT], ACT.Tanh, bias=b1[:, 0:1]))
            ge(act, U["sc_c"], u2 + 2)
            U["sc_e"].by(act.activation(SM[:, :, :], SM[:, :, :], ACT.Exp))
        f = on_unit(t, j, -1)
        if f:
            u2, up = f
            ge(act, U["pt_ps"], u2 + 2)
            U["pt"].by(act.activation(PT[:, :, :], F0[:, 0:UT].rearrange("p (s t) -> p s t", s=2), ACT.Copy))
            ge(act, U["po_ps"], u2 + 2)
            U["po"].by(act.activation(PO[:, :, :], F1[:, :].rearrange("p (k t) -> p k t", k=KD), ACT.Copy))
        f = on_unit(t, j, 3)
        if f:
            u2, up = f
            ge(act, U["v_ps"], u2 + 2)
            ge(act, R["o_ps"], u2 - 2)
            for e in range(2):
                for b in range(2):
                    last = act.activation(
                        VB[S * e:S * e + S, up, :, b, :, e * DH:(e + 1) * DH],
                        F1[S * b:S * b + S, :].rearrange("p (s h e d) -> p s h e d", s=2, h=HP, e=2)[:, :, :, e, :],
                        ACT.Copy)
                U[f"vb{e}"].by(last)

    def dve_slot(dve, t, j):
        n = t - LG
        if has_pair(n):
            par = (j - LG) % 2
            ge(dve, R["g_ps"], n + 1)
            ge(dve, p_xr, n + 1, 16)
            R["x1"].by(dve.tensor_tensor(XR[:, par, :], XR[:, par, :], G[:, D:2 * D], ALU.add))
        n = t - LS
        if has_pair(n):
            par = (j - LS) % 2
            w = W[:, par, :, :]
            flat = w.rearrange("p h s -> p (h s)")
            ge(dve, R["s_ps"], n + 1)
            ge(dve, R["t_ps1"], n - 1)
            R["clip"].by(dve.tensor_scalar(flat, Spair[:, :], -CLAMP, CLAMP, ALU.max, ALU.min))
        f = on_unit(t, j, 0)
        if f:
            u2, up = f
            ge(dve, U["qhi"], u2 + 2)
            U["qlo"].by(dve.scalar_tensor_tensor(
                out=QK[:, 1, :, :].rearrange("p k t -> p (k t)"), in0=F0[:, :], scalar=QSCALE,
                in1=QK[:, 0, :, :].rearrange("p k t -> p (k t)"), op0=ALU.mult, op1=ALU.subtract))
        n = t - LS
        if has_pair(n):
            ge(dve, R["clip"], n + 1)
            R["dec"].by(dve.tensor_tensor(w, w, decay[:, :].unsqueeze(1).broadcast_to([P, NH, S]), ALU.mult))
            ge(dve, R["dec"], n + 1)
            R["max"].by(dve.tensor_reduce(rowmax[:, par, :], w, AX, ALU.max))
            ge(dve, R["max"], n + 1)
            R["sub"].by(dve.tensor_tensor(w, w, rowmax[:, par, :].unsqueeze(2).broadcast_to([P, NH, S]),
                                          ALU.subtract))
        f = on_unit(t, j, 0)
        if f:
            u2, up = f
            ge(dve, U["khi"], u2 + 2)
            U["klo"].by(dve.tensor_tensor(QK[:, 3, :, :].rearrange("p k t -> p (k t)"), F0[:, :],
                                          QK[:, 2, :, :].rearrange("p k t -> p (k t)"), ALU.subtract))
        n = t - LV
        if has_pair(n):
            o = O[:, 0:HP * VW].rearrange("p (h c) -> p h c", h=HP)
            ge(dve, R["o_ps"], n + 1)
            R["rec"].by(dve.reciprocal(rec[:, :, :], o[:, :, 2 * DH:VW]))
            ge(dve, R["rec"], n + 1)
            ge(dve, R["ot_ps"], n)
            R["on"].by(dve.tensor_tensor(ON[:, :, :, :], o[:, :, 0:2 * DH].rearrange("p h (e d) -> p h e d", e=2),
                                         rec[:, :, :].unsqueeze(3).broadcast_to([P, HP, 2, DH]), ALU.mult))
        f = on_unit(t, j, -2)
        if f:
            u2, up = f
            ge(dve, U["sc_ps"], u2 + 2)
            caps = cap[:, u2:u2 + 2, :] if isinstance(u2, int) else cap[:, bass.ds(u2.reg(), 2), :]
            U["sc_a"].by(dve.tensor_tensor(SM[:, :, :], F1[:, UT:UT + P].rearrange("p (s l) -> p s l", s=2), caps,
                                           ALU.min))
            ge(dve, U["sc_a"], u2 + 2)
            U["sc_b"].by(dve.tensor_reduce(smx[:, :], SM[:, :, :], AX, ALU.max))
            ge(dve, U["sc_b"], u2 + 2)
            U["sc_c"].by(dve.tensor_tensor(SM[:, :, :], SM[:, :, :], smx[:, :].unsqueeze(2).broadcast_to([P, 2, S]),
                                           ALU.subtract))
            cnts = count[:, u2:u2 + 2] if isinstance(u2, int) else count[:, bass.ds(u2.reg(), 2)]
            ge(dve, U["sc_e"], u2 + 2)
            U["sc_f"].by(dve.tensor_reduce(ssum[:, :], SM[:, :, :], AX, ALU.add))
            ge(dve, U["sc_f"], u2 + 2)
            U["sc_g"].by(dve.tensor_tensor(ssum[:, :], ssum[:, :], cnts, ALU.mult))
            ge(dve, U["sc_g"], u2 + 2)
            U["sc_h"].by(dve.reciprocal(ssum[:, :], ssum[:, :]))
            ge(dve, U["sc_h"], u2 + 2)
            ge(dve, U["pt_ps"], u2)
            for b in range(2):
                rows = slice(S * b, S * b + S)
                last = dve.tensor_tensor(PB[rows, :, S * b:S * b + S], SM[rows, :, :],
                                         ssum[rows, :].unsqueeze(2).broadcast_to([S, 2, S]), ALU.mult)
            U["pb"].by(last)

    x_rows = io["x"].rearrange("b s d -> (b s) d")

    def sp_slot(sp, t, j):
        f = on_unit(t, j, -4)
        if f:
            u2, up = f
            ge(sp, U["po_ps"], u2 - 2)
            ge(sp, u_x, u2, 8)
            rows = bass.ds(val(u2, P), UT)
            u_x.by(sp.dma_start(XU[:, up, :, :], x_rows[rows, :].rearrange("(s p) d -> p s d", p=P)))
        f = on_unit(t, j, 0)
        if f:
            u2, up = f
            ge(sp, u_qs, u2 - 2, 72)
            for i, k in enumerate(("qhi", "qlo", "khi", "klo")):
                ge(sp, U[k], u2 + 2)
                u_qk_out.by(sp.dma_start(qk_dram[up, i].rearrange("(k p) t -> p k t", p=P), QK[:, i, :, :]))
        f = on_unit(t, j, 1)
        if f:
            u2, up = f
            ge(sp, u_qk_out, u2 + 2, 32)
            ge(sp, R["s_ps"], u2 - 2)
            for part, (qi, ki) in enumerate(((0, 2), (0, 3), (1, 2))):
                rows = slice(32 * part, 32 * part + 32)
                u_qs.by(sp.dma_start(QS[rows, up, :, :], qk_dram[up, qi].rearrange("(h p) t -> p h t", p=32)))
                for e in range(2):
                    r0 = 32 * part + DH * e
                    u_qs.by(sp.dma_start(KS[r0:r0 + DH, up, :, e, :], qk_dram[up, ki].rearrange(
                        "(h e p) t -> e p h t", e=2, p=DH)[e]))
        n = t - LV
        if has_pair(n):
            par = (j - LV) % 2
            ge(sp, p_xr, n, 16)
            ge(sp, p_out, n - 1, 16)
            p_xr.by(sp.dma_start(XR[:, par, :], x_rows[bass.ds(val(n, P), P), :]))
        n = t - LG
        if has_pair(n):
            par = (j - LG) % 2
            ge(sp, R["x1"], n + 1)
            p_out.by(sp.dma_start(x1_dram[bass.ds(val(n, P), P), :], XR[:, par, :]))

    with nc.Block() as block:
        @block.tensor
        def _(pe):
            run(pe, lambda t, j: pe_slot(pe, t, j))

        @block.scalar
        def _(act):
            run(act, lambda t, j: act_slot(act, t, j))

        @block.vector
        def _(dve):
            run(dve, lambda t, j: dve_slot(dve, t, j))

        @block.sync
        def _(sp):
            sp_slot(sp, -4, 0)
            run(sp, lambda t, j: sp_slot(sp, t, j))
            ge(sp, p_out, NPAIR, 16)

        if beside_pool:
            @block.gpsimd
            def _(pool):
                beside_pool(pool)


NP_ = 8
BN = 128
E = 8
GT = 4
GROUP = GT * P
NGROUP = T // GROUP
FT = 256
CAP = T + FT
META = 4
RW = D + META
NTILE = 2 * T // FT + E - 1
NTILE += NTILE % 2
SPARE = E * CAP
NOWHERE = float(1 << 20)
EPS = 1e-5


def dispatch(nc, io, sb, made, dram, ps, ident, x1_dram, xs_dram, table_i, table_f):
    F0, F1, G, O, Spair, Tpair = (ps[k] for k in ("F0", "F1", "G", "O", "Spair", "Tpair"))
    prof_i = sb("prof_i", [P, B], I32)
    prof = sb("prof", [P, B])
    row_of = sb("row_of", [P, 1])
    onehot = sb("onehot", [P, B], BF16)
    raw = sb("raw", [32, 3 * D + BN])
    rest = sb("rest", [32, 3 * D + BN])
    parts = sb("parts", [3 * 32, 3 * D + BN], BF16)
    ohg = sb("ohg", [3 * 32, 2 * GT, S], BF16)
    cent = sb("cent", [E, D])
    centT = sb("centT", [P, KD, E])
    c2 = sb("c2", [P, E])
    cbc = sb("cbc", [P, E, D])
    upper = sb("upper", [P, P], BF16)
    ones = sb("ones", [P, P], BF16)
    rev = sb("rev", [P, E])
    ramp = sb("ramp", [P, NTILE])
    steps = sb("steps", [P, T // FT])
    tok = sb("tok", [P, GT])
    ce = sb("ce", [P, E])
    ce_i = sb("ce_i", [P, E], I32)
    pad = sb("pad", [P, 2, RW])
    spare = sb("spare", [P, 2])
    X1 = sb("X1", [P, 2, GT, D])
    XT = sb("X1T", [P, KD, GROUP])
    WD = sb("WD", [P, 2 * GT, KD, BN])
    WU = sb("WU", [P, 2 * GT, D])
    ZT = sb("ZT", [BN, GROUP])
    Y = sb("Y", [P, GT, D])
    bst = sb("bst", [P, GT, 6])
    mv = sb("mv", [P, GT, 2])
    std = sb("std", [P, GT])
    rstd = sb("rstd", [P, GT])
    ROW = sb("ROW", [P, 2, GT, RW])
    HT = sb("HT", [P, KD, GROUP])
    sq = sb("sq", [P, D])
    x2 = sb("x2", [P, GT])
    small = [P, GT, E]
    d2, eq, tmp, ohlo, ohhi = (sb(n, small) for n in ("d2", "eq", "tmp", "ohlo", "ohhi"))
    m12 = sb("m12", [P, 2, GT])
    s12 = sb("s12", [P, 2, GT])
    r12 = sb("r12", [P, 2, GT])
    first = sb("first", [P, GT])
    ex = sb("ex", [P, GT])
    w12 = sb("w12", [P, 2, GT])
    oh1 = sb("oh1", small)
    oh2 = sb("oh2", small)
    M = sb("M", small, BF16)
    pos = sb("pos", [P, 2, GT])
    idx = sb("idx", [P, 2, 2, GT], I32)
    nt = sb("nt", [P, E])
    cnt = sb("cnt", [P, E])
    incl = sb("incl", [P, E])
    zero8 = sb("zero8", [P, E])
    big = sb("big", [P, NTILE, E])
    big2 = sb("big2", [P, E, T // FT])
    sumt = sb("sumt", [P, NTILE])

    c_w, c_c, c_v, c_a, c_p, c_r = made("c_w", 16), made("c_c"), made("c_v"), made("c_a"), made("c_p"), made("c_r", 16)
    tables = ("L0_cond2_up_b", "L0_cond2_ln_g", "L0_cond2_ln_b", "L0_cond2_down_b")
    loads = [(prof_i[:, :], io["itok_B_0_6"].rearrange("(o b) -> o b", o=1).broadcast_to([P, B])),
             (cent[:, :], io["L0_ffn_centroid"]),
             (cbc[:, :, :], io["L0_ffn_centroid"].rearrange("(o e) d -> o e d", o=1).broadcast_to([P, E, D]))]
    late = [(raw[0:NP_, i * D:i * D + (BN if i == 3 else D)], io[k]) for i, k in enumerate(tables)]
    NW = len(loads) + len(late)
    with nc.Block() as block:
        @block.sync
        def _(sp):
            for o, i in loads:
                c_w.by(sp.dma_start(o, i))
            c_c.wait(sp, 1)
            for o, i in late:
                c_w.by(sp.dma_start(o, i))
            c_c.wait(sp, 9)
            for s in range(2):
                c_r.by(sp.dma_start(xs_dram[SPARE + s * P:SPARE + (s + 1) * P, :], pad[:, s, :]))
            c_r.wait(sp, 32)

        @block.gpsimd
        def _(pool):
            n = [0]

            def step(instruction):
                c_c.by(instruction)
                n[0] += 1
                c_c.wait(pool, n[0])

            step(pool.memset(raw[:, :], 0.0))
            for i in range(4):
                step(pool.iota(row_of[32 * i:32 * i + 32, :], pattern=[[0, 1]], base=0, channel_multiplier=1,
                               allow_small_or_imprecise_dtypes=True))
            step(pool.memset(ones[:, :], 1.0))
            step(pool.memset(pad[:, :, :], 0.0))
            step(pool.memset(pad[:, :, D + 2:D + 3], NOWHERE))
            pool.memset(spare[:, :], 0.0)
            step(pool.memset(zero8[:, :], 0.0))
            step(pool.affine_select(out=upper[:, :], in_=ones[:, :], compare_op=ALU.is_gt, fill=0.0, base=0,
                                    pattern=[[1, P]], channel_multiplier=-1))
            step(pool.iota(rev[:, :], pattern=[[-1, E]], base=E, channel_multiplier=0,
                           allow_small_or_imprecise_dtypes=True))
            step(pool.iota(ramp[:, :], pattern=[[1, NTILE]], base=0, channel_multiplier=0,
                           allow_small_or_imprecise_dtypes=True))
            step(pool.iota(steps[:, :], pattern=[[FT, T // FT]], base=0, channel_multiplier=0,
                           allow_small_or_imprecise_dtypes=True))
            step(pool.iota(tok[:, :], pattern=[[P, GT]], base=-GROUP, channel_multiplier=1,
                           allow_small_or_imprecise_dtypes=True))
            step(pool.iota(ce[:, :], pattern=[[CAP, E]], base=0, channel_multiplier=0,
                           allow_small_or_imprecise_dtypes=True))
            c_w.wait(pool, 16 * NW)
            step(pool.tensor_tensor(cbc[:, :, :], cbc[:, :, :], cbc[:, :, :], ALU.mult))

        @block.vector
        def _(dve):
            n = [0]

            def step(instruction):
                c_v.by(instruction)
                n[0] += 1
                c_v.wait(dve, n[0])

            c_w.wait(dve, 16 * NW)
            c_c.wait(dve, 15)
            step(dve.tensor_copy(prof[:, :], prof_i[:, :]))
            step(dve.tensor_scalar(onehot[:, :], prof[:, :], row_of[:, 0:1], None, ALU.is_equal))
            step(dve.tensor_copy(parts[0:32, :], raw[:, :]))
            step(dve.tensor_tensor(rest[:, :], raw[:, :], parts[0:32, :], ALU.subtract))
            step(dve.tensor_copy(parts[32:64, :], rest[:, :]))
            step(dve.tensor_tensor(rest[:, :], rest[:, :], parts[32:64, :], ALU.subtract))
            step(dve.tensor_copy(parts[64:96, :], rest[:, :]))
            c_c.wait(dve, 16)
            step(dve.tensor_reduce(c2[:, :], cbc[:, :, :], AX, ALU.add))
            c_p.wait(dve, 1)
            step(dve.tensor_scalar(centT[:, :, :], F0[:, 0:KD * E].rearrange("p (k e) -> p k e", k=KD), -2.0, None,
                                   ALU.mult))

        @block.tensor
        def _(pe):
            c_w.wait(pe, 16 * NW)
            for k in range(KD):
                last = pe.transpose(F0[:, k * E:(k + 1) * E], cent[:, k * P:(k + 1) * P], ident[0:E, 0:E])
            c_p.by(last)

    x1_in = [made(f"x1_in{j}", 16) for j in range(2)]
    w_in = made("w_in", 16)
    names = ["xT_ps", "xT", "ohg", "z_ps", "zt", "y_ps", "y", "bst", "mv", "std", "rstd", "veps",
             "gb_ps0", "gb_ps1", "hn", "hg0", "hg1", "hb0", "hb1",
             "hT_ps", "hT", "x2", "dot_ps", "d2a", "d2b", "d2", "m1", "eq1", "eqr1", "r1", "oh1", "d2m",
             "m2", "eq2", "eqr2", "r2", "oh2", "s12", "dif", "ex", "den", "rden", "w2", "first", "wd", "wf", "wlo", "whi",
             "rlo", "M", "ohlo", "ohhi", "rank_ps", "rank", "plo", "phi", "tlo", "idx", "ce", "tok", "tokw", "t2"]
    chains = [("d2b", "d2", "m1", "eq1"), ("eqr1", "r1", "oh1", "d2m"), ("eq2", "eqr2", "r2", "oh2"),
              ("rlo", "ohlo", "den", "rden"), ("tok", "w2", "wd", "wf"), ("wlo", "whi", "tokw", "plo"),
              ("first", "tlo", "t2", "phi")]
    C = {k: made("c_" + k) for k in names if not any(k in c for c in chains)}
    place = {}
    for c in chains:
        C.update(dict.fromkeys(c, made("c_" + "_".join(c))))
        place.update((k, n) for n, k in enumerate(c))
    carried = made("dispatch_carried")
    rows_out = [made(f"rows_out{j}", 16) for j in range(2)]

    def ge(eng, m, x, mul=1):
        if isinstance(x, int):
            if x > 0:
                eng.wait_ge(m.sem, x * mul)
        else:
            eng.wait_ge(m.sem, x * mul if mul != 1 else x)

    def run(eng, body):
        for g in range(3):
            body(g, g % 2)
        with eng.Fori(3, NGROUP - 2, 2) as g:
            for j in range(2):
                body(g + j, (1 + j) % 2)
        body(NGROUP - 1, (NGROUP - 1) % 2)
        body(NGROUP, NGROUP % 2)

    def front(g):
        return not isinstance(g, int) or g < NGROUP

    def back(g):
        return not isinstance(g, int) or g > 0

    def pe_slot(pe, g, j):
        if front(g):
            ge(pe, x1_in[j], g + 2 - j, 8)
            ge(pe, C["hT"], g - 1)
            for k in range(KD):
                for s in range(GT):
                    last = pe.transpose((F0, F1)[k][:, s * P:(s + 1) * P], X1[:, j, s, k * P:(k + 1) * P], ident[:, :])
            C["xT_ps"].by(last)
            ge(pe, C["ohg"], g + 1)
            ge(pe, C["zt"], g)
            pe.matmul(G[:, :], parts[:, 3 * D:3 * D + BN], ohg[:, :, :].rearrange("r b s -> r (b s)"),
                      start=True, stop=False, skip_group_check=True)
            ge(pe, C["xT"], g + 1)
            ge(pe, w_in, g + 1, 16 * 4 * GT)
            for b in range(2 * GT):
                for k in range(KD):
                    last = pe.matmul(G[:, b * S:(b + 1) * S], WD[:, b, k, :], XT[:, k, b * S:(b + 1) * S],
                                     start=False, stop=(k == KD - 1), skip_group_check=True)
            C["z_ps"].by(last)
        if back(g):
            ge(pe, C["hb1"], g)
            if not front(g):
                pass
            else:
                ge(pe, C["xT"], g + 1)
            for k in range(KD):
                for s in range(GT):
                    last = pe.transpose((F0, F1)[k][:, s * P:(s + 1) * P], ROW[:, 1 - j, s, k * P:(k + 1) * P],
                                        ident[:, :])
            C["hT_ps"].by(last)
        if front(g):
            ge(pe, C["zt"], g + 1)
            ge(pe, C["y"], g)
            for s in range(GT):
                at = Spair[:, s * D:(s + 1) * D]
                pe.matmul(at, ohg[:, 2 * s:2 * s + 2, :].rearrange("r b s -> r (b s)"), parts[:, 0:D],
                          start=True, stop=False, skip_group_check=True)
                for h in range(2):
                    b = 2 * s + h
                    last = pe.matmul(Spair[S * h:S * h + S, s * D:(s + 1) * D], ZT[:, b * S:(b + 1) * S], WU[:, b, :],
                                     start=False, stop=True, skip_group_check=True)
            C["y_ps"].by(last)
        if back(g):
            ge(pe, C["hT"], g)
            ge(pe, C["ce"], g - 1)
            for s in range(GT):
                for k in range(KD):
                    last = pe.matmul(O[:, s * E:(s + 1) * E], HT[:, k, s * P:(s + 1) * P], centT[:, k, :],
                                     start=(k == 0), stop=(k == KD - 1))
            C["dot_ps"].by(last)
        if front(g):
            for half in range(2):
                if half == 0:
                    ge(pe, C["hb1"], g)
                for s in range(2 * half, 2 * half + 2):
                    last = pe.matmul(Tpair[:, (s % 2) * 512:(s % 2) * 512 + 512],
                                     ohg[:, 2 * s:2 * s + 2, :].rearrange("r b s -> r (b s)"), parts[:, D:3 * D],
                                     start=True, stop=True)
                C[f"gb_ps{half}"].by(last)
                if half == 0:
                    ge(pe, C["hb0"], g + 1)
        if back(g):
            ge(pe, C["M"], g)
            ge(pe, C["d2a"], g)
            at = O[:, 64:64 + GT * E]
            for s in range(GT):
                last = pe.matmul(at[:, s * E:(s + 1) * E], upper[:, :], M[:, s, :], start=True, stop=(s == 0))
                for q in range(s):
                    last = pe.matmul(at[:, s * E:(s + 1) * E], ones[:, :], M[:, q, :], start=False, stop=(q == s - 1))
            for q in range(GT):
                last = pe.matmul(O[:, 128:128 + E], ones[:, :], M[:, q, :], start=(q == 0), stop=(q == GT - 1))
            C["rank_ps"].by(last)

    def act_slot(act, g, j):
        if front(g):
            ge(act, C["gb_ps1"], g)
            cols = onehot[0:96, 2 * GT * g:2 * GT * (g + 1)] if isinstance(g, int) else \
                onehot[0:96, bass.ds(g * (2 * GT), 2 * GT)]
            C["ohg"].by(act.activation(ohg[:, :, :], cols.unsqueeze(2).broadcast_to([96, 2 * GT, S]), ACT.Copy))
            ge(act, C["xT_ps"], g + 1)
            act.activation(XT[:, 0, :], F0[:, :], ACT.Copy)
            C["xT"].by(act.activation(XT[:, 1, :], F1[:, :], ACT.Copy))
            ge(act, C["z_ps"], g + 1)
            C["zt"].by(act.activation(ZT[:, :], G[:, :], ACT.Relu))
        if back(g):
            ge(act, C["hT_ps"], g)
            act.activation(HT[:, 0, :], F0[:, :], ACT.Copy)
            C["hT"].by(act.activation(HT[:, 1, :], F1[:, :], ACT.Copy))
            for s in range(GT):
                ge(act, C["x2"], (g - 1) * GT + s if not isinstance(g, int) else (g - 1) * GT + s)
                C["x2"].by(act.activation(sq[:, :], ROW[:, 1 - j, s, 0:D], ACT.Square, accum_out=x2[:, s:s + 1]))
            ge(act, C["m2"], g)
            C["s12"].by(act.activation(s12[:, :, :], m12[:, :, :], ACT.Sqrt))
        if front(g):
            ge(act, C["veps"], g + 1)
            C["std"].by(act.activation(std[:, :], std[:, :], ACT.Sqrt))
        if back(g):
            ge(act, C["dif"], g)
            C["ex"].by(act.activation(ex[:, :], ex[:, :], ACT.Exp))

    def dve_slot(dve, g, j):
        bc4 = lambda x: x.unsqueeze(2).broadcast_to(small)
        bce = lambda x: x.unsqueeze(1).broadcast_to(small)

        values = {}

        def after(name, x):
            if name not in place:
                ge(dve, C[name], x)
            elif isinstance(x, int):
                ge(dve, C[name], 4 * (x - 1) + place[name] + 1)
            else:
                n = place[name]
                if n not in values:
                    values[n] = x * 4 + (n - 3)
                dve.wait_ge(C[name].sem, values[n])

        if back(g):
            x = g

            def do(name, instruction, *needs):
                C[name].by(instruction)

            after("dot_ps", x)
            do("d2a", dve.tensor_tensor(d2[:, :, :], O[:, 0:GT * E].rearrange("p (s e) -> p s e", s=GT), bce(c2[:, :]),
                                        ALU.add))
            after("d2a", x)
            ge(dve, C["x2"], x * GT)
            do("d2b", dve.tensor_tensor(d2[:, :, :], d2[:, :, :], bc4(x2[:, :]), ALU.add))
            after("d2b", x)
            do("d2", dve.tensor_scalar(d2[:, :, :], d2[:, :, :], 1e-12, None, ALU.max))
            after("d2", x)
            do("m1", dve.tensor_reduce(m12[:, 0, :], d2[:, :, :], AX, ALU.max))
            after("m1", x)
            do("eq1", dve.tensor_tensor(eq[:, :, :], d2[:, :, :], bc4(m12[:, 0, :]), ALU.is_equal))
            after("eq1", x)
            do("eqr1", dve.tensor_tensor(eq[:, :, :], eq[:, :, :], bce(rev[:, :]), ALU.mult))
            after("eqr1", x)
            do("r1", dve.tensor_reduce(r12[:, 0, :], eq[:, :, :], AX, ALU.max))
            after("r1", x)
            do("oh1", dve.tensor_tensor(oh1[:, :, :], bc4(r12[:, 0, :]), bce(rev[:, :]), ALU.is_equal))
            after("oh1", x)
            do("d2m", dve.scalar_tensor_tensor(out=d2[:, :, :], in0=oh1[:, :, :], scalar=-3.0e38, in1=d2[:, :, :],
                                               op0=ALU.mult, op1=ALU.add))
            after("d2m", x)
            do("m2", dve.tensor_reduce(m12[:, 1, :], d2[:, :, :], AX, ALU.max))
            after("m2", x)
            do("eq2", dve.tensor_tensor(eq[:, :, :], d2[:, :, :], bc4(m12[:, 1, :]), ALU.is_equal))
            after("eq2", x)
            do("eqr2", dve.tensor_tensor(eq[:, :, :], eq[:, :, :], bce(rev[:, :]), ALU.mult))
            after("eqr2", x)
            do("r2", dve.tensor_reduce(r12[:, 1, :], eq[:, :, :], AX, ALU.max))
            after("r2", x)
            do("oh2", dve.tensor_tensor(oh2[:, :, :], bc4(r12[:, 1, :]), bce(rev[:, :]), ALU.is_equal))
            after("oh2", x)
            ge(dve, C["rank_ps"], x - 1)
            do("M", dve.tensor_tensor(M[:, :, :], oh1[:, :, :], oh2[:, :, :], ALU.add))
            do("first", dve.tensor_tensor(first[:, :], r12[:, 0, :], r12[:, 1, :], ALU.is_gt))
            ge(dve, C["hT_ps"], x)
            rl = ROW[:, 1 - j, :, D + 3]
            do("rlo", dve.tensor_tensor(rl, r12[:, 0, :], r12[:, 1, :], ALU.max))
            after("rlo", x)
            do("ohlo", dve.tensor_tensor(ohlo[:, :, :], bc4(rl), bce(rev[:, :]), ALU.is_equal))
            after("ohlo", x)
            after("M", x)
            do("ohhi", dve.tensor_tensor(ohhi[:, :, :], M[:, :, :], ohlo[:, :, :], ALU.subtract))
            after("s12", x)
            do("dif", dve.tensor_tensor(ex[:, :], s12[:, 1, :], s12[:, 0, :], ALU.subtract))
        if front(g):
            front_dve(dve, g, j, after)
        if back(g):
            after("ex", x)
            if not front(g):
                do("tok", dve.tensor_scalar(tok[:, :], tok[:, :], float(GROUP), None, ALU.add))
            do("den", dve.tensor_scalar(w12[:, 0, :], ex[:, :], 1.0, None, ALU.add))
            after("den", x)
            do("rden", dve.reciprocal(w12[:, 0, :], w12[:, 0, :]))
            after("rden", x)
            do("w2", dve.tensor_tensor(w12[:, 1, :], w12[:, 0, :], ex[:, :], ALU.mult))
            after("w2", x)
            do("wd", dve.tensor_tensor(ex[:, :], w12[:, 0, :], w12[:, 1, :], ALU.subtract))
            after("wd", x)
            after("first", x)
            do("wf", dve.tensor_tensor(ex[:, :], ex[:, :], first[:, :], ALU.mult))
            after("wf", x)
            do("wlo", dve.tensor_tensor(ROW[:, 1 - j, :, D], w12[:, 1, :], ex[:, :], ALU.add))
            do("whi", dve.tensor_tensor(ROW[:, 1 - j, :, D + 1], w12[:, 0, :], ex[:, :], ALU.subtract))
            after("tok", x)
            do("tokw", dve.tensor_copy(ROW[:, 1 - j, :, D + 2], tok[:, :]))
            after("rank_ps", x)
            do("rank", dve.tensor_tensor(tmp[:, :, :], O[:, 64:64 + GT * E].rearrange("p (s e) -> p s e", s=GT),
                                         bce(ce[:, :]), ALU.add))
            after("rank", x)
            after("ohhi", x)
            do("tlo", dve.tensor_tensor(ohlo[:, :, :], ohlo[:, :, :], tmp[:, :, :], ALU.mult))
            do("t2", dve.tensor_tensor(ohhi[:, :, :], ohhi[:, :, :], tmp[:, :, :], ALU.mult))
            do("ce", dve.tensor_tensor(ce[:, :], ce[:, :], O[:, 128:128 + E], ALU.add))
            after("tlo", x)
            after("t2", x)
            do("plo", dve.tensor_reduce(pos[:, 0, :], ohlo[:, :, :], AX, ALU.add))
            do("phi", dve.tensor_reduce(pos[:, 1, :], ohhi[:, :, :], AX, ALU.add))
            after("plo", x)
            after("phi", x)
            ge(dve, rows_out[1 - j], x - 2 + j, 16 * GT)
            after("whi", x)
            after("wlo", x)
            after("tokw", x)
            do("idx", dve.tensor_copy(idx[:, 1 - j, :, :], pos[:, :, :]))

    def front_dve(dve, g, j, after):
        x = g + 1
        after("y_ps", x)
        C["y"].by(dve.tensor_tensor(Y[:, :, :], Spair[:, :].rearrange("p (s d) -> p s d", s=GT), X1[:, j, :, :],
                                    ALU.add))
        after("y", x)
        for s in range(GT):
            last = dve.bn_stats(bst[:, s, :], Y[:, s, :])
        C["bst"].by(last)
        after("bst", x)
        if back(g):
            C["tok"].by(dve.tensor_scalar(tok[:, :], tok[:, :], float(GROUP), None, ALU.add))
        for s in range(GT):
            last = dve.bn_aggr(mv[:, s, :], bst[:, s, :])
        C["mv"].by(last)
        after("mv", x)
        C["veps"].by(dve.tensor_scalar(std[:, :], mv[:, :, 1], EPS, None, ALU.add))
        after("std", x)
        C["rstd"].by(dve.reciprocal(rstd[:, :], std[:, :]))
        after("rstd", x)
        for s in range(GT):
            last = dve.tensor_scalar(Y[:, s, :], Y[:, s, :], mv[:, s, 0:1], rstd[:, s:s + 1], ALU.subtract, ALU.mult)
        C["hn"].by(last)
        after("hn", x)
        ge(dve, rows_out[j], g - j, 16 * GT)
        for half in range(2):
            ss = slice(2 * half, 2 * half + 2)
            gb = Tpair[:, :].rearrange("p (s c d) -> p s c d", s=2, c=2)
            after(f"gb_ps{half}", x)
            C[f"hg{half}"].by(dve.tensor_tensor(Y[:, ss, :], Y[:, ss, :], gb[:, :, 0, :], ALU.mult))
            after(f"hg{half}", x)
            C[f"hb{half}"].by(dve.tensor_tensor(ROW[:, j, ss, 0:D], Y[:, ss, :], gb[:, :, 1, :], ALU.add))

    def pool_slot(pool, g, j):
        if back(g):
            ge(pool, C["idx"], g)
            carry(pool, spare, carried, g - 1)
            for k in range(2):
                for s in range(GT):
                    rows_out[1 - j].by(pool.indirect_dma_start(
                        xs_dram, bass.IndirectOffsetOnAxis(idx[:, 1 - j, k, s:s + 1], 0), ROW[:, 1 - j, s, :], None))

    x1_rows = x1_dram.rearrange("(n p) d -> p n d", p=P)
    NREG = 8

    def sp_load(sp, g, j):
        ge(sp, C["xT_ps"], g - 1)
        ge(sp, C["y"], g - 1)
        tiles = slice(GT * g, GT * g + GT) if isinstance(g, int) else bass.ds(g * GT, GT)
        x1_in[j].by(sp.dma_start(X1[:, j, :, :], x1_rows[:, tiles, :]))
        ge(sp, C["y_ps"], g)
        for b in range(2 * GT):
            col = 2 * GT * g + b
            at = prof_i[0:1, col:col + 1] if isinstance(g, int) else prof_i[0:1, bass.ds(g * (2 * GT) + b, 1)]
            q = sp.value_load(at, min_val=0, max_val=NP_ - 1)
            w_in.by(sp.dma_start(WD[:, b, :, :], io["L0_cond2_down_w"][bass.ds(q, 1)].rearrange(
                "o (k p) n -> p (o k) n", p=P)))
            w_in.by(sp.dma_start(WU[:, b, :], io["L0_cond2_up_w"][bass.ds(q, 1)].rearrange("o p n -> p (o n)")))

    with nc.Block() as block:
        @block.tensor
        def _(pe):
            run(pe, lambda g, j: pe_slot(pe, g, j))

        @block.scalar
        def _(act):
            run(act, lambda g, j: act_slot(act, g, j))

        @block.vector
        def _(dve):
            run(dve, lambda g, j: dve_slot(dve, g, j))
            ch = [0]
            done = C["t3"] = made("c_t3")

            def step(instruction):
                done.by(instruction)
                ch[0] += 1
                ge(dve, done, ch[0])

            ge(dve, C["ce"], NGROUP)
            step(dve.tensor_copy(ce_i[:, :], ce[:, :]))
            step(dve.scalar_tensor_tensor(out=cnt[:, :], in0=rev[:, :], scalar=float(CAP), in1=ce[:, :], op0=ALU.mult,
                                          op1=ALU.add))
            step(dve.tensor_scalar(cnt[:, :], cnt[:, :], -float(SPARE), None, ALU.add))
            step(dve.tensor_tensor(big2[:, :, :], cnt[:, :].unsqueeze(2).broadcast_to([P, E, T // FT]),
                                   steps[:, :].unsqueeze(1).broadcast_to([P, E, T // FT]), ALU.is_gt))
            step(dve.tensor_reduce(nt[:, :], big2[:, :, :], AX, ALU.add))
            step(dve.tensor_tensor_scan(incl[:, :], nt[:, :], zero8[:, :], 0.0, ALU.add, ALU.add))
            wide = [P, NTILE, E]
            step(dve.tensor_tensor(big[:, :, :], incl[:, :].unsqueeze(1).broadcast_to(wide),
                                   ramp[:, :].unsqueeze(2).broadcast_to(wide), ALU.is_le))
            step(dve.tensor_reduce(table_f[:, :], big[:, :, :], AX, ALU.add))
            step(dve.tensor_tensor(big[:, :, :], big[:, :, :], nt[:, :].unsqueeze(1).broadcast_to(wide), ALU.mult))
            step(dve.tensor_reduce(sumt[:, :], big[:, :, :], AX, ALU.add))
            step(dve.tensor_tensor(sumt[:, :], ramp[:, :], sumt[:, :], ALU.subtract))
            step(dve.tensor_scalar(sumt[:, :], sumt[:, :], float(FT), None, ALU.mult))
            step(dve.scalar_tensor_tensor(out=sumt[:, :], in0=table_f[:, :], scalar=float(CAP), in1=sumt[:, :],
                                          op0=ALU.mult, op1=ALU.add))
            step(dve.tensor_scalar(sumt[:, :], sumt[:, :], float(SPARE), None, ALU.min))
            step(dve.tensor_copy(table_i[:, 0, :], sumt[:, :]))
            step(dve.tensor_scalar(table_i[:, 1, :], table_f[:, :], float(E - 1), None, ALU.min))
            step(dve.memset(table_i[:, 2, 0:2], 1))
            step(dve.tensor_tensor(table_i[:, 2, 2:NTILE], table_i[:, 1, 2:NTILE], table_i[:, 1, 0:NTILE - 2],
                                   ALU.not_equal))
            step(dve.tensor_scalar(table_f[:, :], table_f[:, :], -1.0, float(E), ALU.mult, ALU.add))

        @block.gpsimd
        def _(pool):
            run(pool, lambda g, j: pool_slot(pool, g, j))
            for j in range(2):
                ge(pool, rows_out[j], NGROUP, 16 * GT)

        @block.sync
        def _(sp):
            sp_load(sp, 0, 0)
            sp_load(sp, 1, 1)
            with sp.Fori(2, NGROUP - 1, 2) as g:
                for j in range(2):
                    sp_load(sp, g + j, j)
            done = C["t3"]
            ge(sp, done, 1)
            for e in range(E):
                r = sp.value_load(ce_i[0:1, e:e + 1], min_val=e * CAP, max_val=e * CAP + T)
                c_r.by(sp.dma_start(xs_dram[bass.ds(r, FT), :].rearrange("(s p) w -> p s w", p=P), pad[:, :, :]))
            c_r.wait(sp, 16 * (2 + E))


H = 684
NFULL = H // P
HR = H - NFULL * P
NBLK = 2 * NFULL + 1
NCH = NFULL + 1
UW = 2 * KD * NBLK * P
DW = 2 * NCH * D
FS = FT // P


def load_biases(nc, io, sb, made, ps, ident, bias):
    rows = sb("bias_rows", [NCH * E, 2, P])
    clear, arrived, turned, done = made("b_clear"), made("b_arrived", 16), made("b_turned"), made("b_done")

    with nc.Block() as block:
        @block.gpsimd
        def _(pool):
            clear.by(pool.memset(rows[:, :, :], 0.0))

        @block.sync
        def _(sp):
            clear.wait(sp, 1)
            for i, k in enumerate(("L0_ffn_bg", "L0_ffn_b1")):
                arrived.by(sp.dma_start(rows[0:E, i, 0:HR], io[k][:, NFULL * P:H]))
                for c in range(NFULL):
                    arrived.by(sp.dma_start(rows[(c + 1) * E:(c + 2) * E, i, :], io[k][:, c * P:(c + 1) * P]))

        @block.tensor
        def _(pe):
            arrived.wait(pe, 16 * 2 * NCH)
            for i in range(2):
                last = pe.transpose(ps["F0"][:, i * NCH * E:(i + 1) * NCH * E], rows[:, i, :],
                                    ident[0:NCH * E, 0:NCH * E])
            turned.by(last)

        @block.scalar
        def _(act):
            turned.wait(act, 1)
            for i in range(2):
                done.by(act.activation(bias[:, :, i * NCH:(i + 1) * NCH],
                                       ps["F0"][:, i * NCH * E:(i + 1) * NCH * E].rearrange(
                                           "p (c e) -> p e c", c=NCH), ACT.Copy))
            done.wait(act, 2)


def split_weights(nc, io, sb, made, pool, up_dram, dn_dram):
    up = sb("up_stage", [P, KD, NBLK, P])
    dn = sb("dn_stage", [P, NCH, D])
    upb = sb("up_parts", [P, 2, KD, NBLK, P], BF16)
    dnb = sb("dn_parts", [P, 2, NCH, D], BF16)
    spare = sb("split_spare", [P, 2])
    carried = made("split_carried")
    s_in, s_out, s_do = made("split_in", 16), made("split_out", 16), made("split_do")
    last = NBLK - 1
    s_do.by(pool.memset(up[:, :, last, :], 0.0))
    s_do.by(pool.memset(dn[:, NCH - 1, :], 0.0))
    s_do.by(pool.memset(spare[:, :], 0.0))
    s_do.wait(pool, 3)
    NIN, NDO = 7, 4

    def split(e):
        pick = bass.ds(e, 1)
        s_do.wait(pool, e * NDO + 3)
        wg, w1, w2 = (io[k][pick] for k in ("L0_ffn_Wg", "L0_ffn_W1", "L0_ffn_W2"))
        for i, w in enumerate((wg, w1)):
            rows = w.rearrange("o (k p) n -> p (o k) n", p=P)
            s_in.by(pool.dma_start(up[:, :, i * NFULL:(i + 1) * NFULL, :].rearrange("p k b n -> p k (b n)"),
                                   rows[:, :, 0:NFULL * P]))
            s_in.by(pool.dma_start(up[:, :, last, 64 * i:64 * i + HR], rows[:, :, NFULL * P:H]))
        s_in.by(pool.dma_start(dn[:, 0:NFULL, :], w2[:, 0:NFULL * P, :].rearrange("o (c p) d -> p (o c) d", p=P)))
        s_in.by(pool.dma_start(dn[0:HR, NFULL, :], w2[:, NFULL * P:H, :].rearrange("o p d -> p (o d)")))
        s_in.by(pool.dma_start(dn[HR:HR + 1, NFULL, :], io["L0_ffn_b2"][pick, :]))
        s_in.wait(pool, (e + 1) * (16 * NIN))
        s_out.wait(pool, e * 32)
        n = e * NDO
        for stage, parts in ((up, upb), (dn, dnb)):
            carry(pool, spare, carried, e * 2 + (0 if stage is up else 1))
            s_do.by(pool.tensor_copy(parts[:, 0], stage[:]))
            s_do.wait(pool, n + (4 if stage is up else 6))
            s_do.by(pool.tensor_tensor(parts[:, 1], stage[:], parts[:, 0], ALU.subtract))
            s_do.wait(pool, n + (5 if stage is up else 7))
        s_out.by(pool.dma_start(up_dram[pick].rearrange("o p w -> p (o w)"),
                                upb[:, :, :, :, :].rearrange("p a k b n -> p (a k b n)")))
        s_out.by(pool.dma_start(dn_dram[pick].rearrange("o p w -> p (o w)"),
                                dnb[:, :, :, :].rearrange("p a c d -> p (a c d)")))

    split(0)
    with pool.Fori(1, E, 1) as e:
        split(e)
    s_out.wait(pool, 32 * E)


def experts(nc, io, sb, made, ps, ident, bias, xs_dram, up_dram, dn_dram, table_i, table_f, out):
    Spair, Tpair = ps["Spair"], ps["Tpair"]
    GU = [Spair[:, 0:512], Spair[:, 512:1024], Tpair[:, 0:512], Tpair[:, 512:1024]]
    YP = [ps["F1"], ps["O"]]
    XP = ps["G"]
    XR = sb("rows", [P, 2, FS, RW])
    XT = sb("rowsT", [P, 2, KD, FT], BF16)
    UP = sb("UP", [P, 2, 2, KD, NBLK, P], BF16)
    DN = sb("DN", [P, 2, 2, NCH, D], BF16)
    BT = sb("BT", [P, 2, 2 * NCH])
    SIL = sb("SIL", [P, 2, FT])
    H32 = sb("H32", [P, 2, FT])
    UR = sb("UR", [HR, FT])
    HT = sb("innerT", [P, 2, NCH, FT], BF16)
    Z = sb("Z", [P, 2, FS, D])
    idx = sb("row_idx", [P, 2, FS], I32)
    wt = sb("row_wt", [P, 2, FS])
    islo = sb("islo", [P, FS])
    tl = sb("tl", [P, FS])
    spare = sb("expert_spare", [P, 2])

    e_set, spared, carried = made("e_set"), made("spared"), made("carried")
    xr_in, up_in, dn_in, bt_in, z_in, sent = ([made(f"{k}{j}", 16) for j in range(2)]
                                              for k in ("xr_in", "up_in", "dn_in", "bt_in", "z_in", "sent"))
    gu, sil, h32, hhi, hlo = ([made(f"{k}{c}") for c in range(3)] for k in ("gu", "sil", "h32", "hhi", "hlo"))
    ur, xT_ps, xhi, xlo, y_ps, yo, ilo, wl, wh, wdone, idone = (made("e_" + k) for k in (
        "ur", "xT_ps", "xhi", "xlo", "y_ps", "yo", "ilo", "wl", "wh", "wdone", "idone"))

    def ge(eng, m, x, mul=1):
        if isinstance(x, int):
            if x > 0:
                eng.wait_ge(m.sem, x * mul)
        else:
            eng.wait_ge(m.sem, x * mul if mul != 1 else x)

    def run(eng, body):
        for i in range(2):
            body(i, i)
        with eng.Fori(2, NTILE - 3, 2) as i:
            for j in range(2):
                body(i + j if j else i, j)
        for i in range(NTILE - 2, NTILE):
            body(i, i % 2)

    def loaded(eng, m, i, j, each=1):
        ge(eng, m[j], i + (2 - j), 8 * each)

    values = {}

    def chunk(eng, m, c, i):
        if isinstance(i, int):
            ge(eng, m[c % 3], 2 * i + c // 3 + 1 if i >= 0 else 0)
        else:
            key = (id(eng), id(i), c // 3)
            if key not in values:
                values[key] = (i, i * 2 + (c // 3 + 1))
            eng.wait_ge(m[c % 3].sem, values[key][1])

    def kr(c):
        return HR if c == 0 else P

    def transposes(pe, i, j):
        loaded(pe, xr_in, i, j)
        ge(pe, xlo, i)
        for k in range(KD):
            for s in range(FS):
                last = pe.transpose(XP[:, k * FT + s * P:k * FT + (s + 1) * P], XR[:, j, s, k * P:(k + 1) * P],
                                    ident[:, :])
        xT_ps.by(last)

    def pe_slot(pe, i, j):
        if isinstance(i, int) and i == 0:
            e_set.wait(pe, 2)
            transposes(pe, 0, 0)
        i1, im = i + 1, i - 1
        ge(pe, xlo, i1)
        loaded(pe, up_in, i, j)
        for c in range(NCH):
            at = GU[(NCH * j + c) % 4]
            if c >= 4:
                chunk(pe, h32, c - 4, i)
            else:
                chunk(pe, h32, c + 2, im)
            blocks = ((2 * NFULL, at[:, 0:FT]),) if c == 0 else ((c - 1, at[:, 0:FT]), (NFULL + c - 1, at[:, FT:2 * FT]))
            for b, to in blocks:
                for k in range(KD):
                    for n, (wp, xp) in enumerate(((0, 0), (0, 1), (1, 0))):
                        last = pe.matmul(to, UP[:, j, wp, k, b, :], XT[:, xp, k, :], start=(k == 0 and n == 0),
                                         stop=(k == KD - 1 and n == 2))
            gu[c % 3].by(last)
        if not (isinstance(i, int) and i == NTILE - 1):
            transposes(pe, i1, 1 - j)
        loaded(pe, dn_in, i, j)
        ge(pe, yo, i)
        for c in range(NCH):
            chunk(pe, hlo, c, i)
            dc, K = (c - 1) % NCH, kr(c) + (c == 0)
            for s in range(FS):
                for n, (hp, wp) in enumerate(((0, 0), (0, 1), (1, 0))):
                    last = pe.matmul(YP[s][:, 0:D], HT[0:K, hp, c, s * P:(s + 1) * P], DN[0:K, j, wp, dc, :],
                                     start=(c == 0 and n == 0), stop=(c == NCH - 1 and n == 2))
        y_ps.by(last)

    def act_slot(act, i, j):
        def high(c):
            chunk(act, h32, c, i)
            if c == 0:
                ge(act, y_ps, i)
            hhi[c % 3].by(act.activation(HT[0:kr(c), 0, c, :], H32[0:kr(c), c % 2, :], ACT.Copy))

        def xhigh(i, i1):
            ge(act, xT_ps, i1)
            xhi.by(act.activation(XT[:, 0, :, :], XP[:, :].rearrange("p (k t) -> p k t", k=KD), ACT.Copy))

        if isinstance(i, int) and i == 0:
            xhigh(0, 1)
        i1, im = i + 1, i - 1
        loaded(act, bt_in, i, j)
        for c in range(NCH):
            at = GU[(NCH * j + c) % 4]
            chunk(act, gu, c, i)
            if c >= 2:
                chunk(act, h32, c - 2, i)
            else:
                chunk(act, h32, c + 4, im)
            sil[c % 3].by(act.activation(SIL[0:kr(c), c % 2, :], at[0:kr(c), 0:FT], ACT.Silu, bias=BT[0:kr(c), j, c:c + 1]))
            if c == 0:
                ur.by(act.activation(UR[:, :], at[64:64 + HR, 0:FT], ACT.Copy))
            else:
                high(c - 1)
        high(NCH - 1)
        if not (isinstance(i, int) and i == NTILE - 1):
            xhigh(i1, i + 2)

    def dve_slot(dve, i, j):
        def low(c):
            chunk(dve, hhi, c, i)
            hlo[c % 3].by(dve.tensor_tensor(HT[0:kr(c), 1, c, :], H32[0:kr(c), c % 2, :], HT[0:kr(c), 0, c, :],
                                        ALU.subtract))

        def incoming(i, i1, j):
            ge(dve, xhi, i1)
            xlo.by(dve.tensor_tensor(XT[:, 1, :, :].rearrange("p k t -> p (k t)"), XP[:, :],
                                     XT[:, 0, :, :].rearrange("p k t -> p (k t)"), ALU.subtract))
            if isinstance(i, int):
                tf = table_f[:, i:i + 1]
            else:
                tf = table_f[:, bass.ds(i, 1)]
            loaded(dve, sent, i - 2 if isinstance(i, int) else i - 2, j, 2)
            ilo.by(dve.tensor_tensor(islo[:, :], XR[:, j, :, D + 3], tf.broadcast_to([P, FS]), ALU.is_equal))
            idone.by(dve.tensor_copy(idx[:, j, :], XR[:, j, :, D + 2]))
            ge(dve, ilo, i1)
            wl.by(dve.tensor_tensor(tl[:, :], islo[:, :], XR[:, j, :, D], ALU.mult))
            wh.by(dve.scalar_tensor_tensor(out=wt[:, j, :], in0=islo[:, :], scalar=-1.0, in1=XR[:, j, :, D + 1],
                                           op0=ALU.add, op1=ALU.mult))
            ge(dve, wl, i1)
            ge(dve, wh, i1)
            wdone.by(dve.tensor_tensor(wt[:, j, :], tl[:, :], wt[:, j, :], ALU.subtract))

        if isinstance(i, int) and i == 0:
            incoming(0, 1, 0)
            loaded(dve, bt_in, 0, 0)
        else:
            loaded(dve, bt_in, i, j)
        i1, im = i + 1, i - 1
        for c in range(NCH):
            at = GU[(NCH * j + c) % 4]
            lin = UR[:, :] if c == 0 else at[:, FT:2 * FT]
            if c:
                chunk(dve, sil, c, i)
            else:
                ge(dve, ur, i1)
            if c >= 2:
                chunk(dve, hlo, c - 2, i)
            else:
                chunk(dve, hlo, c + 4, im)
            h32[c % 3].by(dve.scalar_tensor_tensor(out=H32[0:kr(c), c % 2, :], in0=lin, scalar=BT[0:kr(c), j, NCH + c:NCH + c + 1],
                                               in1=SIL[0:kr(c), c % 2, :], op0=ALU.add, op1=ALU.mult))
            if c:
                low(c - 1)
        low(NCH - 1)
        if not (isinstance(i, int) and i == NTILE - 1):
            incoming(i1, i + 2, 1 - j)
        ge(dve, y_ps, i1)
        ge(dve, wdone, i1)
        loaded(dve, z_in, i, j, 2)
        for s in range(FS):
            last = dve.scalar_tensor_tensor(out=Z[:, j, s, :], in0=YP[s][:, 0:D], scalar=wt[:, j, s:s + 1],
                                            in1=Z[:, j, s, :], op0=ALU.mult, op1=ALU.add)
        yo.by(last)

    def pool_slot(pool, i, j):
        i1 = i + 1
        ge(pool, idone, i1)
        loaded(pool, sent, i - 1, 1 - j, 2)
        carry(pool, spare, carried, i * 2)
        for s in range(FS):
            z_in[j].by(pool.indirect_dma_start(Z[:, j, s, :], None, out,
                                               bass.IndirectOffsetOnAxis(idx[:, j, s:s + 1], 0),
                                               bounds_check=T - 1, oob_is_err=False))
        ge(pool, yo, i1)
        carry(pool, spare, carried, i * 2 + 1)
        for s in range(FS):
            sent[j].by(pool.indirect_dma_start(out, bass.IndirectOffsetOnAxis(idx[:, j, s:s + 1], 0),
                                               Z[:, j, s, :], None, bounds_check=T - 1, oob_is_err=False))

    def sp_load(sp, i, j, waits):
        def at(k):
            col = slice(i, i + 1) if isinstance(i, int) else bass.ds(i, 1)
            return table_i[0:1, k, col]

        row = sp.value_load(at(0), min_val=0, max_val=SPARE)
        e = sp.value_load(at(1), min_val=0, max_val=E - 1)
        new = sp.value_load(at(2), min_val=0, max_val=1)
        if waits:
            n = i - 1
            ge(sp, xT_ps, n)
            ge(sp, wdone, n)
        xr_in[j].by(sp.dma_start(XR[:, j, :, :], xs_dram[bass.ds(row, FT), :].rearrange("(s p) w -> p s w", p=P)))
        if waits:
            chunk(sp, gu, NCH - 1, i - 2)
        up_in[j].by(sp.dma_start(UP[:, j, :, :, :, :].rearrange("p a k b n -> p (a k b n)"),
                                 up_dram[bass.ds(e, 1)].rearrange("o p w -> p (o w)"), cond=new))
        if waits:
            chunk(sp, h32, NCH - 1, i - 2)
        bt_in[j].by(sp.dma_start(BT[:, j, :], bias[:, bass.ds(e, 1), :].rearrange("p o c -> p (o c)")))
        if waits:
            ge(sp, y_ps, n)
        dn_in[j].by(sp.dma_start(DN[:, j, :, :, :].rearrange("p a c d -> p (a c d)"),
                                 dn_dram[bass.ds(e, 1)].rearrange("o p w -> p (o w)"), cond=new))

    with nc.Block() as block:
        @block.sync
        def _(sp):
            sp_load(sp, 0, 0, False)
            sp_load(sp, 1, 1, False)
            with sp.Fori(2, NTILE - 1, 2) as i:
                for j in range(2):
                    sp_load(sp, i + j if j else i, j, True)

        @block.tensor
        def _(pe):
            run(pe, lambda i, j: pe_slot(pe, i, j))

        @block.scalar
        def _(act):
            run(act, lambda i, j: act_slot(act, i, j))

        @block.vector
        def _(dve):
            e_set.by(dve.memset(HT[32:64, 0, 0, :], 1.0))
            e_set.by(dve.memset(HT[32:64, 1, 0, :], 0.0))
            dve.memset(Z[:, :, :, :], 0.0)
            e_set.wait(dve, 2)
            run(dve, lambda i, j: dve_slot(dve, i, j))

        @block.gpsimd
        def _(pool):
            spared.by(pool.memset(spare[:, :], 0.0))
            spared.wait(pool, 1)
            run(pool, lambda i, j: pool_slot(pool, i, j))
            for j in range(2):
                loaded(pool, sent, NTILE - 2 + j, j, 2)


def build(nc, io, out):
    with ExitStack() as ctx:
        def made(name, step=1):
            return Made(ctx.enter_context(nc.semaphore(name)), step)

        def dram(name, shape, dt=F32):
            return nc.dram_tensor(name, shape, dt).ap()

        def keep(name, shape, dt=F32):
            return ctx.enter_context(nc.sbuf_tensor(name, shape, dt))

        ps = {k: ctx.enter_context(nc.psum_tensor(k, [P, w], F32)) for k, w in
              (("Spair", 1024), ("Tpair", 1024), ("F0", 512), ("F1", 512), ("G", 512), ("O", 512))}
        xs_dram = dram("xs_dram", [E * CAP + FT, RW])
        up_dram = dram("up_dram", [E, P, UW], BF16)
        dn_dram = dram("dn_dram", [E, P, DW], BF16)
        ident = keep("ident", [P, P])
        table_i = keep("table_i", [P, 3, NTILE], I32)
        table_f = keep("table_f", [P, NTILE])
        bias = keep("bias", [P, E, 2 * NCH])
        with ExitStack() as phase:
            sb = lambda name, shape, dt=F32: phase.enter_context(nc.sbuf_tensor(name, shape, dt))
            setup_and_attention(nc, io, sb, made, dram, ps, ident, out,
                                lambda pool: split_weights(nc, io, sb, made, pool, up_dram, dn_dram))
        with ExitStack() as phase:
            sb = lambda name, shape, dt=F32: phase.enter_context(nc.sbuf_tensor(name, shape, dt))
            load_biases(nc, io, sb, made, ps, ident, bias)
            dispatch(nc, io, sb, made, dram, ps, ident, out, xs_dram, table_i, table_f)
        with ExitStack() as phase:
            sb = lambda name, shape, dt=F32: phase.enter_context(nc.sbuf_tensor(name, shape, dt))
            experts(nc, io, sb, made, ps, ident, bias, xs_dram, up_dram, dn_dram, table_i, table_f, out)


_INS = ["x", "itok_B_0_2", "itok_B_0_6", "L0_cond_W1", "L0_cond_b1",
        "L0_cond_v", "L0_attn_Wq", "L0_attn_Wk", "L0_attn_Wv", "L0_attn_Wo",
        "L0_attn_W_down_kv", "L0_attn_W_up_k", "L0_attn_W_up_v", "L0_cond2_down_w", "L0_cond2_down_b",
        "L0_cond2_up_w", "L0_cond2_up_b", "L0_cond2_ln_g", "L0_cond2_ln_b", "L0_ffn_centroid",
        "L0_ffn_Wg", "L0_ffn_bg", "L0_ffn_W1", "L0_ffn_b1", "L0_ffn_W2",
        "L0_ffn_b2"]
_OUTS = [((64, 64, 256), "float32")]


def kernel(**inputs):
    import numpy as _np
    import concourse.bacc as _bacc
    from concourse import mybir as _mybir
    from concourse.bass_utils import run_bass_kernel_spmd as _run

    nc = _bacc.Bacc("TRN2", target_bir_lowering=False, num_devices=1)
    arrays, io = {}, {}
    for name in _INS:
        a = _np.ascontiguousarray(inputs[name])
        arrays[f"in_{name}_dram"] = a
        io[name] = nc.dram_tensor(f"in_{name}_dram", a.shape, _mybir.dt.from_np(a.dtype), kind="ExternalInput").ap()
    outs = [nc.dram_tensor(f"out_{i}_dram", shape, _mybir.dt.from_np(_np.dtype(dtype)), kind="ExternalOutput").ap()
            for i, (shape, dtype) in enumerate(_OUTS)]
    build(nc, io, outs[0].rearrange("b s d -> (b s) d"))
    r = _run(nc, [arrays], core_ids=[0])
    return r.results[0]["out_0_dram"]
```

```python
import numpy as np
from contextlib import ExitStack

import concourse.bass as bass
from concourse import mybir

F32 = mybir.dt.float32
BF16 = mybir.dt.bfloat16
I32 = mybir.dt.int32
ALU = mybir.AluOpType
ACT = mybir.ActivationFunctionType
AX = mybir.AxisListType.X

P = 128
B, S, D = 64, 64, 256
T = B * S
KD = D // P
A = 64
L = 64
NH, DH = 16, 16
HP = NH // 2
NPAIR = T // P
UT = 2 * P
NUNIT = T // UT
VW = 2 * DH + 2
QSCALE = 1.0 / 16.0
CLAMP = 10000.0
DECAY = -0.01 * 0.01
FAR = 1.0e30


class Made:

    def __init__(self, sem, step=1):
        self.sem, self.step = sem, step

    def by(self, instruction):
        return instruction.then_inc(self.sem, self.step)

    def wait(self, eng, value):
        if isinstance(value, int) and value <= 0:
            return
        eng.wait_ge(self.sem, value)


def carry(pool, spare, carried, n):
    carried.wait(pool, n)
    carried.by(pool.tensor_tensor(spare[:, 1:2], spare[:, 0:1], spare[:, 0:1], ALU.add))


def setup_and_attention(nc, io, sb, made, dram, ps, ident, x1_dram, beside_pool=None):
    F0, F1, G, O, Spair, Tpair = (ps[k] for k in ("F0", "F1", "G", "O", "Spair", "Tpair"))
    qk_dram = dram("qk_dram", [2, 4, D, UT], BF16)

    w1 = sb("w1", [P, KD, A])
    b1 = sb("b1", [A, 1])
    v = sb("v", [A, 1])
    vrep = sb("vrep", [A, S])
    wq = sb("wq", [P, KD, D])
    wk = sb("wk", [P, KD, D])
    wv = sb("wv", [P, KD, D])
    wkvT = sb("wkvT", [P, KD, D])
    wdown = sb("wdown", [P, KD, L])
    wkvd = sb("wkvd", [P, KD, L])
    wuk = sb("wuk", [L, D])
    wuv = sb("wuv", [L, D])
    wo = sb("wo", [P, KD, D])
    types_i = sb("types_i", [P, B], I32)
    types = sb("types", [P, NPAIR])
    is_t = sb("is_t", [P, 3, NPAIR])
    diff = sb("diff", [P, S])
    shut = sb("shut", [P, 3, S])
    cap = sb("cap", [P, NPAIR, S])
    capt = sb("capt", [P, NPAIR, S])
    count = sb("count", [P, NPAIR])
    decay = sb("decay", [P, S])
    XU = sb("XU", [P, 2, 2, D])
    XT = sb("XT", [P, KD, UT])
    AT = sb("AT", [A, UT])
    SM = sb("SM", [P, 2, S])
    smx = sb("smx", [P, 2])
    ssum = sb("ssum", [P, 2])
    PB = sb("PB", [P, 2, P])
    PT = sb("PT", [P, 2, P])
    PO = sb("PO", [P, KD, UT])
    QK = sb("QK", [P, 4, KD, UT], BF16)
    LT = sb("LT", [L, 2, UT])
    QS = sb("QS", [3 * 32, 2, HP, UT], BF16)
    KS = sb("KS", [3 * 32, 2, HP, 2, UT], BF16)
    VB = sb("VB", [P, 2, 2, 2, HP, VW])
    W = sb("W", [P, 2, NH, S])
    rowmax = sb("rowmax", [P, 2, NH])
    PX = sb("PX", [P, 2, HP, P])
    rec = sb("rec", [P, HP, 2])
    ON = sb("ON", [P, HP, 2, DH])
    OT = sb("OT", [P, KD, P])
    XR = sb("XR", [P, 2, D])

    s_w = made("s_w", 16)
    s_c = made("s_c")
    s_v = made("s_v")
    s_a = made("s_a")
    s_p = made("s_p")

    loads = [
        (w1[:, :, :], io["L0_cond_W1"].rearrange("(k p) a -> p k a", p=P)),
        (b1[:, :], io["L0_cond_b1"].rearrange("(a o) -> a o", o=1)),
        (v[:, :], io["L0_cond_v"].rearrange("(a o) -> a o", o=1)),
        (types_i[:, :], io["itok_B_0_2"].rearrange("(o b) -> o b", o=1).partition_broadcast(P)
         if False else io["itok_B_0_2"].rearrange("(o b) -> o b", o=1).broadcast_to([P, B])),
        (wk[:, :, :], io["L0_attn_Wk"].rearrange("(k p) n -> p k n", p=P)),
        (wv[:, :, :], io["L0_attn_Wv"].rearrange("(k p) n -> p k n", p=P)),
        (wdown[:, :, :], io["L0_attn_W_down_kv"].rearrange("(k p) n -> p k n", p=P)),
        (wq[:, :, :], io["L0_attn_Wq"].rearrange("(k p) n -> p k n", p=P)),
        (wuk[:, :], io["L0_attn_W_up_k"]),
        (wuv[:, :], io["L0_attn_W_up_v"]),
        (wo[:, :, :], io["L0_attn_Wo"].rearrange("(k p) n -> p k n", p=P)),
    ]

    with nc.Block() as block:
        @block.sync
        def _(sp):
            for out, in_ in loads:
                s_w.by(sp.dma_start(out, in_))
            s_w.wait(sp, 16 * len(loads))

        @block.gpsimd
        def _(pool):
            n = [0]

            def step(instruction):
                s_c.by(instruction)
                n[0] += 1
                s_c.wait(pool, n[0])

            step(pool.memset(ident[:, :], 0.0))
            step(pool.affine_select(out=ident[:, :], in_=ident[:, :], compare_op=ALU.not_equal, fill=1.0,
                                    base=0, pattern=[[-1, P]], channel_multiplier=1))
            for h in range(2):
                step(pool.iota(diff[S * h:S * h + S, :], pattern=[[1, S]], base=0, channel_multiplier=-1,
                               allow_small_or_imprecise_dtypes=True))
            step(pool.memset(PB[:, :, :], 0.0))
            step(pool.memset(KS[:, :, :, :, :], 0.0))
            step(pool.memset(VB[:, :, :, :, :, :], 0.0))
            for half in range(2):
                col = 2 * DH + half
                step(pool.memset(VB[S * half:S * half + S, :, :, :, :, :].rearrange(
                    "p u s b h c -> p (u s b h) c")[:, :, col], 1.0))

        @block.vector
        def _(dve):
            n = [0]

            def step(instruction):
                s_v.by(instruction)
                n[0] += 1
                s_v.wait(dve, n[0])

            s_w.wait(dve, 16 * len(loads))
            s_c.wait(dve, 4)
            step(dve.memset(vrep[:, :], 1.0))
            step(dve.tensor_scalar(vrep[:, :], vrep[:, :], v[:, 0:1], None, ALU.mult))
            step(dve.tensor_tensor(wk[:, :, :], wk[:, :, :], wv[:, :, :], ALU.add))
            for h in range(2):
                rows = slice(S * h, S * h + S)
                step(dve.tensor_copy(types[rows, :], types_i[rows, :].rearrange("p (n b) -> p n b", b=2)[:, :, h]))
            step(dve.tensor_scalar(is_t[:, 0, :], types[:, :], 0.0, None, ALU.is_equal))
            step(dve.tensor_scalar(is_t[:, 1, :], types[:, :], 1.0, None, ALU.is_equal))
            step(dve.tensor_tensor(is_t[:, 2, :], is_t[:, 0, :], is_t[:, 1, :], ALU.add))
            step(dve.tensor_scalar(is_t[:, 2, :], is_t[:, 2, :], -1.0, 1.0, ALU.mult, ALU.add))
            for k, op in enumerate((ALU.is_gt, ALU.is_lt, ALU.is_equal)):
                step(dve.tensor_scalar(shut[:, k, :], diff[:, :], 0.0, None, op))
            wide = [P, NPAIR, S]
            for k in range(3):
                to = cap if k == 0 else capt
                step(dve.tensor_tensor(to[:, :, :], is_t[:, k, :].unsqueeze(2).broadcast_to(wide),
                                       shut[:, k, :].unsqueeze(1).broadcast_to(wide), ALU.mult))
                if k:
                    step(dve.tensor_tensor(cap[:, :, :], cap[:, :, :], capt[:, :, :], ALU.add))
            step(dve.tensor_reduce(count[:, :], cap[:, :, :], AX, ALU.add))
            step(dve.tensor_scalar(count[:, :], count[:, :], -1.0, float(S), ALU.mult, ALU.add))
            step(dve.tensor_scalar(cap[:, :, :], cap[:, :, :], -2.0 * FAR, FAR, ALU.mult, ALU.add))

        @block.scalar
        def _(act):
            s_c.wait(act, 4)
            s_a.by(act.activation(decay[:, :], diff[:, :], ACT.Abs))
            s_a.wait(act, 1)
            s_a.by(act.activation(decay[:, :], decay[:, :], ACT.Exp, scale=DECAY))
            for k in range(KD):
                s_p.wait(act, k + 1)
                s_a.by(act.activation(wkvT[:, k, :], F0[:, 0:D], ACT.Copy))
            s_p.wait(act, KD + 1)
            s_a.by(act.activation(wkvd[:, :, :], F1[:, 0:KD * L].rearrange("p (k l) -> p k l", k=KD), ACT.Copy))

        @block.tensor
        def _(pe):
            s_c.wait(pe, 2)
            s_v.wait(pe, 3)
            for k in range(KD):
                if k:
                    s_a.wait(pe, 2 + k)
                for m in range(KD):
                    last = pe.transpose(F0[:, m * P:(m + 1) * P], wk[:, m, k * P:(k + 1) * P], ident[:, :])
                s_p.by(last)
            s_a.wait(pe, 2 + KD)
            for m in range(KD):
                for k in range(KD):
                    last = pe.matmul(F1[:, m * L:(m + 1) * L], wkvT[:, k, m * P:(m + 1) * P], wdown[:, k, :],
                                     start=(k == 0), stop=(k == KD - 1))
            s_p.by(last)

    u_x = made("u_x", 16)
    names_u = ["xt_ps", "xt", "at_ps", "at", "sc_ps", "sc_a", "sc_b", "sc_c", "sc_e", "sc_f", "sc_g", "sc_h", "pb",
               "pt_ps", "pt", "po_ps", "po", "q_ps", "qhi", "qlo", "lt_ps", "lt", "k_ps", "khi", "klo",
               "v_ps", "vb0", "vb1"]
    U = {k: made("u_" + k, 2) for k in names_u}
    names_p = ["s_ps", "clip", "dec", "max", "sub", "t_ps0", "t_ps1", "px0", "px1", "o_ps", "rec", "on",
               "ot_ps", "ot", "g_ps", "x1"]
    R = {k: made("p_" + k) for k in names_p}
    u_qk_out = made("u_qk_out", 16)
    u_qs = made("u_qs", 16)
    p_xr = made("p_xr", 16)
    p_out = made("p_out", 16)

    LS, LT_, LV, LG = 3, 4, 5, 6

    def has_pair(n):
        return not isinstance(n, int) or 0 <= n < NPAIR

    def run(eng, body):
        first, last = 8, 28
        for t in range(-3, first):
            body(t, t % 4)
        with eng.Fori(first, last - 3, 4) as t:
            cache = {}
            for j in range(4):
                body(Slot(t, cache, eng) + j, j)
        for t in range(last, NPAIR + LG):
            body(t, t % 4)

    class Slot:

        def __init__(self, t, cache, eng, c=0):
            self.t, self.cache, self.eng, self.c = t, cache, eng, c

        def __add__(self, c):
            return Slot(self.t, self.cache, self.eng, self.c + c)

        def __sub__(self, c):
            return self + (-c)

        def reg(self):
            return self.t + self.c

    def val(x, mul=1):
        if isinstance(x, int):
            return x * mul
        return x.reg() * mul if mul != 1 else x.reg()

    def ge(eng, m, x, mul=1):
        if isinstance(x, int):
            if x > 0:
                eng.wait_ge(m.sem, x * mul)
            return
        eng.wait_ge(m.sem, val(x, mul))

    def on_unit(t, j, start):
        if (j - start) % 2:
            return None
        u2 = t - start
        if isinstance(u2, int) and not 0 <= u2 < 2 * NUNIT:
            return None
        return u2, ((j - start) // 2) % 2

    def most(x):
        return min(x, 2 * NUNIT) if isinstance(x, int) else x

    def pe_slot(pe, t, j):
        def scores(n):
            up, h = ((j - LS) % 4) // 2, (j - LS) % 2
            if h == 0:
                ge(pe, u_qs, n + 2, 72)
            ge(pe, R["clip"], n)
            for b in range(2):
                c0 = h * P + b * S
                for hp in range(HP):
                    last = pe.matmul(Spair[S * b:S * b + S, hp * P:(hp + 1) * P], QS[:, up, hp, c0:c0 + S],
                                     KS[:, up, hp, :, c0:c0 + S], start=True, stop=True)
            R["s_ps"].by(last)

        def turn_heads_out(n):
            ge(pe, R["on"], n + 1)
            ge(pe, R["x1"], n)
            for m in range(KD):
                last = pe.transpose(G[:, m * P:(m + 1) * P],
                                    ON[:, :, :, :].rearrange("p h e d -> p (h e d)")[:, m * P:(m + 1) * P], ident[:, :])
            R["ot_ps"].by(last)

        def project_out(n):
            ge(pe, R["ot"], n + 1)
            for m in range(KD):
                last = pe.matmul(G[:, D:2 * D], OT[:, m, :], wo[:, m, :], start=(m == 0), stop=(m == KD - 1))
            R["g_ps"].by(last)

        def turn_weights(n):
            w = W[:, (j - LT_) % 2, :, :].rearrange("p h s -> p (h s)")
            ge(pe, R["sub"], n + 1)
            for half in range(2):
                ge(pe, R[f"px{half}"], n)
                for hp in range(4 * half, 4 * half + 4):
                    last = pe.transpose(Tpair[:, hp * P:(hp + 1) * P], w[:, hp * P:(hp + 1) * P], ident[:, :])
                R[f"t_ps{half}"].by(last)

        def values(n, b):
            up, h = ((j - LV) % 4) // 2, (j - LV) % 2
            if b == 0:
                ge(pe, R["px0"], n + 1)
                ge(pe, R["px1"], n + 1)
                if h == 0:
                    ge(pe, U["vb0"], n + 2)
                    ge(pe, U["vb1"], n + 2)
                ge(pe, R["on"], n)
            for hp in range(HP):
                last = pe.matmul(O[S * b:S * b + S, hp * VW:(hp + 1) * VW], PX[:, h, hp, S * b:S * b + S],
                                 VB[:, up, h, b, hp, :], start=True, stop=True)
            if b:
                R["o_ps"].by(last)

        def queries(u2):
            ge(pe, U["po"], u2 + 2)
            ge(pe, U["xt"], most(u2 + 4))
            for m in range(KD):
                for k in range(KD):
                    last = pe.matmul(F0[:, m * UT:(m + 1) * UT], wq[:, k, m * P:(m + 1) * P], PO[:, k, :],
                                     start=(k == 0), stop=(k == KD - 1))
            U["q_ps"].by(last)

        def latent(u2):
            ge(pe, U["sc_a"], most(u2 + 4))
            for k in range(KD):
                last = pe.matmul(F1[0:L, 0:UT], wkvd[:, k, :], PO[:, k, :], start=(k == 0), stop=(k == KD - 1))
            U["lt_ps"].by(last)

        def keys(u2, up):
            ge(pe, U["lt"], u2 + 2)
            ge(pe, U["qlo"], u2 + 2)
            for m in range(KD):
                last = pe.matmul(F0[:, m * UT:(m + 1) * UT], wuk[:, m * P:(m + 1) * P], LT[:, up, :],
                                 start=True, stop=True)
            U["k_ps"].by(last)

        def project_values(u2, up):
            ge(pe, U["lt"], most(u2 + 4))
            for s in range(2):
                last = pe.matmul(F1[:, s * D:(s + 1) * D], LT[:, up, s * P:(s + 1) * P], wuv[:, :],
                                 start=True, stop=True)
            U["v_ps"].by(last)

        def turn_pooling(u2):
            ge(pe, U["pb"], u2 + 2)
            ge(pe, U["klo"], u2)
            for s in range(2):
                last = pe.transpose(F0[:, s * P:(s + 1) * P], PB[:, s, :], ident[:, :])
            U["pt_ps"].by(last)

        def pool(u2, up):
            ge(pe, U["pt"], u2 + 2)
            ge(pe, U["vb1"], u2 - 2)
            for k in range(KD):
                for s in range(2):
                    last = pe.matmul(F1[:, k * UT + s * P:k * UT + (s + 1) * P], XU[:, up, s, k * P:(k + 1) * P],
                                     PT[:, s, :], start=True, stop=True)
            U["po_ps"].by(last)

        def turn_x(u2, up):
            ge(pe, U["pt"], u2)
            ge(pe, u_x, u2 + 2, 8)
            for k in range(KD):
                for s in range(2):
                    last = pe.transpose(F0[:, k * UT + s * P:k * UT + (s + 1) * P], XU[:, up, s, k * P:(k + 1) * P],
                                        ident[:, :])
            U["xt_ps"].by(last)

        def inner_layer(u2):
            ge(pe, U["xt"], u2 + 2)
            ge(pe, U["po"], u2)
            for k in range(KD):
                last = pe.matmul(F1[0:A, 0:UT], w1[:, k, :], XT[:, k, :], start=(k == 0), stop=(k == KD - 1))
            U["at_ps"].by(last)

        def pooling_scores():
            for b in range(2):
                last = pe.matmul(F1[S * b:S * b + S, UT:UT + P].rearrange("p (s l) -> p s l", s=2), vrep[:, :],
                                 AT[:, :].rearrange("a (s b l) -> a s b l", s=2, b=2)[:, :, b, :],
                                 start=True, stop=True)
            U["sc_ps"].by(last)

        n_s, n_t, n_v, n_g = t - LS, t - LT_, t - LV, t - LG
        if has_pair(n_s):
            scores(n_s)
        f = on_unit(t, j, 0)
        if f:
            queries(f[0])
        if has_pair(n_g):
            turn_heads_out(n_g)
        if f:
            latent(f[0])
        f3 = on_unit(t, j, 3)
        if f3:
            project_values(*f3)
        f1 = on_unit(t, j, -1)
        if f1:
            turn_pooling(f1[0])
        if has_pair(n_t):
            turn_weights(n_t)
        if has_pair(n_g):
            project_out(n_g)
        if f:
            keys(*f)
        if f1:
            pool(*f1)
        fx = on_unit(t, j, -3)
        if fx:
            turn_x(*fx)
        if has_pair(n_v):
            values(n_v, 0)
        if fx:
            inner_layer(fx[0])
            if not has_pair(n_v):
                ge(pe, U["at"], fx[0] + 2)
        if has_pair(n_v):
            if fx:
                ge(pe, U["at"], fx[0] + 2)
            values(n_v, 1)
        if fx:
            pooling_scores()

    def act_slot(act, t, j):
        def halves(x):
            return x.rearrange("p (k t) -> p k t", k=KD)

        f, f1, fx, f3 = (on_unit(t, j, start) for start in (0, -1, -3, 3))
        fs = on_unit(t, j, -2)
        if f:
            u2, up = f
            ge(act, U["q_ps"], u2 + 2)
            ge(act, u_qk_out, u2, 32)
            U["qhi"].by(act.activation(QK[:, 0, :, :], halves(F0[:, :]), ACT.Copy, scale=QSCALE))
        if fs:
            ge(act, U["sc_c"], fs[0] + 2)
            U["sc_e"].by(act.activation(SM[:, :, :], SM[:, :, :], ACT.Exp))
        n = t - LG
        if has_pair(n):
            ge(act, R["ot_ps"], n + 1)
            R["ot"].by(act.activation(OT[:, :, :], halves(G[:, 0:KD * P]), ACT.Copy))
        if f:
            ge(act, U["lt_ps"], u2 + 2)
            ge(act, U["v_ps"], u2 - 2)
            U["lt"].by(act.activation(LT[:, up, :], F1[0:L, 0:UT], ACT.Copy))
        if f3:
            u2, up = f3
            ge(act, U["v_ps"], u2 + 2)
            ge(act, R["o_ps"], u2 - 2)
            for e in range(2):
                for b in range(2):
                    last = act.activation(
                        VB[S * e:S * e + S, up, :, b, :, e * DH:(e + 1) * DH],
                        F1[S * b:S * b + S, :].rearrange("p (s h e d) -> p s h e d", s=2, h=HP, e=2)[:, :, :, e, :],
                        ACT.Copy)
                U[f"vb{e}"].by(last)
        if f1:
            ge(act, U["pt_ps"], f1[0] + 2)
            U["pt"].by(act.activation(PT[:, :, :], F0[:, 0:UT].rearrange("p (s t) -> p s t", s=2), ACT.Copy))
        n = t - LT_
        if has_pair(n):
            for half in range(2):
                ge(act, R[f"t_ps{half}"], n + 1)
                ge(act, R["o_ps"], n - 1)
                R[f"px{half}"].by(act.activation(
                    PX[:, (j - LT_) % 2, 4 * half:4 * half + 4, :],
                    Tpair[:, 512 * half:512 * half + 512].rearrange("p (h t) -> p h t", h=4), ACT.Exp))
        if f:
            ge(act, U["k_ps"], f[0] + 2)
            U["khi"].by(act.activation(QK[:, 2, :, :], halves(F0[:, :]), ACT.Copy))
        if f1:
            ge(act, U["po_ps"], f1[0] + 2)
            U["po"].by(act.activation(PO[:, :, :], halves(F1[:, :]), ACT.Copy))
        if fx:
            ge(act, U["xt_ps"], fx[0] + 2)
            U["xt"].by(act.activation(XT[:, :, :], halves(F0[:, :]), ACT.Copy))
            ge(act, U["at_ps"], fx[0] + 2)
            U["at"].by(act.activation(AT[:, :], F1[0:A, 0:UT], ACT.Tanh, bias=b1[:, 0:1]))

    def dve_slot(dve, t, j):
        f, fs = on_unit(t, j, 0), on_unit(t, j, -2)
        n_g, n_s = t - LG, t - LS
        o = O[:, 0:HP * VW].rearrange("p (h c) -> p h c", h=HP)
        par = (j - LS) % 2
        w = W[:, par, :, :]
        flat = w.rearrange("p h s -> p (h s)")
        if has_pair(n_g):
            ge(dve, R["o_ps"], n_g + 1)
            R["rec"].by(dve.reciprocal(rec[:, :, :], o[:, :, 2 * DH:VW]))
        if fs:
            u2 = fs[0]
            ge(dve, U["sc_ps"], u2 + 2)
            caps = cap[:, u2:u2 + 2, :] if isinstance(u2, int) else cap[:, bass.ds(u2.reg(), 2), :]
            U["sc_a"].by(dve.tensor_tensor(SM[:, :, :], F1[:, UT:UT + P].rearrange("p (s l) -> p s l", s=2), caps,
                                           ALU.min))
        if has_pair(n_g):
            ge(dve, R["rec"], n_g + 1)
            ge(dve, R["ot_ps"], n_g)
            R["on"].by(dve.tensor_tensor(ON[:, :, :, :], o[:, :, 0:2 * DH].rearrange("p h (e d) -> p h e d", e=2),
                                         rec[:, :, :].unsqueeze(3).broadcast_to([P, HP, 2, DH]), ALU.mult))
        if fs:
            ge(dve, U["sc_a"], u2 + 2)
            U["sc_b"].by(dve.tensor_reduce(smx[:, :], SM[:, :, :], AX, ALU.max))
        if has_pair(n_s):
            ge(dve, R["s_ps"], n_s + 1)
            ge(dve, R["t_ps1"], n_s - 1)
            R["clip"].by(dve.tensor_scalar(flat, Spair[:, :], -CLAMP, CLAMP, ALU.max, ALU.min))
        if fs:
            ge(dve, U["sc_b"], u2 + 2)
            U["sc_c"].by(dve.tensor_tensor(SM[:, :, :], SM[:, :, :], smx[:, :].unsqueeze(2).broadcast_to([P, 2, S]),
                                           ALU.subtract))
        if has_pair(n_s):
            ge(dve, R["clip"], n_s + 1)
            R["dec"].by(dve.tensor_tensor(w, w, decay[:, :].unsqueeze(1).broadcast_to([P, NH, S]), ALU.mult))
        if f:
            ge(dve, U["qhi"], f[0] + 2)
            U["qlo"].by(dve.scalar_tensor_tensor(
                out=QK[:, 1, :, :].rearrange("p k t -> p (k t)"), in0=F0[:, :], scalar=QSCALE,
                in1=QK[:, 0, :, :].rearrange("p k t -> p (k t)"), op0=ALU.mult, op1=ALU.subtract))
        if fs:
            ge(dve, U["sc_e"], u2 + 2)
            U["sc_f"].by(dve.tensor_reduce(ssum[:, :], SM[:, :, :], AX, ALU.add))
        if has_pair(n_s):
            ge(dve, R["dec"], n_s + 1)
            R["max"].by(dve.tensor_reduce(rowmax[:, par, :], w, AX, ALU.max))
        if fs:
            cnts = count[:, u2:u2 + 2] if isinstance(u2, int) else count[:, bass.ds(u2.reg(), 2)]
            ge(dve, U["sc_f"], u2 + 2)
            U["sc_g"].by(dve.tensor_tensor(ssum[:, :], ssum[:, :], cnts, ALU.mult))
        if has_pair(n_g):
            ge(dve, R["g_ps"], n_g + 1)
            ge(dve, p_xr, n_g + 1, 16)
            xr = XR[:, (j - LG) % 2, :]
            R["x1"].by(dve.tensor_tensor(xr, xr, G[:, D:2 * D], ALU.add))
        if fs:
            ge(dve, U["sc_g"], u2 + 2)
            U["sc_h"].by(dve.reciprocal(ssum[:, :], ssum[:, :]))
        if has_pair(n_s):
            ge(dve, R["max"], n_s + 1)
            R["sub"].by(dve.tensor_tensor(w, w, rowmax[:, par, :].unsqueeze(2).broadcast_to([P, NH, S]),
                                          ALU.subtract))
        if fs:
            ge(dve, U["sc_h"], u2 + 2)
            ge(dve, U["pt_ps"], u2)
            for b in range(2):
                rows = slice(S * b, S * b + S)
                last = dve.tensor_tensor(PB[rows, :, S * b:S * b + S], SM[rows, :, :],
                                         ssum[rows, :].unsqueeze(2).broadcast_to([S, 2, S]), ALU.mult)
            U["pb"].by(last)
        if f:
            ge(dve, U["khi"], f[0] + 2)
            U["klo"].by(dve.tensor_tensor(QK[:, 3, :, :].rearrange("p k t -> p (k t)"), F0[:, :],
                                          QK[:, 2, :, :].rearrange("p k t -> p (k t)"), ALU.subtract))

    x_rows = io["x"].rearrange("b s d -> (b s) d")

    def sp_slot(sp, t, j):
        n = t - LV
        if has_pair(n):
            ge(sp, p_xr, n, 16)
            ge(sp, p_out, n - 1, 16)
            p_xr.by(sp.dma_start(XR[:, (j - LV) % 2, :], x_rows[bass.ds(val(n, P), P), :]))
        f = on_unit(t, j, -4)
        if f:
            u2, up = f
            ge(sp, U["po_ps"], u2 - 2)
            ge(sp, u_x, u2, 8)
            rows = bass.ds(val(u2, P), UT)
            u_x.by(sp.dma_start(XU[:, up, :, :], x_rows[rows, :].rearrange("(s p) d -> p s d", p=P)))
        f = on_unit(t, j, 0)

        def parts_out(parts):
            for i, k in parts:
                ge(sp, U[k], f[0] + 2)
                u_qk_out.by(sp.dma_start(qk_dram[f[1], i].rearrange("(k p) t -> p k t", p=P), QK[:, i, :, :]))

        if f:
            ge(sp, u_qs, f[0] - 2, 72)
            parts_out(((0, "qhi"), (1, "qlo")))
        f1 = on_unit(t, j, 1)
        if f1:
            u2, up = f1
            ge(sp, u_qk_out, u2 + 2, 32)
            ge(sp, R["s_ps"], u2 - 2)
            for part, (qi, ki) in enumerate(((0, 2), (0, 3), (1, 2))):
                rows = slice(32 * part, 32 * part + 32)
                u_qs.by(sp.dma_start(QS[rows, up, :, :], qk_dram[up, qi].rearrange("(h p) t -> p h t", p=32)))
                for e in range(2):
                    r0 = 32 * part + DH * e
                    u_qs.by(sp.dma_start(KS[r0:r0 + DH, up, :, e, :], qk_dram[up, ki].rearrange(
                        "(h e p) t -> e p h t", e=2, p=DH)[e]))
        n = t - LG
        if has_pair(n):
            ge(sp, R["x1"], n + 1)
            p_out.by(sp.dma_start(x1_dram[bass.ds(val(n, P), P), :], XR[:, (j - LG) % 2, :]))
        if f:
            parts_out(((2, "khi"), (3, "klo")))

    with nc.Block() as block:
        @block.tensor
        def _(pe):
            run(pe, lambda t, j: pe_slot(pe, t, j))

        @block.scalar
        def _(act):
            run(act, lambda t, j: act_slot(act, t, j))

        @block.vector
        def _(dve):
            run(dve, lambda t, j: dve_slot(dve, t, j))

        @block.sync
        def _(sp):
            sp_slot(sp, -4, 0)
            run(sp, lambda t, j: sp_slot(sp, t, j))
            ge(sp, p_out, NPAIR, 16)

        if beside_pool:
            @block.gpsimd
            def _(pool):
                beside_pool(pool)


NP_ = 8
BN = 128
E = 8
GT = 4
GROUP = GT * P
NGROUP = T // GROUP
FT = 256
CAP = T + FT
META = 4
RW = D + META
NTILE = 2 * T // FT + E - 1
NTILE += NTILE % 2
SPARE = E * CAP
NOWHERE = float(1 << 20)
EPS = 1e-5


def dispatch(nc, io, sb, made, dram, ps, ident, x1_dram, xs_dram, table_i, table_f):
    F0, F1, G, O, Spair, Tpair = (ps[k] for k in ("F0", "F1", "G", "O", "Spair", "Tpair"))
    prof_i = sb("prof_i", [P, B], I32)
    prof = sb("prof", [P, B])
    row_of = sb("row_of", [P, 1])
    onehot = sb("onehot", [P, B], BF16)
    raw = sb("raw", [32, 3 * D + BN])
    rest = sb("rest", [32, 3 * D + BN])
    parts = sb("parts", [3 * 32, 3 * D + BN], BF16)
    ohg = sb("ohg", [3 * 32, 2, 2 * GT, S], BF16)
    cent = sb("cent", [E, D])
    centT = sb("centT", [P, KD, E])
    c2 = sb("c2", [P, E])
    cbc = sb("cbc", [P, E, D])
    upper = sb("upper", [P, P], BF16)
    ones = sb("ones", [P, P], BF16)
    rev = sb("rev", [P, E])
    ramp = sb("ramp", [P, NTILE])
    steps = sb("steps", [P, T // FT])
    tok = sb("tok", [P, GT])
    ce = sb("ce", [P, E])
    ce_i = sb("ce_i", [P, E], I32)
    pad = sb("pad", [P, 2, RW])
    spare = sb("spare", [P, 2])
    X1 = sb("X1", [P, 2, GT, D])
    XT = sb("X1T", [P, KD, GROUP])
    WD = sb("WD", [P, 2, 2 * GT, KD, BN])
    WU = sb("WU", [P, 2, 2 * GT, D])
    ZT = sb("ZT", [BN, GROUP])
    Y = sb("Y", [P, GT, D])
    bst = sb("bst", [P, GT, 6])
    mv = sb("mv", [P, GT, 2])
    std = sb("std", [P, GT])
    rstd = sb("rstd", [P, GT])
    ROW = sb("ROW", [P, 2, GT, RW])
    HT = sb("HT", [P, KD, GROUP])
    sq = sb("sq", [P, D])
    x2 = sb("x2", [P, GT])
    small = [P, GT, E]
    d2, eq, tmp, ohlo, ohhi = (sb(n, small) for n in ("d2", "eq", "tmp", "ohlo", "ohhi"))
    m12 = sb("m12", [P, 2, GT])
    s12 = sb("s12", [P, 2, GT])
    r12 = sb("r12", [P, 2, GT])
    first = sb("first", [P, GT])
    ex = sb("ex", [P, GT])
    w12 = sb("w12", [P, 2, GT])
    oh1 = sb("oh1", small)
    oh2 = sb("oh2", small)
    M = sb("M", small, BF16)
    pos = sb("pos", [P, 2, GT])
    idx = sb("idx", [P, 2, 2, GT], I32)
    nt = sb("nt", [P, E])
    cnt = sb("cnt", [P, E])
    incl = sb("incl", [P, E])
    zero8 = sb("zero8", [P, E])
    big = sb("big", [P, NTILE, E])
    big2 = sb("big2", [P, E, T // FT])
    sumt = sb("sumt", [P, NTILE])

    c_w, c_c, c_v, c_a, c_p, c_r = made("c_w", 16), made("c_c"), made("c_v"), made("c_a"), made("c_p"), made("c_r", 16)
    tables = ("L0_cond2_up_b", "L0_cond2_ln_g", "L0_cond2_ln_b", "L0_cond2_down_b")
    loads = [(prof_i[:, :], io["itok_B_0_6"].rearrange("(o b) -> o b", o=1).broadcast_to([P, B])),
             (cent[:, :], io["L0_ffn_centroid"]),
             (cbc[:, :, :], io["L0_ffn_centroid"].rearrange("(o e) d -> o e d", o=1).broadcast_to([P, E, D]))]
    late = [(raw[0:NP_, i * D:i * D + (BN if i == 3 else D)], io[k]) for i, k in enumerate(tables)]
    NW = len(loads) + len(late)
    with nc.Block() as block:
        @block.sync
        def _(sp):
            for o, i in loads:
                c_w.by(sp.dma_start(o, i))
            c_c.wait(sp, 1)
            for o, i in late:
                c_w.by(sp.dma_start(o, i))
            c_c.wait(sp, 9)
            for s in range(2):
                c_r.by(sp.dma_start(xs_dram[SPARE + s * P:SPARE + (s + 1) * P, :], pad[:, s, :]))
            c_r.wait(sp, 32)

        @block.gpsimd
        def _(pool):
            n = [0]

            def step(instruction):
                c_c.by(instruction)
                n[0] += 1
                c_c.wait(pool, n[0])

            step(pool.memset(raw[:, :], 0.0))
            for i in range(4):
                step(pool.iota(row_of[32 * i:32 * i + 32, :], pattern=[[0, 1]], base=0, channel_multiplier=1,
                               allow_small_or_imprecise_dtypes=True))
            step(pool.memset(ones[:, :], 1.0))
            step(pool.memset(pad[:, :, :], 0.0))
            step(pool.memset(pad[:, :, D + 2:D + 3], NOWHERE))
            pool.memset(spare[:, :], 0.0)
            step(pool.memset(zero8[:, :], 0.0))
            step(pool.affine_select(out=upper[:, :], in_=ones[:, :], compare_op=ALU.is_gt, fill=0.0, base=0,
                                    pattern=[[1, P]], channel_multiplier=-1))
            step(pool.iota(rev[:, :], pattern=[[-1, E]], base=E, channel_multiplier=0,
                           allow_small_or_imprecise_dtypes=True))
            step(pool.iota(ramp[:, :], pattern=[[1, NTILE]], base=0, channel_multiplier=0,
                           allow_small_or_imprecise_dtypes=True))
            step(pool.iota(steps[:, :], pattern=[[FT, T // FT]], base=0, channel_multiplier=0,
                           allow_small_or_imprecise_dtypes=True))
            step(pool.iota(tok[:, :], pattern=[[P, GT]], base=-GROUP, channel_multiplier=1,
                           allow_small_or_imprecise_dtypes=True))
            step(pool.iota(ce[:, :], pattern=[[CAP, E]], base=0, channel_multiplier=0,
                           allow_small_or_imprecise_dtypes=True))
            c_w.wait(pool, 16 * NW)
            step(pool.tensor_tensor(cbc[:, :, :], cbc[:, :, :], cbc[:, :, :], ALU.mult))

        @block.vector
        def _(dve):
            n = [0]

            def step(instruction):
                c_v.by(instruction)
                n[0] += 1
                c_v.wait(dve, n[0])

            c_w.wait(dve, 16 * NW)
            c_c.wait(dve, 15)
            step(dve.tensor_copy(prof[:, :], prof_i[:, :]))
            step(dve.tensor_scalar(onehot[:, :], prof[:, :], row_of[:, 0:1], None, ALU.is_equal))
            step(dve.tensor_copy(parts[0:32, :], raw[:, :]))
            step(dve.tensor_tensor(rest[:, :], raw[:, :], parts[0:32, :], ALU.subtract))
            step(dve.tensor_copy(parts[32:64, :], rest[:, :]))
            step(dve.tensor_tensor(rest[:, :], rest[:, :], parts[32:64, :], ALU.subtract))
            step(dve.tensor_copy(parts[64:96, :], rest[:, :]))
            c_c.wait(dve, 16)
            step(dve.tensor_reduce(c2[:, :], cbc[:, :, :], AX, ALU.add))
            c_p.wait(dve, 1)
            step(dve.tensor_scalar(centT[:, :, :], F0[:, 0:KD * E].rearrange("p (k e) -> p k e", k=KD), -2.0, None,
                                   ALU.mult))

        @block.tensor
        def _(pe):
            c_w.wait(pe, 16 * NW)
            for k in range(KD):
                last = pe.transpose(F0[:, k * E:(k + 1) * E], cent[:, k * P:(k + 1) * P], ident[0:E, 0:E])
            c_p.by(last)

    x1_in = [made(f"x1_in{j}", 16) for j in range(2)]
    w_in = [made(f"w_in{j}", 16) for j in range(2)]
    names = ["xT_ps", "xT", "ohg", "z_ps", "zt", "y_ps", "y", "bst", "mv", "std", "rstd", "veps",
             "gb_ps0", "gb_ps1", "hn", "hg0", "hg1", "hb0", "hb1",
             "hT_ps", "hT", "x2", "dot_ps", "d2a", "d2b", "d2", "m1", "eq1", "eqr1", "r1", "oh1", "d2m",
             "m2", "eq2", "eqr2", "r2", "oh2", "s12", "dif", "ex", "den", "rden", "w2", "first", "wd", "wf", "wlo", "whi",
             "rlo", "M", "ohlo", "ohhi", "rank_ps", "rank", "plo", "phi", "tlo", "idx", "ce", "tok", "tokw", "t2"]
    chains = [("d2b", "d2", "m1", "eq1"), ("eqr1", "r1", "oh1", "d2m"), ("eq2", "eqr2", "r2", "oh2"),
              ("rlo", "ohlo", "den", "rden"), ("tok", "w2", "wd", "wf"), ("wlo", "whi", "tokw", "plo"),
              ("first", "tlo", "t2", "phi"), ("bst", "mv", "rstd", "hn")]
    C = {k: made("c_" + k) for k in names if not any(k in c for c in chains)}
    place = {}
    for c in chains:
        C.update(dict.fromkeys(c, made("c_" + "_".join(c))))
        place.update((k, n) for n, k in enumerate(c))
    carried = made("dispatch_carried")
    rows_out = [made(f"rows_out{j}", 16) for j in range(2)]

    def ge(eng, m, x, mul=1):
        if isinstance(x, int):
            if x > 0:
                eng.wait_ge(m.sem, x * mul)
        else:
            eng.wait_ge(m.sem, x * mul if mul != 1 else x)

    def run(eng, body):
        for g in range(-1, 3):
            body(g, g % 2)
        with eng.Fori(3, NGROUP - 2, 2) as g:
            for j in range(2):
                body(g + j, (1 + j) % 2)
        body(NGROUP - 1, (NGROUP - 1) % 2)
        body(NGROUP, NGROUP % 2)

    def x1_loaded(eng, n, j):
        ge(eng, x1_in[j], n + (1 - j), 8)

    def front(g):
        return not isinstance(g, int) or 0 <= g < NGROUP

    def back(g):
        return not isinstance(g, int) or g > 0

    def ahead(g):
        return not isinstance(g, int) or g + 1 < NGROUP

    def pe_slot(pe, g, j):
        def ranks(x):
            ge(pe, C["M"], x)
            ge(pe, C["d2a"], x)
            at = O[:, 64:64 + GT * E]
            for s in range(GT):
                last = pe.matmul(at[:, s * E:(s + 1) * E], upper[:, :], M[:, s, :], start=True, stop=(s == 0))
                for q in range(s):
                    last = pe.matmul(at[:, s * E:(s + 1) * E], ones[:, :], M[:, q, :], start=False, stop=(q == s - 1))
            for q in range(GT):
                last = pe.matmul(O[:, 128:128 + E], ones[:, :], M[:, q, :], start=(q == 0), stop=(q == GT - 1))
            C["rank_ps"].by(last)

        def turned(rows, done):
            for k in range(KD):
                for s in range(GT):
                    last = pe.transpose((F0, F1)[k][:, s * P:(s + 1) * P], rows[:, s, k * P:(k + 1) * P], ident[:, :])
            C[done].by(last)

        def gains(half):
            ge(pe, C["hb0" if half else "hb1"], g + half)
            for s in range(2 * half, 2 * half + 2):
                last = pe.matmul(Tpair[:, (s % 2) * 512:(s % 2) * 512 + 512],
                                 ohg[:, j, 2 * s:2 * s + 2, :].rearrange("r b s -> r (b s)"), parts[:, D:3 * D],
                                 start=True, stop=True)
            C[f"gb_ps{half}"].by(last)

        def down(b0, b1):
            for b in range(b0, b1):
                for k in range(KD):
                    last = pe.matmul(G[:, b * S:(b + 1) * S], WD[:, 1 - j, b, k, :], XT[:, k, b * S:(b + 1) * S],
                                     start=False, stop=(k == KD - 1), skip_group_check=True)
            return last

        if ahead(g):
            x1_loaded(pe, g + 2, 1 - j)
            ge(pe, C["hT"], g - 1)
            turned(X1[:, 1 - j, :, :], "xT_ps")
        if front(g):
            ge(pe, C["zt"], g + 1)
            ge(pe, C["y"], g)
            for s in range(GT):
                pe.matmul(Spair[:, s * D:(s + 1) * D], ohg[:, j, 2 * s:2 * s + 2, :].rearrange("r b s -> r (b s)"),
                          parts[:, 0:D], start=True, stop=False, skip_group_check=True)
                for h in range(2):
                    b = 2 * s + h
                    last = pe.matmul(Spair[S * h:S * h + S, s * D:(s + 1) * D], ZT[:, b * S:(b + 1) * S], WU[:, j, b, :],
                                     start=False, stop=True, skip_group_check=True)
            C["y_ps"].by(last)
        if back(g):
            ge(pe, C["hb1"], g)
            ge(pe, C["xT"], min(g + 2, NGROUP) if isinstance(g, int) else g + 2)
            turned(ROW[:, 1 - j, :, :], "hT_ps")
        if front(g):
            gains(0)
        if ahead(g):
            ge(pe, C["ohg"], g + 2)
            ge(pe, C["zt"], g + 1)
            pe.matmul(G[:, :], parts[:, 3 * D:3 * D + BN], ohg[:, 1 - j, :, :].rearrange("r b s -> r (b s)"),
                      start=True, stop=False, skip_group_check=True)
            ge(pe, C["xT"], g + 2)
            ge(pe, w_in[1 - j], g + 2 + j, 8 * 4 * GT)
            down(0, 2)
        if back(g):
            ge(pe, C["hT"], g)
            ge(pe, C["ce"], g - 1)
            for s in range(GT):
                for k in range(KD):
                    last = pe.matmul(O[:, s * E:(s + 1) * E], HT[:, k, s * P:(s + 1) * P], centT[:, k, :],
                                     start=(k == 0), stop=(k == KD - 1))
            C["dot_ps"].by(last)
        if ahead(g):
            C["z_ps"].by(down(2, 2 * GT))
        if back(g):
            ranks(g)
        if front(g):
            gains(1)

    def act_slot(act, g, j):
        if ahead(g):
            ge(act, C["xT_ps"], g + 2)
            act.activation(XT[:, 0, :], F0[:, :], ACT.Copy)
            C["xT"].by(act.activation(XT[:, 1, :], F1[:, :], ACT.Copy))
        if ahead(g):
            ge(act, C["gb_ps1"], g)
            at = 2 * GT * (g + 1) if isinstance(g, int) else g * (2 * GT) + 2 * GT
            C["ohg"].by(act.activation(ohg[:, 1 - j, :, :],
                                       onehot[0:96, bass.ds(at, 2 * GT)].unsqueeze(2).broadcast_to([96, 2 * GT, S]),
                                       ACT.Copy))
        if back(g):
            ge(act, C["hT_ps"], g)
            act.activation(HT[:, 0, :], F0[:, :], ACT.Copy)
            C["hT"].by(act.activation(HT[:, 1, :], F1[:, :], ACT.Copy))
        if front(g):
            ge(act, C["veps"], g + 1)
            C["std"].by(act.activation(std[:, :], std[:, :], ACT.Sqrt))
        if back(g):
            for s in range(GT):
                ge(act, C["x2"], (g - 1) * GT + s)
                C["x2"].by(act.activation(sq[:, :], ROW[:, 1 - j, s, 0:D], ACT.Square, accum_out=x2[:, s:s + 1]))
            ge(act, C["m2"], g)
            C["s12"].by(act.activation(s12[:, :, :], m12[:, :, :], ACT.Sqrt))
            ge(act, C["dif"], g)
            C["ex"].by(act.activation(ex[:, :], ex[:, :], ACT.Exp))
        if ahead(g):
            ge(act, C["z_ps"], g + 2)
            C["zt"].by(act.activation(ZT[:, :], G[:, :], ACT.Relu))

    GB = Tpair[:, :].rearrange("p (s c d) -> p s c d", s=2, c=2)

    def dve_slot(dve, g, j):
        bc4 = lambda x: x.unsqueeze(2).broadcast_to(small)
        bce = lambda x: x.unsqueeze(1).broadcast_to(small)

        values = {}

        def after(name, x):
            if name not in place:
                ge(dve, C[name], x)
            elif isinstance(x, int):
                ge(dve, C[name], 4 * (x - 1) + place[name] + 1)
            else:
                n, fore = place[name], name in chains[-1]
                if (n, fore) not in values:
                    values[n, fore] = x * 4 + (n - 3)
                dve.wait_ge(C[name].sem, values[n, fore])

        if front(g):
            front_dve(dve, g, j, after)
        if back(g):
            x = g

            def do(name, instruction, *needs):
                C[name].by(instruction)

            after("dot_ps", x)
            do("d2a", dve.tensor_tensor(d2[:, :, :], O[:, 0:GT * E].rearrange("p (s e) -> p s e", s=GT), bce(c2[:, :]),
                                        ALU.add))
            after("d2a", x)
            ge(dve, C["x2"], x * GT)
            do("d2b", dve.tensor_tensor(d2[:, :, :], d2[:, :, :], bc4(x2[:, :]), ALU.add))
            after("d2b", x)
            do("d2", dve.tensor_scalar(d2[:, :, :], d2[:, :, :], 1e-12, None, ALU.max))
            after("d2", x)
            do("m1", dve.tensor_reduce(m12[:, 0, :], d2[:, :, :], AX, ALU.max))
            after("m1", x)
            do("eq1", dve.tensor_tensor(eq[:, :, :], d2[:, :, :], bc4(m12[:, 0, :]), ALU.is_equal))
            after("eq1", x)
            do("eqr1", dve.tensor_tensor(eq[:, :, :], eq[:, :, :], bce(rev[:, :]), ALU.mult))
            after("eqr1", x)
            do("r1", dve.tensor_reduce(r12[:, 0, :], eq[:, :, :], AX, ALU.max))
            after("r1", x)
            do("oh1", dve.tensor_tensor(oh1[:, :, :], bc4(r12[:, 0, :]), bce(rev[:, :]), ALU.is_equal))
            after("oh1", x)
            do("d2m", dve.scalar_tensor_tensor(out=d2[:, :, :], in0=oh1[:, :, :], scalar=-3.0e38, in1=d2[:, :, :],
                                               op0=ALU.mult, op1=ALU.add))
            after("d2m", x)
            do("m2", dve.tensor_reduce(m12[:, 1, :], d2[:, :, :], AX, ALU.max))
            after("m2", x)
            do("eq2", dve.tensor_tensor(eq[:, :, :], d2[:, :, :], bc4(m12[:, 1, :]), ALU.is_equal))
            after("eq2", x)
            do("eqr2", dve.tensor_tensor(eq[:, :, :], eq[:, :, :], bce(rev[:, :]), ALU.mult))
            after("eqr2", x)
            do("r2", dve.tensor_reduce(r12[:, 1, :], eq[:, :, :], AX, ALU.max))
            after("r2", x)
            do("oh2", dve.tensor_tensor(oh2[:, :, :], bc4(r12[:, 1, :]), bce(rev[:, :]), ALU.is_equal))
            after("oh2", x)
            ge(dve, C["rank_ps"], x - 1)
            do("M", dve.tensor_tensor(M[:, :, :], oh1[:, :, :], oh2[:, :, :], ALU.add))
            do("first", dve.tensor_tensor(first[:, :], r12[:, 0, :], r12[:, 1, :], ALU.is_gt))
            ge(dve, C["hT_ps"], x)
            rl = ROW[:, 1 - j, :, D + 3]
            do("rlo", dve.tensor_tensor(rl, r12[:, 0, :], r12[:, 1, :], ALU.max))
            after("rlo", x)
            do("ohlo", dve.tensor_tensor(ohlo[:, :, :], bc4(rl), bce(rev[:, :]), ALU.is_equal))
            after("ohlo", x)
            after("M", x)
            do("ohhi", dve.tensor_tensor(ohhi[:, :, :], M[:, :, :], ohlo[:, :, :], ALU.subtract))
            after("s12", x)
            do("dif", dve.tensor_tensor(ex[:, :], s12[:, 1, :], s12[:, 0, :], ALU.subtract))
        if front(g):
            ge(dve, rows_out[j], g - j, 16 * GT)
            shift(dve, g, j, 0, after)
            gain(dve, g, 1, after)
            shift(dve, g, j, 1, after)
        if back(g):
            after("ex", x)
            if not front(g):
                do("tok", dve.tensor_scalar(tok[:, :], tok[:, :], float(GROUP), None, ALU.add))
            do("den", dve.tensor_scalar(w12[:, 0, :], ex[:, :], 1.0, None, ALU.add))
            after("den", x)
            do("rden", dve.reciprocal(w12[:, 0, :], w12[:, 0, :]))
            after("rden", x)
            do("w2", dve.tensor_tensor(w12[:, 1, :], w12[:, 0, :], ex[:, :], ALU.mult))
            after("w2", x)
            do("wd", dve.tensor_tensor(ex[:, :], w12[:, 0, :], w12[:, 1, :], ALU.subtract))
            after("wd", x)
            after("first", x)
            do("wf", dve.tensor_tensor(ex[:, :], ex[:, :], first[:, :], ALU.mult))
            after("wf", x)
            do("wlo", dve.tensor_tensor(ROW[:, 1 - j, :, D], w12[:, 1, :], ex[:, :], ALU.add))
            do("whi", dve.tensor_tensor(ROW[:, 1 - j, :, D + 1], w12[:, 0, :], ex[:, :], ALU.subtract))
            after("tok", x)
            do("tokw", dve.tensor_copy(ROW[:, 1 - j, :, D + 2], tok[:, :]))
            after("rank_ps", x)
            do("rank", dve.tensor_tensor(tmp[:, :, :], O[:, 64:64 + GT * E].rearrange("p (s e) -> p s e", s=GT),
                                         bce(ce[:, :]), ALU.add))
            after("rank", x)
            after("ohhi", x)
            do("tlo", dve.tensor_tensor(ohlo[:, :, :], ohlo[:, :, :], tmp[:, :, :], ALU.mult))
            do("t2", dve.tensor_tensor(ohhi[:, :, :], ohhi[:, :, :], tmp[:, :, :], ALU.mult))
            do("ce", dve.tensor_tensor(ce[:, :], ce[:, :], O[:, 128:128 + E], ALU.add))
            after("tlo", x)
            after("t2", x)
            do("plo", dve.tensor_reduce(pos[:, 0, :], ohlo[:, :, :], AX, ALU.add))
            do("phi", dve.tensor_reduce(pos[:, 1, :], ohhi[:, :, :], AX, ALU.add))
            after("plo", x)
            after("phi", x)
            ge(dve, rows_out[1 - j], x - 2 + j, 16 * GT)
            after("whi", x)
            after("wlo", x)
            after("tokw", x)
            do("idx", dve.tensor_copy(idx[:, 1 - j, :, :], pos[:, :, :]))

    def front_dve(dve, g, j, after):
        x = g + 1
        after("hb1", g)
        after("y_ps", x)
        C["y"].by(dve.tensor_tensor(Y[:, :, :], Spair[:, :].rearrange("p (s d) -> p s d", s=GT), X1[:, j, :, :],
                                    ALU.add))
        after("y", x)
        for s in range(GT):
            last = dve.bn_stats(bst[:, s, :], Y[:, s, :])
        C["bst"].by(last)
        after("bst", x)
        if back(g):
            C["tok"].by(dve.tensor_scalar(tok[:, :], tok[:, :], float(GROUP), None, ALU.add))
        for s in range(GT):
            last = dve.bn_aggr(mv[:, s, :], bst[:, s, :])
        C["mv"].by(last)
        after("mv", x)
        C["veps"].by(dve.tensor_scalar(std[:, :], mv[:, :, 1], EPS, None, ALU.add))
        after("std", x)
        C["rstd"].by(dve.reciprocal(rstd[:, :], std[:, :]))
        after("rstd", x)
        for s in range(GT):
            last = dve.tensor_scalar(Y[:, s, :], Y[:, s, :], mv[:, s, 0:1], rstd[:, s:s + 1], ALU.subtract, ALU.mult)
        C["hn"].by(last)
        after("hn", x)
        gain(dve, g, 0, after)

    def gain(dve, g, half, after):
        ss = slice(2 * half, 2 * half + 2)
        after(f"gb_ps{half}", g + 1)
        C[f"hg{half}"].by(dve.tensor_tensor(Y[:, ss, :], Y[:, ss, :], GB[:, :, 0, :], ALU.mult))

    def shift(dve, g, j, half, after):
        ss = slice(2 * half, 2 * half + 2)
        after(f"hg{half}", g + 1)
        C[f"hb{half}"].by(dve.tensor_tensor(ROW[:, j, ss, 0:D], Y[:, ss, :], GB[:, :, 1, :], ALU.add))

    def pool_slot(pool, g, j):
        if back(g):
            ge(pool, C["idx"], g)
            carry(pool, spare, carried, g - 1)
            for k in range(2):
                for s in range(GT):
                    rows_out[1 - j].by(pool.indirect_dma_start(
                        xs_dram, bass.IndirectOffsetOnAxis(idx[:, 1 - j, k, s:s + 1], 0), ROW[:, 1 - j, s, :], None))

    x1_rows = x1_dram.rearrange("(n p) d -> p n d", p=P)
    NREG = 8

    def sp_load(sp, g, j):
        ge(sp, C["xT_ps"], g)
        ge(sp, C["y"], min(g, NGROUP - 1) if isinstance(g, int) else g)
        if ahead(g):
            tiles = bass.ds(g * GT + GT, GT)
            x1_in[1 - j].by(sp.dma_start(X1[:, 1 - j, :, :], x1_rows[:, tiles, :]))
        if ahead(g):
            ge(sp, C["z_ps"], g)
            ge(sp, C["y_ps"], g)
            for b in range(2 * GT):
                q = sp.value_load(prof_i[0:1, bass.ds(g * (2 * GT) + (2 * GT + b), 1)], min_val=0, max_val=NP_ - 1)
                w_in[1 - j].by(sp.dma_start(WD[:, 1 - j, b, :, :], io["L0_cond2_down_w"][bass.ds(q, 1)].rearrange(
                    "o (k p) n -> p (o k) n", p=P)))
                w_in[1 - j].by(sp.dma_start(WU[:, 1 - j, b, :], io["L0_cond2_up_w"][bass.ds(q, 1)].rearrange(
                    "o p n -> p (o n)")))

    with nc.Block() as block:
        @block.tensor
        def _(pe):
            run(pe, lambda g, j: pe_slot(pe, g, j))

        @block.scalar
        def _(act):
            run(act, lambda g, j: act_slot(act, g, j))

        @block.vector
        def _(dve):
            run(dve, lambda g, j: dve_slot(dve, g, j))
            ch = [0]
            done = C["t3"] = made("c_t3")

            def step(instruction):
                done.by(instruction)
                ch[0] += 1
                ge(dve, done, ch[0])

            ge(dve, C["ce"], NGROUP)
            step(dve.tensor_copy(ce_i[:, :], ce[:, :]))
            step(dve.scalar_tensor_tensor(out=cnt[:, :], in0=rev[:, :], scalar=float(CAP), in1=ce[:, :], op0=ALU.mult,
                                          op1=ALU.add))
            step(dve.tensor_scalar(cnt[:, :], cnt[:, :], -float(SPARE), None, ALU.add))
            step(dve.tensor_tensor(big2[:, :, :], cnt[:, :].unsqueeze(2).broadcast_to([P, E, T // FT]),
                                   steps[:, :].unsqueeze(1).broadcast_to([P, E, T // FT]), ALU.is_gt))
            step(dve.tensor_reduce(nt[:, :], big2[:, :, :], AX, ALU.add))
            step(dve.tensor_tensor_scan(incl[:, :], nt[:, :], zero8[:, :], 0.0, ALU.add, ALU.add))
            wide = [P, NTILE, E]
            step(dve.tensor_tensor(big[:, :, :], incl[:, :].unsqueeze(1).broadcast_to(wide),
                                   ramp[:, :].unsqueeze(2).broadcast_to(wide), ALU.is_le))
            step(dve.tensor_reduce(table_f[:, :], big[:, :, :], AX, ALU.add))
            step(dve.tensor_tensor(big[:, :, :], big[:, :, :], nt[:, :].unsqueeze(1).broadcast_to(wide), ALU.mult))
            step(dve.tensor_reduce(sumt[:, :], big[:, :, :], AX, ALU.add))
            step(dve.tensor_tensor(sumt[:, :], ramp[:, :], sumt[:, :], ALU.subtract))
            step(dve.tensor_scalar(sumt[:, :], sumt[:, :], float(FT), None, ALU.mult))
            step(dve.scalar_tensor_tensor(out=sumt[:, :], in0=table_f[:, :], scalar=float(CAP), in1=sumt[:, :],
                                          op0=ALU.mult, op1=ALU.add))
            step(dve.tensor_scalar(sumt[:, :], sumt[:, :], float(SPARE), None, ALU.min))
            step(dve.tensor_copy(table_i[:, 0, :], sumt[:, :]))
            step(dve.tensor_scalar(table_i[:, 1, :], table_f[:, :], float(E - 1), None, ALU.min))
            step(dve.memset(table_i[:, 2, 0:2], 1))
            step(dve.tensor_tensor(table_i[:, 2, 2:NTILE], table_i[:, 1, 2:NTILE], table_i[:, 1, 0:NTILE - 2],
                                   ALU.not_equal))
            step(dve.tensor_scalar(table_f[:, :], table_f[:, :], -1.0, float(E), ALU.mult, ALU.add))

        @block.gpsimd
        def _(pool):
            run(pool, lambda g, j: pool_slot(pool, g, j))
            for j in range(2):
                ge(pool, rows_out[j], NGROUP, 16 * GT)

        @block.sync
        def _(sp):
            run(sp, lambda g, j: sp_load(sp, g, j))
            done = C["t3"]
            ge(sp, done, 1)
            for e in range(E):
                r = sp.value_load(ce_i[0:1, e:e + 1], min_val=e * CAP, max_val=e * CAP + T)
                c_r.by(sp.dma_start(xs_dram[bass.ds(r, FT), :].rearrange("(s p) w -> p s w", p=P), pad[:, :, :]))
            c_r.wait(sp, 16 * (2 + E))


H = 684
NFULL = H // P
HR = H - NFULL * P
NBLK = 2 * NFULL + 1
NCH = NFULL + 1
UW = 2 * KD * NBLK * P
DW = 2 * NCH * D
FS = FT // P


def load_biases(nc, io, sb, made, ps, ident, bias):
    rows = sb("bias_rows", [NCH * E, 2, P])
    clear, arrived, turned, done = made("b_clear"), made("b_arrived", 16), made("b_turned"), made("b_done")

    with nc.Block() as block:
        @block.gpsimd
        def _(pool):
            clear.by(pool.memset(rows[:, :, :], 0.0))

        @block.sync
        def _(sp):
            clear.wait(sp, 1)
            for i, k in enumerate(("L0_ffn_bg", "L0_ffn_b1")):
                arrived.by(sp.dma_start(rows[0:E, i, 0:HR], io[k][:, NFULL * P:H]))
                for c in range(NFULL):
                    arrived.by(sp.dma_start(rows[(c + 1) * E:(c + 2) * E, i, :], io[k][:, c * P:(c + 1) * P]))

        @block.tensor
        def _(pe):
            arrived.wait(pe, 16 * 2 * NCH)
            for i in range(2):
                last = pe.transpose(ps["F0"][:, i * NCH * E:(i + 1) * NCH * E], rows[:, i, :],
                                    ident[0:NCH * E, 0:NCH * E])
            turned.by(last)

        @block.scalar
        def _(act):
            turned.wait(act, 1)
            for i in range(2):
                done.by(act.activation(bias[:, :, i * NCH:(i + 1) * NCH],
                                       ps["F0"][:, i * NCH * E:(i + 1) * NCH * E].rearrange(
                                           "p (c e) -> p e c", c=NCH), ACT.Copy))
            done.wait(act, 2)


def split_weights(nc, io, sb, made, pool, up_dram, dn_dram):
    up = sb("up_stage", [P, KD, NBLK, P])
    dn = sb("dn_stage", [P, NCH, D])
    upb = sb("up_parts", [P, 2, KD, NBLK, P], BF16)
    dnb = sb("dn_parts", [P, 2, NCH, D], BF16)
    spare = sb("split_spare", [P, 2])
    carried = made("split_carried")
    s_in, s_out, s_do = made("split_in", 16), made("split_out", 16), made("split_do")
    last = NBLK - 1
    s_do.by(pool.memset(up[:, :, last, :], 0.0))
    s_do.by(pool.memset(dn[:, NCH - 1, :], 0.0))
    s_do.by(pool.memset(spare[:, :], 0.0))
    s_do.wait(pool, 3)
    NIN, NDO = 7, 4

    def split(e):
        pick = bass.ds(e, 1)
        s_do.wait(pool, e * NDO + 3)
        wg, w1, w2 = (io[k][pick] for k in ("L0_ffn_Wg", "L0_ffn_W1", "L0_ffn_W2"))
        for i, w in enumerate((wg, w1)):
            rows = w.rearrange("o (k p) n -> p (o k) n", p=P)
            s_in.by(pool.dma_start(up[:, :, i * NFULL:(i + 1) * NFULL, :].rearrange("p k b n -> p k (b n)"),
                                   rows[:, :, 0:NFULL * P]))
            s_in.by(pool.dma_start(up[:, :, last, 64 * i:64 * i + HR], rows[:, :, NFULL * P:H]))
        s_in.by(pool.dma_start(dn[:, 0:NFULL, :], w2[:, 0:NFULL * P, :].rearrange("o (c p) d -> p (o c) d", p=P)))
        s_in.by(pool.dma_start(dn[0:HR, NFULL, :], w2[:, NFULL * P:H, :].rearrange("o p d -> p (o d)")))
        s_in.by(pool.dma_start(dn[HR:HR + 1, NFULL, :], io["L0_ffn_b2"][pick, :]))
        s_in.wait(pool, (e + 1) * (16 * NIN))
        s_out.wait(pool, e * 32)
        n = e * NDO
        for stage, parts in ((up, upb), (dn, dnb)):
            carry(pool, spare, carried, e * 2 + (0 if stage is up else 1))
            s_do.by(pool.tensor_copy(parts[:, 0], stage[:]))
            s_do.wait(pool, n + (4 if stage is up else 6))
            s_do.by(pool.tensor_tensor(parts[:, 1], stage[:], parts[:, 0], ALU.subtract))
            s_do.wait(pool, n + (5 if stage is up else 7))
        s_out.by(pool.dma_start(up_dram[pick].rearrange("o p w -> p (o w)"),
                                upb[:, :, :, :, :].rearrange("p a k b n -> p (a k b n)")))
        s_out.by(pool.dma_start(dn_dram[pick].rearrange("o p w -> p (o w)"),
                                dnb[:, :, :, :].rearrange("p a c d -> p (a c d)")))

    split(0)
    with pool.Fori(1, E, 1) as e:
        split(e)
    s_out.wait(pool, 32 * E)


def experts(nc, io, sb, made, ps, ident, bias, xs_dram, up_dram, dn_dram, table_i, table_f, out):
    Spair, Tpair = ps["Spair"], ps["Tpair"]
    GU = [Spair[:, 0:512], Spair[:, 512:1024], Tpair[:, 0:512], Tpair[:, 512:1024]]
    YP = [ps["F1"], ps["O"]]
    XP = ps["G"]
    XR = sb("rows", [P, 2, FS, RW])
    XT = sb("rowsT", [P, 2, KD, FT], BF16)
    UP = sb("UP", [P, 2, 2, KD, NBLK, P], BF16)
    DN = sb("DN", [P, 2, 2, NCH, D], BF16)
    BT = sb("BT", [P, 2, 2 * NCH])
    SIL = sb("SIL", [P, 2, FT])
    H32 = sb("H32", [P, 2, FT])
    UR = sb("UR", [HR, FT])
    HT = sb("innerT", [P, 2, NCH, FT], BF16)
    Z = sb("Z", [P, 2, FS, D])
    idx = sb("row_idx", [P, 2, FS], I32)
    wt = sb("row_wt", [P, 2, FS])
    islo = sb("islo", [P, FS])
    tl = sb("tl", [P, FS])
    spare = sb("expert_spare", [P, 2])

    e_set, spared, carried = made("e_set"), made("spared"), made("carried")
    xr_in, up_in, dn_in, bt_in, z_in, sent = ([made(f"{k}{j}", 16) for j in range(2)]
                                              for k in ("xr_in", "up_in", "dn_in", "bt_in", "z_in", "sent"))
    gu, sil, h32, hhi, hlo = ([made(f"{k}{c}") for c in range(3)] for k in ("gu", "sil", "h32", "hhi", "hlo"))
    ur, xT_ps, xhi, xlo, y_ps, yo, ilo, wl, wh, wdone, idone = (made("e_" + k) for k in (
        "ur", "xT_ps", "xhi", "xlo", "y_ps", "yo", "ilo", "wl", "wh", "wdone", "idone"))

    def ge(eng, m, x, mul=1):
        if isinstance(x, int):
            if x > 0:
                eng.wait_ge(m.sem, x * mul)
        else:
            eng.wait_ge(m.sem, x * mul if mul != 1 else x)

    def run(eng, body):
        for i in range(2):
            body(i, i)
        with eng.Fori(2, NTILE - 3, 2) as i:
            for j in range(2):
                body(i + j if j else i, j)
        for i in range(NTILE - 2, NTILE):
            body(i, i % 2)

    def loaded(eng, m, i, j, each=1):
        ge(eng, m[j], i + (2 - j), 8 * each)

    values = {}

    def chunk(eng, m, c, i):
        if isinstance(i, int):
            ge(eng, m[c % 3], 2 * i + c // 3 + 1 if i >= 0 else 0)
        else:
            key = (id(eng), id(i), c // 3)
            if key not in values:
                values[key] = (i, i * 2 + (c // 3 + 1))
            eng.wait_ge(m[c % 3].sem, values[key][1])

    def kr(c):
        return HR if c == 0 else P

    def transposes(pe, i, j):
        loaded(pe, xr_in, i, j)
        ge(pe, xlo, i)
        for k in range(KD):
            for s in range(FS):
                last = pe.transpose(XP[:, k * FT + s * P:k * FT + (s + 1) * P], XR[:, j, s, k * P:(k + 1) * P],
                                    ident[:, :])
        xT_ps.by(last)

    def pe_slot(pe, i, j):
        if isinstance(i, int) and i == 0:
            e_set.wait(pe, 2)
            transposes(pe, 0, 0)
        i1, im = i + 1, i - 1
        ge(pe, xlo, i1)
        loaded(pe, up_in, i, j)
        for c in range(NCH):
            at = GU[(NCH * j + c) % 4]
            if c >= 4:
                chunk(pe, h32, c - 4, i)
            else:
                chunk(pe, h32, c + 2, im)
            blocks = ((2 * NFULL, at[:, 0:FT]),) if c == 0 else ((c - 1, at[:, 0:FT]), (NFULL + c - 1, at[:, FT:2 * FT]))
            for b, to in blocks:
                for k in range(KD):
                    for n, (wp, xp) in enumerate(((0, 0), (0, 1), (1, 0))):
                        last = pe.matmul(to, UP[:, j, wp, k, b, :], XT[:, xp, k, :], start=(k == 0 and n == 0),
                                         stop=(k == KD - 1 and n == 2))
            gu[c % 3].by(last)
        if not (isinstance(i, int) and i == NTILE - 1):
            transposes(pe, i1, 1 - j)
        loaded(pe, dn_in, i, j)
        ge(pe, yo, i)
        for c in range(NCH):
            chunk(pe, hlo, c, i)
            dc, K = (c - 1) % NCH, kr(c) + (c == 0)
            for s in range(FS):
                for n, (hp, wp) in enumerate(((0, 0), (0, 1), (1, 0))):
                    last = pe.matmul(YP[s][:, 0:D], HT[0:K, hp, c, s * P:(s + 1) * P], DN[0:K, j, wp, dc, :],
                                     start=(c == 0 and n == 0), stop=(c == NCH - 1 and n == 2))
        y_ps.by(last)

    def act_slot(act, i, j):
        def high(c):
            chunk(act, h32, c, i)
            if c == 0:
                ge(act, y_ps, i)
            hhi[c % 3].by(act.activation(HT[0:kr(c), 0, c, :], H32[0:kr(c), c % 2, :], ACT.Copy))

        def xhigh(i, i1):
            ge(act, xT_ps, i1)
            xhi.by(act.activation(XT[:, 0, :, :], XP[:, :].rearrange("p (k t) -> p k t", k=KD), ACT.Copy))

        if isinstance(i, int) and i == 0:
            xhigh(0, 1)
        i1, im = i + 1, i - 1
        loaded(act, bt_in, i, j)
        for c in range(NCH):
            at = GU[(NCH * j + c) % 4]
            chunk(act, gu, c, i)
            if c >= 2:
                chunk(act, h32, c - 2, i)
            else:
                chunk(act, h32, c + 4, im)
            sil[c % 3].by(act.activation(SIL[0:kr(c), c % 2, :], at[0:kr(c), 0:FT], ACT.Silu, bias=BT[0:kr(c), j, c:c + 1]))
            if c == 0:
                ur.by(act.activation(UR[:, :], at[64:64 + HR, 0:FT], ACT.Copy))
            else:
                high(c - 1)
        high(NCH - 1)
        if not (isinstance(i, int) and i == NTILE - 1):
            xhigh(i1, i + 2)

    def dve_slot(dve, i, j):
        def low(c):
            chunk(dve, hhi, c, i)
            hlo[c % 3].by(dve.tensor_tensor(HT[0:kr(c), 1, c, :], H32[0:kr(c), c % 2, :], HT[0:kr(c), 0, c, :],
                                        ALU.subtract))

        def incoming(i, i1, j):
            ge(dve, xhi, i1)
            xlo.by(dve.tensor_tensor(XT[:, 1, :, :].rearrange("p k t -> p (k t)"), XP[:, :],
                                     XT[:, 0, :, :].rearrange("p k t -> p (k t)"), ALU.subtract))
            if isinstance(i, int):
                tf = table_f[:, i:i + 1]
            else:
                tf = table_f[:, bass.ds(i, 1)]
            loaded(dve, sent, i - 2 if isinstance(i, int) else i - 2, j, 2)
            ilo.by(dve.tensor_tensor(islo[:, :], XR[:, j, :, D + 3], tf.broadcast_to([P, FS]), ALU.is_equal))
            idone.by(dve.tensor_copy(idx[:, j, :], XR[:, j, :, D + 2]))
            ge(dve, ilo, i1)
            wl.by(dve.tensor_tensor(tl[:, :], islo[:, :], XR[:, j, :, D], ALU.mult))
            wh.by(dve.scalar_tensor_tensor(out=wt[:, j, :], in0=islo[:, :], scalar=-1.0, in1=XR[:, j, :, D + 1],
                                           op0=ALU.add, op1=ALU.mult))
            ge(dve, wl, i1)
            ge(dve, wh, i1)
            wdone.by(dve.tensor_tensor(wt[:, j, :], tl[:, :], wt[:, j, :], ALU.subtract))

        if isinstance(i, int) and i == 0:
            incoming(0, 1, 0)
            loaded(dve, bt_in, 0, 0)
        else:
            loaded(dve, bt_in, i, j)
        i1, im = i + 1, i - 1
        for c in range(NCH):
            at = GU[(NCH * j + c) % 4]
            lin = UR[:, :] if c == 0 else at[:, FT:2 * FT]
            if c:
                chunk(dve, sil, c, i)
            else:
                ge(dve, ur, i1)
            if c >= 2:
                chunk(dve, hlo, c - 2, i)
            else:
                chunk(dve, hlo, c + 4, im)
            h32[c % 3].by(dve.scalar_tensor_tensor(out=H32[0:kr(c), c % 2, :], in0=lin, scalar=BT[0:kr(c), j, NCH + c:NCH + c + 1],
                                               in1=SIL[0:kr(c), c % 2, :], op0=ALU.add, op1=ALU.mult))
            if c:
                low(c - 1)
        low(NCH - 1)
        if not (isinstance(i, int) and i == NTILE - 1):
            incoming(i1, i + 2, 1 - j)
        ge(dve, y_ps, i1)
        ge(dve, wdone, i1)
        loaded(dve, z_in, i, j, 2)
        for s in range(FS):
            last = dve.scalar_tensor_tensor(out=Z[:, j, s, :], in0=YP[s][:, 0:D], scalar=wt[:, j, s:s + 1],
                                            in1=Z[:, j, s, :], op0=ALU.mult, op1=ALU.add)
        yo.by(last)

    def pool_slot(pool, i, j):
        i1 = i + 1
        ge(pool, idone, i1)
        loaded(pool, sent, i - 1, 1 - j, 2)
        carry(pool, spare, carried, i * 2)
        for s in range(FS):
            z_in[j].by(pool.indirect_dma_start(Z[:, j, s, :], None, out,
                                               bass.IndirectOffsetOnAxis(idx[:, j, s:s + 1], 0),
                                               bounds_check=T - 1, oob_is_err=False))
        ge(pool, yo, i1)
        carry(pool, spare, carried, i * 2 + 1)
        for s in range(FS):
            sent[j].by(pool.indirect_dma_start(out, bass.IndirectOffsetOnAxis(idx[:, j, s:s + 1], 0),
                                               Z[:, j, s, :], None, bounds_check=T - 1, oob_is_err=False))

    def sp_load(sp, i, j, waits):
        def at(k):
            col = slice(i, i + 1) if isinstance(i, int) else bass.ds(i, 1)
            return table_i[0:1, k, col]

        row = sp.value_load(at(0), min_val=0, max_val=SPARE)
        e = sp.value_load(at(1), min_val=0, max_val=E - 1)
        new = sp.value_load(at(2), min_val=0, max_val=1)
        if waits:
            n = i - 1
            ge(sp, xT_ps, n)
            ge(sp, wdone, n)
        xr_in[j].by(sp.dma_start(XR[:, j, :, :], xs_dram[bass.ds(row, FT), :].rearrange("(s p) w -> p s w", p=P)))
        if waits:
            chunk(sp, gu, NCH - 1, i - 2)
        up_in[j].by(sp.dma_start(UP[:, j, :, :, :, :].rearrange("p a k b n -> p (a k b n)"),
                                 up_dram[bass.ds(e, 1)].rearrange("o p w -> p (o w)"), cond=new))
        if waits:
            chunk(sp, h32, NCH - 1, i - 2)
        bt_in[j].by(sp.dma_start(BT[:, j, :], bias[:, bass.ds(e, 1), :].rearrange("p o c -> p (o c)")))
        if waits:
            ge(sp, y_ps, n)
        dn_in[j].by(sp.dma_start(DN[:, j, :, :, :].rearrange("p a c d -> p (a c d)"),
                                 dn_dram[bass.ds(e, 1)].rearrange("o p w -> p (o w)"), cond=new))

    with nc.Block() as block:
        @block.sync
        def _(sp):
            sp_load(sp, 0, 0, False)
            sp_load(sp, 1, 1, False)
            with sp.Fori(2, NTILE - 1, 2) as i:
                for j in range(2):
                    sp_load(sp, i + j if j else i, j, True)

        @block.tensor
        def _(pe):
            run(pe, lambda i, j: pe_slot(pe, i, j))

        @block.scalar
        def _(act):
            run(act, lambda i, j: act_slot(act, i, j))

        @block.vector
        def _(dve):
            e_set.by(dve.memset(HT[32:64, 0, 0, :], 1.0))
            e_set.by(dve.memset(HT[32:64, 1, 0, :], 0.0))
            dve.memset(Z[:, :, :, :], 0.0)
            e_set.wait(dve, 2)
            run(dve, lambda i, j: dve_slot(dve, i, j))

        @block.gpsimd
        def _(pool):
            spared.by(pool.memset(spare[:, :], 0.0))
            spared.wait(pool, 1)
            run(pool, lambda i, j: pool_slot(pool, i, j))
            for j in range(2):
                loaded(pool, sent, NTILE - 2 + j, j, 2)


def build(nc, io, out):
    with ExitStack() as ctx:
        def made(name, step=1):
            return Made(ctx.enter_context(nc.semaphore(name)), step)

        def dram(name, shape, dt=F32):
            return nc.dram_tensor(name, shape, dt).ap()

        def keep(name, shape, dt=F32):
            return ctx.enter_context(nc.sbuf_tensor(name, shape, dt))

        ps = {k: ctx.enter_context(nc.psum_tensor(k, [P, w], F32)) for k, w in
              (("Spair", 1024), ("Tpair", 1024), ("F0", 512), ("F1", 512), ("G", 512), ("O", 512))}
        xs_dram = dram("xs_dram", [E * CAP + FT, RW])
        up_dram = dram("up_dram", [E, P, UW], BF16)
        dn_dram = dram("dn_dram", [E, P, DW], BF16)
        ident = keep("ident", [P, P])
        table_i = keep("table_i", [P, 3, NTILE], I32)
        table_f = keep("table_f", [P, NTILE])
        bias = keep("bias", [P, E, 2 * NCH])
        with ExitStack() as phase:
            sb = lambda name, shape, dt=F32: phase.enter_context(nc.sbuf_tensor(name, shape, dt))
            setup_and_attention(nc, io, sb, made, dram, ps, ident, out,
                                lambda pool: split_weights(nc, io, sb, made, pool, up_dram, dn_dram))
        with ExitStack() as phase:
            sb = lambda name, shape, dt=F32: phase.enter_context(nc.sbuf_tensor(name, shape, dt))
            load_biases(nc, io, sb, made, ps, ident, bias)
            dispatch(nc, io, sb, made, dram, ps, ident, out, xs_dram, table_i, table_f)
        with ExitStack() as phase:
            sb = lambda name, shape, dt=F32: phase.enter_context(nc.sbuf_tensor(name, shape, dt))
            experts(nc, io, sb, made, ps, ident, bias, xs_dram, up_dram, dn_dram, table_i, table_f, out)


_INS = ["x", "itok_B_0_2", "itok_B_0_6", "L0_cond_W1", "L0_cond_b1",
        "L0_cond_v", "L0_attn_Wq", "L0_attn_Wk", "L0_attn_Wv", "L0_attn_Wo",
        "L0_attn_W_down_kv", "L0_attn_W_up_k", "L0_attn_W_up_v", "L0_cond2_down_w", "L0_cond2_down_b",
        "L0_cond2_up_w", "L0_cond2_up_b", "L0_cond2_ln_g", "L0_cond2_ln_b", "L0_ffn_centroid",
        "L0_ffn_Wg", "L0_ffn_bg", "L0_ffn_W1", "L0_ffn_b1", "L0_ffn_W2",
        "L0_ffn_b2"]
_OUTS = [((64, 64, 256), "float32")]


def kernel(**inputs):
    import numpy as _np
    import concourse.bacc as _bacc
    from concourse import mybir as _mybir
    from concourse.bass_utils import run_bass_kernel_spmd as _run

    nc = _bacc.Bacc("TRN2", target_bir_lowering=False, num_devices=1)
    arrays, io = {}, {}
    for name in _INS:
        a = _np.ascontiguousarray(inputs[name])
        arrays[f"in_{name}_dram"] = a
        io[name] = nc.dram_tensor(f"in_{name}_dram", a.shape, _mybir.dt.from_np(a.dtype), kind="ExternalInput").ap()
    outs = [nc.dram_tensor(f"out_{i}_dram", shape, _mybir.dt.from_np(_np.dtype(dtype)), kind="ExternalOutput").ap()
            for i, (shape, dtype) in enumerate(_OUTS)]
    build(nc, io, outs[0].rearrange("b s d -> (b s) d"))
    r = _run(nc, [arrays], core_ids=[0])
    return r.results[0]["out_0_dram"]
```

```python
import numpy as np
from contextlib import ExitStack

import concourse.bass as bass
from concourse import mybir

F32 = mybir.dt.float32
BF16 = mybir.dt.bfloat16
I32 = mybir.dt.int32
ALU = mybir.AluOpType
ACT = mybir.ActivationFunctionType
AX = mybir.AxisListType.X

P = 128
B, S, D = 64, 64, 256
T = B * S
KD = D // P
A = 64
L = 64
NH, DH = 16, 16
HP = NH // 2
NPAIR = T // P
UT = 2 * P
NUNIT = T // UT
VW = 2 * DH + 2
QSCALE = 1.0 / 16.0
CLAMP = 10000.0
DECAY = -0.01 * 0.01
FAR = 1.0e30


class Made:

    def __init__(self, sem, step=1):
        self.sem, self.step = sem, step

    def by(self, instruction):
        return instruction.then_inc(self.sem, self.step)

    def wait(self, eng, value):
        if isinstance(value, int) and value <= 0:
            return
        eng.wait_ge(self.sem, value)


def carry(pool, spare, carried, n):
    carried.wait(pool, n)
    carried.by(pool.tensor_tensor(spare[:, 1:2], spare[:, 0:1], spare[:, 0:1], ALU.add))


def setup_and_attention(nc, io, sb, made, dram, ps, ident, x1_dram, beside):
    F0, F1, G, O, Spair, Tpair = (ps[k] for k in ("F0", "F1", "G", "O", "Spair", "Tpair"))
    qk_dram = dram("qk_dram", [2, 4, D, UT], BF16)

    w1 = sb("w1", [P, KD, A])
    b1 = sb("b1", [A, 1])
    v = sb("v", [A, 1])
    vrep = sb("vrep", [A, S])
    wq = sb("wq", [P, KD, D])
    wk = sb("wk", [P, KD, D])
    wv = sb("wv", [P, KD, D])
    wkvT = sb("wkvT", [P, KD, D])
    wdown = sb("wdown", [P, KD, L])
    wkvd = sb("wkvd", [P, KD, L])
    wuk = sb("wuk", [L, D])
    wuv = sb("wuv", [L, D])
    wo = sb("wo", [P, KD, D])
    types_i = sb("types_i", [P, B], I32)
    types = sb("types", [P, NPAIR])
    is_t = sb("is_t", [P, 3, NPAIR])
    diff = sb("diff", [P, S])
    shut = sb("shut", [P, 3, S])
    cap = sb("cap", [P, NPAIR, S])
    capt = sb("capt", [P, 8, S])
    capt_n = sb("capt_n", [P, NPAIR])
    pos = sb("pos_in_batch", [P, 1])
    opens = sb("opens", [P, 1])
    count = sb("count", [P, NPAIR])
    decay = sb("decay", [P, S])
    XU = sb("XU", [P, 2, 2, D])
    XT = sb("XT", [P, KD, UT])
    AT = sb("AT", [A, UT])
    SM = sb("SM", [P, 2, S])
    smx = sb("smx", [P, 2])
    ssum = sb("ssum", [P, 2])
    PB = sb("PB", [P, 2, P])
    PT = sb("PT", [P, 2, P])
    PO = sb("PO", [P, KD, UT])
    QK = sb("QK", [P, 4, KD, UT], BF16)
    LT = sb("LT", [L, 2, UT])
    QS = sb("QS", [3 * 32, 2, HP, UT], BF16)
    KS = sb("KS", [3 * 32, 2, HP, 2, UT], BF16)
    VB = sb("VB", [P, 2, 2, 2, HP, VW])
    W = sb("W", [P, 2, NH, S])
    rowmax = sb("rowmax", [P, 2, NH])
    PX = sb("PX", [P, 2, HP, P])
    rec = sb("rec", [P, HP, 2])
    ON = sb("ON", [P, HP, 2, DH])
    OT = sb("OT", [P, KD, P])
    XR = sb("XR", [P, 2, D])

    s_w = made("s_w", 16)
    s_c = made("s_c")
    s_v = made("s_v")
    s_a = made("s_a")
    s_p = made("s_p")
    s_m = made("s_m")
    u_x = made("u_x", 16)

    loads = [
        (w1[:, :, :], io["L0_cond_W1"].rearrange("(k p) a -> p k a", p=P)),
        (b1[:, :], io["L0_cond_b1"].rearrange("(a o) -> a o", o=1)),
        (v[:, :], io["L0_cond_v"].rearrange("(a o) -> a o", o=1)),
        (types_i[:, :], io["itok_B_0_2"].rearrange("(o b) -> o b", o=1).broadcast_to([P, B])),
        (wk[:, :, :], io["L0_attn_Wk"].rearrange("(k p) n -> p k n", p=P)),
        (wv[:, :, :], io["L0_attn_Wv"].rearrange("(k p) n -> p k n", p=P)),
        (wdown[:, :, :], io["L0_attn_W_down_kv"].rearrange("(k p) n -> p k n", p=P)),
        (wq[:, :, :], io["L0_attn_Wq"].rearrange("(k p) n -> p k n", p=P)),
        (wuk[:, :], io["L0_attn_W_up_k"]),
        (wuv[:, :], io["L0_attn_W_up_v"]),
        (wo[:, :, :], io["L0_attn_Wo"].rearrange("(k p) n -> p k n", p=P)),
    ]

    x_rows = io["x"].rearrange("b s d -> (b s) d")

    def load_x(sp, row, up):
        u_x.by(sp.dma_start(XU[:, up, :, :], x_rows[bass.ds(row, UT), :].rearrange("(s p) d -> p s d", p=P)))

    caps_made = [0]

    def build_caps(dve, n0, n1):
        wide = [P, n1 - n0, S]
        at, also = cap[:, n0:n1, :], capt[:, 0:n1 - n0, :]

        def step(instruction):
            s_m.by(instruction)
            caps_made[0] += 1
            s_m.wait(dve, caps_made[0])

        for k in range(3):
            step(dve.tensor_tensor(also if k else at, is_t[:, k, n0:n1].unsqueeze(2).broadcast_to(wide),
                                   shut[:, k, :].unsqueeze(1).broadcast_to(wide), ALU.mult))
            if k:
                step(dve.tensor_tensor(at, at, also, ALU.add))
        step(dve.tensor_scalar(at, at, -2.0 * FAR, FAR, ALU.mult, ALU.add))

    CAPS = {-2: (4, 10), 0: (10, 17), 1: (17, 24), 2: (24, NPAIR)}

    with nc.Block() as block:
        @block.sync
        def _(sp):
            load_x(sp, 0, 0)
            for out, in_ in loads:
                s_w.by(sp.dma_start(out, in_))
            s_w.wait(sp, 16 * len(loads))

        @block.gpsimd
        def _(pool):
            n = [0]

            def step(instruction):
                s_c.by(instruction)
                n[0] += 1
                s_c.wait(pool, n[0])

            step(pool.memset(ident[:, :], 0.0))
            step(pool.affine_select(out=ident[:, :], in_=ident[:, :], compare_op=ALU.not_equal, fill=1.0,
                                    base=0, pattern=[[-1, P]], channel_multiplier=1))
            for h in range(2):
                step(pool.iota(diff[S * h:S * h + S, :], pattern=[[1, S]], base=0, channel_multiplier=-1,
                               allow_small_or_imprecise_dtypes=True))
                step(pool.iota(pos[S * h:S * h + S, :], pattern=[[0, 1]], base=0, channel_multiplier=1,
                               allow_small_or_imprecise_dtypes=True))
            step(pool.memset(PB[:, :, :], 0.0))
            step(pool.memset(KS[:, :, :, :, :], 0.0))
            step(pool.memset(VB[:, :, :, :, :, :], 0.0))
            for half in range(2):
                col = 2 * DH + half
                step(pool.memset(VB[S * half:S * half + S, :, :, :, :, :].rearrange(
                    "p u s b h c -> p (u s b h) c")[:, :, col], 1.0))

        @block.vector
        def _(dve):
            n = [0]

            def step(instruction):
                s_v.by(instruction)
                n[0] += 1
                s_v.wait(dve, n[0])

            s_w.wait(dve, 16 * len(loads))
            s_c.wait(dve, 6)
            step(dve.memset(vrep[:, :], 1.0))
            step(dve.tensor_scalar(vrep[:, :], vrep[:, :], v[:, 0:1], None, ALU.mult))
            step(dve.tensor_tensor(wk[:, :, :], wk[:, :, :], wv[:, :, :], ALU.add))
            for h in range(2):
                rows = slice(S * h, S * h + S)
                step(dve.tensor_copy(types[rows, :], types_i[rows, :].rearrange("p (n b) -> p n b", b=2)[:, :, h]))
            step(dve.tensor_scalar(is_t[:, 0, :], types[:, :], 0.0, None, ALU.is_equal))
            step(dve.tensor_scalar(is_t[:, 1, :], types[:, :], 1.0, None, ALU.is_equal))
            step(dve.tensor_tensor(is_t[:, 2, :], is_t[:, 0, :], is_t[:, 1, :], ALU.add))
            step(dve.tensor_scalar(is_t[:, 2, :], is_t[:, 2, :], -1.0, 1.0, ALU.mult, ALU.add))
            for k, op in enumerate((ALU.is_gt, ALU.is_lt, ALU.is_equal)):
                step(dve.tensor_scalar(shut[:, k, :], diff[:, :], 0.0, None, op))
            for k, (scale, more) in enumerate(((1.0, 1.0), (-1.0, float(S)), (0.0, float(S - 1)))):
                step(dve.tensor_scalar(opens[:, :], pos[:, :], scale, more, ALU.mult, ALU.add))
                to = count if k == 0 else capt_n
                step(dve.tensor_scalar(to[:, :], is_t[:, k, :], opens[:, 0:1], None, ALU.mult))
                if k:
                    step(dve.tensor_tensor(count[:, :], count[:, :], capt_n[:, :], ALU.add))
            build_caps(dve, 0, 4)

        @block.scalar
        def _(act):
            s_c.wait(act, 6)
            s_a.by(act.activation(decay[:, :], diff[:, :], ACT.Abs))
            s_a.wait(act, 1)
            s_a.by(act.activation(decay[:, :], decay[:, :], ACT.Exp, scale=DECAY))
            for k in range(KD):
                s_p.wait(act, k + 1)
                s_a.by(act.activation(wkvT[:, k, :], F0[:, 0:D], ACT.Copy))
            s_p.wait(act, KD + 1)
            s_a.by(act.activation(wkvd[:, :, :], F1[:, 0:KD * L].rearrange("p (k l) -> p k l", k=KD), ACT.Copy))

        @block.tensor
        def _(pe):
            s_c.wait(pe, 2)
            s_v.wait(pe, 3)
            for k in range(KD):
                if k:
                    s_a.wait(pe, 2 + k)
                for m in range(KD):
                    last = pe.transpose(F0[:, m * P:(m + 1) * P], wk[:, m, k * P:(k + 1) * P], ident[:, :])
                s_p.by(last)
            s_a.wait(pe, 2 + KD)
            for m in range(KD):
                for k in range(KD):
                    last = pe.matmul(F1[:, m * L:(m + 1) * L], wkvT[:, k, m * P:(m + 1) * P], wdown[:, k, :],
                                     start=(k == 0), stop=(k == KD - 1))
            s_p.by(last)

    names_u = ["xt_ps", "xt", "at_ps", "at", "sc_ps", "sc_a", "sc_b", "sc_c", "sc_e", "sc_f", "sc_g", "sc_h", "pb",
               "pt_ps", "pt", "po_ps", "po", "q_ps", "qhi", "qlo", "lt_ps", "lt", "k_ps", "khi", "klo",
               "v_ps", "vb0", "vb1"]
    U = {k: made("u_" + k, 2) for k in names_u}
    names_p = ["s_ps", "clip", "dec", "max", "sub", "t_ps0", "t_ps1", "px0", "px1", "o_ps", "rec", "on",
               "ot_ps", "ot", "g_ps", "x1"]
    R = {k: made("p_" + k) for k in names_p}
    u_qk_out = made("u_qk_out", 16)
    u_qs = made("u_qs", 16)
    p_xr = made("p_xr", 16)
    p_out = made("p_out", 16)

    LS, LT_, LV, LG = 3, 4, 5, 6

    def has_pair(n):
        return not isinstance(n, int) or 0 <= n < NPAIR

    def run(eng, body):
        first, last = 8, 28
        for t in range(-3, first):
            body(t, t % 4)
        with eng.Fori(first, last - 3, 4) as t:
            cache = {}
            for j in range(4):
                body(Slot(t, cache, eng) + j, j)
        for t in range(last, NPAIR + LG):
            body(t, t % 4)

    class Slot:

        def __init__(self, t, cache, eng, c=0):
            self.t, self.cache, self.eng, self.c = t, cache, eng, c

        def __add__(self, c):
            return Slot(self.t, self.cache, self.eng, self.c + c)

        def __sub__(self, c):
            return self + (-c)

        def reg(self):
            return self.t + self.c

    def val(x, mul=1):
        if isinstance(x, int):
            return x * mul
        return x.reg() * mul if mul != 1 else x.reg()

    def ge(eng, m, x, mul=1):
        if isinstance(x, int):
            if x > 0:
                eng.wait_ge(m.sem, x * mul)
            return
        eng.wait_ge(m.sem, val(x, mul))

    def on_unit(t, j, start):
        if (j - start) % 2:
            return None
        u2 = t - start
        if isinstance(u2, int) and not 0 <= u2 < 2 * NUNIT:
            return None
        return u2, ((j - start) // 2) % 2

    def most(x):
        return min(x, 2 * NUNIT) if isinstance(x, int) else x

    def pe_slot(pe, t, j):
        def scores(n):
            up, h = ((j - LS) % 4) // 2, (j - LS) % 2
            if h == 0:
                ge(pe, u_qs, n + 2, 72)
            ge(pe, R["clip"], n)
            for b in range(2):
                c0 = h * P + b * S
                for hp in range(HP):
                    last = pe.matmul(Spair[S * b:S * b + S, hp * P:(hp + 1) * P], QS[:, up, hp, c0:c0 + S],
                                     KS[:, up, hp, :, c0:c0 + S], start=True, stop=True)
            R["s_ps"].by(last)

        def turn_heads_out(n):
            ge(pe, R["on"], n + 1)
            ge(pe, R["x1"], n)
            for m in range(KD):
                last = pe.transpose(G[:, m * P:(m + 1) * P],
                                    ON[:, :, :, :].rearrange("p h e d -> p (h e d)")[:, m * P:(m + 1) * P], ident[:, :])
            R["ot_ps"].by(last)

        def project_out(n):
            ge(pe, R["ot"], n + 1)
            for m in range(KD):
                last = pe.matmul(G[:, D:2 * D], OT[:, m, :], wo[:, m, :], start=(m == 0), stop=(m == KD - 1))
            R["g_ps"].by(last)

        def turn_weights(n):
            w = W[:, (j - LT_) % 2, :, :].rearrange("p h s -> p (h s)")
            ge(pe, R["sub"], n + 1)
            for half in range(2):
                ge(pe, R[f"px{half}"], n)
                for hp in range(4 * half, 4 * half + 4):
                    last = pe.transpose(Tpair[:, hp * P:(hp + 1) * P], w[:, hp * P:(hp + 1) * P], ident[:, :])
                R[f"t_ps{half}"].by(last)

        def values(n):
            up, h = ((j - LV) % 4) // 2, (j - LV) % 2
            ge(pe, R["px0"], n + 1)
            ge(pe, R["px1"], n + 1)
            if h == 0:
                ge(pe, U["vb0"], n + 2)
                ge(pe, U["vb1"], n + 2)
            ge(pe, R["on"], n)
            for b in range(2):
                for hp in range(HP):
                    last = pe.matmul(O[S * b:S * b + S, hp * VW:(hp + 1) * VW], PX[:, h, hp, S * b:S * b + S],
                                     VB[:, up, h, b, hp, :], start=True, stop=True)
            R["o_ps"].by(last)

        def queries(u2):
            ge(pe, U["po"], u2 + 2)
            ge(pe, U["xt"], most(u2 + 4))
            for m in range(KD):
                for k in range(KD):
                    last = pe.matmul(F0[:, m * UT:(m + 1) * UT], wq[:, k, m * P:(m + 1) * P], PO[:, k, :],
                                     start=(k == 0), stop=(k == KD - 1))
            U["q_ps"].by(last)

        def latent(u2):
            ge(pe, U["sc_a"], most(u2 + 4))
            for k in range(KD):
                last = pe.matmul(F1[0:L, 0:UT], wkvd[:, k, :], PO[:, k, :], start=(k == 0), stop=(k == KD - 1))
            U["lt_ps"].by(last)

        def keys(u2, up):
            ge(pe, U["lt"], u2 + 2)
            ge(pe, U["qlo"], u2 + 2)
            for m in range(KD):
                last = pe.matmul(F0[:, m * UT:(m + 1) * UT], wuk[:, m * P:(m + 1) * P], LT[:, up, :],
                                 start=True, stop=True)
            U["k_ps"].by(last)

        def project_values(u2, up):
            ge(pe, U["lt"], most(u2 + 4))
            for s in range(2):
                last = pe.matmul(F1[:, s * D:(s + 1) * D], LT[:, up, s * P:(s + 1) * P], wuv[:, :],
                                 start=True, stop=True)
            U["v_ps"].by(last)

        def turn_pooling(u2):
            ge(pe, U["pb"], u2 + 2)
            ge(pe, U["klo"], u2)
            for s in range(2):
                last = pe.transpose(F0[:, s * P:(s + 1) * P], PB[:, s, :], ident[:, :])
            U["pt_ps"].by(last)

        def pool(u2, up):
            ge(pe, U["pt"], u2 + 2)
            ge(pe, U["vb1"], u2 - 2)
            for k in range(KD):
                for s in range(2):
                    last = pe.matmul(F1[:, k * UT + s * P:k * UT + (s + 1) * P], XU[:, up, s, k * P:(k + 1) * P],
                                     PT[:, s, :], start=True, stop=True)
            U["po_ps"].by(last)

        def turn_x(u2, up):
            ge(pe, U["pt"], u2)
            ge(pe, u_x, u2 + 2, 8)
            for k in range(KD):
                for s in range(2):
                    last = pe.transpose(F0[:, k * UT + s * P:k * UT + (s + 1) * P], XU[:, up, s, k * P:(k + 1) * P],
                                        ident[:, :])
            U["xt_ps"].by(last)

        def inner_layer(u2):
            ge(pe, U["xt"], u2 + 2)
            ge(pe, U["po"], u2)
            for k in range(KD):
                last = pe.matmul(F1[0:A, 0:UT], w1[:, k, :], XT[:, k, :], start=(k == 0), stop=(k == KD - 1))
            U["at_ps"].by(last)

        def pooling_scores():
            for b in range(2):
                last = pe.matmul(F1[S * b:S * b + S, UT:UT + P].rearrange("p (s l) -> p s l", s=2), vrep[:, :],
                                 AT[:, :].rearrange("a (s b l) -> a s b l", s=2, b=2)[:, :, b, :],
                                 start=True, stop=True)
            U["sc_ps"].by(last)

        n_s, n_t, n_v, n_g = t - LS, t - LT_, t - LV, t - LG
        f, f1, fs, fx, f3 = (on_unit(t, j, start) for start in (0, -1, -2, -3, 3))
        if fs:
            ge(pe, U["at"], fs[0] + 2)
        if has_pair(n_s):
            scores(n_s)
        if fs:
            pooling_scores()
        if f:
            queries(f[0])
            latent(f[0])
        if f3:
            project_values(*f3)
        if f1:
            turn_pooling(f1[0])
        if has_pair(n_t):
            turn_weights(n_t)
        if has_pair(n_g):
            turn_heads_out(n_g)
        if fx:
            turn_x(*fx)
        if f:
            keys(*f)
        if f1:
            pool(*f1)
        if has_pair(n_g):
            project_out(n_g)
        if fx:
            inner_layer(fx[0])
        if has_pair(n_v):
            values(n_v)

    def act_slot(act, t, j):
        def halves(x):
            return x.rearrange("p (k t) -> p k t", k=KD)

        f, f1, fs, fx, f3 = (on_unit(t, j, start) for start in (0, -1, -2, -3, 3))
        if f1:
            ge(act, U["pt_ps"], f1[0] + 2)
            U["pt"].by(act.activation(PT[:, :, :], F0[:, 0:UT].rearrange("p (s t) -> p s t", s=2), ACT.Copy))
        if f:
            u2, up = f
            ge(act, U["q_ps"], u2 + 2)
            ge(act, u_qk_out, u2, 32)
            U["qhi"].by(act.activation(QK[:, 0, :, :], halves(F0[:, :]), ACT.Copy, scale=QSCALE))
            ge(act, U["lt_ps"], u2 + 2)
            ge(act, U["v_ps"], u2 - 2)
            U["lt"].by(act.activation(LT[:, up, :], F1[0:L, 0:UT], ACT.Copy))
        if f3:
            u2, up = f3
            ge(act, U["v_ps"], u2 + 2)
            ge(act, R["o_ps"], u2 - 2)
            for e in range(2):
                for b in range(2):
                    last = act.activation(
                        VB[S * e:S * e + S, up, :, b, :, e * DH:(e + 1) * DH],
                        F1[S * b:S * b + S, :].rearrange("p (s h e d) -> p s h e d", s=2, h=HP, e=2)[:, :, :, e, :],
                        ACT.Copy)
                U[f"vb{e}"].by(last)
        n = t - LT_
        if has_pair(n):
            for half in range(2):
                ge(act, R[f"t_ps{half}"], n + 1)
                ge(act, R["o_ps"], n - 1)
                R[f"px{half}"].by(act.activation(
                    PX[:, (j - LT_) % 2, 4 * half:4 * half + 4, :],
                    Tpair[:, 512 * half:512 * half + 512].rearrange("p (h t) -> p h t", h=4), ACT.Exp))
        n = t - LG
        if has_pair(n):
            ge(act, R["ot_ps"], n + 1)
            R["ot"].by(act.activation(OT[:, :, :], halves(G[:, 0:KD * P]), ACT.Copy))
        if fs:
            ge(act, U["sc_c"], fs[0] + 2)
            U["sc_e"].by(act.activation(SM[:, :, :], SM[:, :, :], ACT.Exp))
        if f:
            ge(act, U["k_ps"], f[0] + 2)
            U["khi"].by(act.activation(QK[:, 2, :, :], halves(F0[:, :]), ACT.Copy))
        if fx:
            ge(act, U["xt_ps"], fx[0] + 2)
            U["xt"].by(act.activation(XT[:, :, :], halves(F0[:, :]), ACT.Copy))
        if f1:
            ge(act, U["po_ps"], f1[0] + 2)
            U["po"].by(act.activation(PO[:, :, :], halves(F1[:, :]), ACT.Copy))
        if fx:
            ge(act, U["at_ps"], fx[0] + 2)
            U["at"].by(act.activation(AT[:, :], F1[0:A, 0:UT], ACT.Tanh, bias=b1[:, 0:1]))
        if isinstance(t, int) and 4 <= t < 8:
            beside.act_loads(act, t - 4, 4)

    def dve_slot(dve, t, j):
        f, fs = on_unit(t, j, 0), on_unit(t, j, -2)
        n_g, n_s = t - LG, t - LS
        o = O[:, 0:HP * VW].rearrange("p (h c) -> p h c", h=HP)
        par = (j - LS) % 2
        w = W[:, par, :, :]
        flat = w.rearrange("p h s -> p (h s)")
        if has_pair(n_g):
            ge(dve, R["o_ps"], n_g + 1)
            R["rec"].by(dve.reciprocal(rec[:, :, :], o[:, :, 2 * DH:VW]))
            ge(dve, R["rec"], n_g + 1)
            ge(dve, R["ot_ps"], n_g)
            R["on"].by(dve.tensor_tensor(ON[:, :, :, :], o[:, :, 0:2 * DH].rearrange("p h (e d) -> p h e d", e=2),
                                         rec[:, :, :].unsqueeze(3).broadcast_to([P, HP, 2, DH]), ALU.mult))
        if has_pair(n_s):
            ge(dve, R["s_ps"], n_s + 1)
            ge(dve, R["t_ps1"], n_s - 1)
            R["clip"].by(dve.tensor_scalar(flat, Spair[:, :], -CLAMP, CLAMP, ALU.max, ALU.min))
        if fs:
            u2 = fs[0]
            ge(dve, U["sc_ps"], u2 + 2)
            caps = cap[:, u2:u2 + 2, :] if isinstance(u2, int) else cap[:, bass.ds(u2.reg(), 2), :]
            U["sc_a"].by(dve.tensor_tensor(SM[:, :, :], F1[:, UT:UT + P].rearrange("p (s l) -> p s l", s=2), caps,
                                           ALU.min))
        if has_pair(n_s):
            ge(dve, R["clip"], n_s + 1)
            R["dec"].by(dve.tensor_tensor(w, w, decay[:, :].unsqueeze(1).broadcast_to([P, NH, S]), ALU.mult))
        if fs:
            ge(dve, U["sc_a"], u2 + 2)
            U["sc_b"].by(dve.tensor_reduce(smx[:, :], SM[:, :, :], AX, ALU.max))
        if f:
            ge(dve, U["qhi"], f[0] + 2)
            U["qlo"].by(dve.scalar_tensor_tensor(
                out=QK[:, 1, :, :].rearrange("p k t -> p (k t)"), in0=F0[:, :], scalar=QSCALE,
                in1=QK[:, 0, :, :].rearrange("p k t -> p (k t)"), op0=ALU.mult, op1=ALU.subtract))
        if fs:
            ge(dve, U["sc_b"], u2 + 2)
            U["sc_c"].by(dve.tensor_tensor(SM[:, :, :], SM[:, :, :], smx[:, :].unsqueeze(2).broadcast_to([P, 2, S]),
                                           ALU.subtract))
        if has_pair(n_s):
            ge(dve, R["dec"], n_s + 1)
            R["max"].by(dve.tensor_reduce(rowmax[:, par, :], w, AX, ALU.max))
        if fs:
            ge(dve, U["sc_e"], u2 + 2)
            U["sc_f"].by(dve.tensor_reduce(ssum[:, :], SM[:, :, :], AX, ALU.add))
        if has_pair(n_s):
            ge(dve, R["max"], n_s + 1)
            R["sub"].by(dve.tensor_tensor(w, w, rowmax[:, par, :].unsqueeze(2).broadcast_to([P, NH, S]),
                                          ALU.subtract))
        if fs:
            cnts = count[:, u2:u2 + 2] if isinstance(u2, int) else count[:, bass.ds(u2.reg(), 2)]
            ge(dve, U["sc_f"], u2 + 2)
            U["sc_g"].by(dve.tensor_tensor(ssum[:, :], ssum[:, :], cnts, ALU.mult))
        if has_pair(n_g):
            ge(dve, R["g_ps"], n_g + 1)
            ge(dve, p_xr, n_g + 1, 16)
            xr = XR[:, (j - LG) % 2, :]
            R["x1"].by(dve.tensor_tensor(xr, xr, G[:, D:2 * D], ALU.add))
        if fs:
            ge(dve, U["sc_g"], u2 + 2)
            U["sc_h"].by(dve.reciprocal(ssum[:, :], ssum[:, :]))
        if f:
            ge(dve, U["khi"], f[0] + 2)
            U["klo"].by(dve.tensor_tensor(QK[:, 3, :, :].rearrange("p k t -> p (k t)"), F0[:, :],
                                          QK[:, 2, :, :].rearrange("p k t -> p (k t)"), ALU.subtract))
        if fs:
            ge(dve, U["sc_h"], u2 + 2)
            ge(dve, U["pt_ps"], u2)
            for b in range(2):
                rows = slice(S * b, S * b + S)
                last = dve.tensor_tensor(PB[rows, :, S * b:S * b + S], SM[rows, :, :],
                                         ssum[rows, :].unsqueeze(2).broadcast_to([S, 2, S]), ALU.mult)
            U["pb"].by(last)
        if isinstance(t, int) and t in CAPS:
            build_caps(dve, *CAPS[t])
        if isinstance(t, int) and t >= NPAIR + 3:
            beside.dve_program(dve, t - NPAIR - 3)

    def sp_slot(sp, t, j):
        n = t - LV
        if has_pair(n):
            ge(sp, p_xr, n, 16)
            ge(sp, p_out, n - 1, 16)
            p_xr.by(sp.dma_start(XR[:, (j - LV) % 2, :], x_rows[bass.ds(val(n, P), P), :]))
        f = on_unit(t, j, -4)
        if f:
            u2, up = f
            ge(sp, U["po_ps"], u2 - 2)
            ge(sp, u_x, u2, 8)
            load_x(sp, val(u2, P), up)
        f = on_unit(t, j, 0)

        def parts_out(parts):
            for i, k in parts:
                ge(sp, U[k], f[0] + 2)
                u_qk_out.by(sp.dma_start(qk_dram[f[1], i].rearrange("(k p) t -> p k t", p=P), QK[:, i, :, :]))

        if f:
            ge(sp, u_qs, f[0] - 2, 72)
            parts_out(((0, "qhi"), (1, "qlo")))
        f1 = on_unit(t, j, 1)
        if f1:
            u2, up = f1
            ge(sp, u_qk_out, u2 + 2, 32)
            ge(sp, R["s_ps"], u2 - 2)
            for part, (qi, ki) in enumerate(((0, 2), (0, 3), (1, 2))):
                rows = slice(32 * part, 32 * part + 32)
                u_qs.by(sp.dma_start(QS[rows, up, :, :], qk_dram[up, qi].rearrange("(h p) t -> p h t", p=32)))
                for e in range(2):
                    r0 = 32 * part + DH * e
                    u_qs.by(sp.dma_start(KS[r0:r0 + DH, up, :, e, :], qk_dram[up, ki].rearrange(
                        "(h e p) t -> e p h t", e=2, p=DH)[e]))
        n = t - LG
        if has_pair(n):
            ge(sp, R["x1"], n + 1)
            p_out.by(sp.dma_start(x1_dram[bass.ds(val(n, P), P), :], XR[:, (j - LG) % 2, :]))
        if f:
            parts_out(((2, "khi"), (3, "klo")))
        if isinstance(t, int) and t >= NPAIR - 2:
            beside.sp_loads(sp, t - NPAIR + 2)

    with nc.Block() as block:
        @block.tensor
        def _(pe):
            run(pe, lambda t, j: pe_slot(pe, t, j))
            beside.pe_end(pe)

        @block.scalar
        def _(act):
            run(act, lambda t, j: act_slot(act, t, j))
            beside.act_end(act)

        @block.vector
        def _(dve):
            run(dve, lambda t, j: dve_slot(dve, t, j))
            beside.dve_end(dve)

        @block.sync
        def _(sp):
            run(sp, lambda t, j: sp_slot(sp, t, j))
            ge(sp, p_out, NPAIR, 16)

        @block.gpsimd
        def _(pool):
            beside.pool_program(pool)


NP_ = 8
BN = 128
E = 8
GT = 4
GROUP = GT * P
NGROUP = T // GROUP
FT = 256
CAP = T + FT
META = 4
RW = D + META
NTILE = 2 * T // FT + E - 1
SPARE = E * CAP
NBESIDE = 7 + 12
NOWHERE = float(1 << 20)
EPS = 1e-5


class DispatchConstants:

    def __init__(self, nc, io, keep, made, xs_dram):
        self.io, self.made, self.xs_dram = io, made, xs_dram
        self.prof_i = keep("prof_i", [P, B], I32)
        self.onehot = keep("onehot", [P, B], BF16)
        self.parts = keep("parts", [3 * 32, 3 * D + BN], BF16)
        self.centT = keep("centT", [P, KD, E])
        self.c2 = keep("c2", [P, E])
        self.upper = keep("upper", [P, P], BF16)
        self.ones = keep("ones", [P, P], BF16)
        self.rev = keep("rev", [P, E])
        self.ramp = keep("ramp", [P, NTILE])
        self.steps = keep("steps", [P, T // FT])
        self.tok = keep("tok", [P, GT])
        self.ce = keep("ce", [P, E])
        self.pad = keep("pad", [P, 2, RW])
        self.spare = keep("spare", [P, 2])
        self.zero8 = keep("zero8", [P, E])
        self.WD = keep("WD", [P, 2, 2 * GT, KD, BN])
        self.WU = keep("WU", [P, 2, 2 * GT, D])
        self.c_w, self.c_c, self.c_v = made("beside_in", 16), made("c_c"), made("c_v")
        self.c_p, self.c_r, self.c_f = made("c_p"), made("c_r", 16), made("c_f", 16)
        self.w_in = [made(f"w_in{j}", 16) for j in range(2)]

    def temporaries(self, sb):
        self.prof = sb("prof", [P, B])
        self.row_of = sb("row_of", [P, 1])
        self.raw = sb("raw", [32, 3 * D + BN])
        self.rest = sb("rest", [32, 3 * D + BN])
        self.cent = sb("cent", [E, D])
        self.cbc = sb("cbc", [P, E, D])
        self.nvec = 0

    def loads(self, eng):
        io = self.io
        tables = ("L0_cond2_up_b", "L0_cond2_ln_g", "L0_cond2_ln_b", "L0_cond2_down_b")
        self.c_c.wait(eng, 1)
        loads = [(self.prof_i[:, :], io["itok_B_0_6"].rearrange("(o b) -> o b", o=1).broadcast_to([P, B])),
                 (self.cent[:, :], io["L0_ffn_centroid"]),
                 (self.cbc[:, :, :],
                  io["L0_ffn_centroid"].rearrange("(o e) d -> o e d", o=1).broadcast_to([P, E, D]))]
        loads += [(self.raw[0:NP_, i * D:i * D + (BN if i == 3 else D)], io[k]) for i, k in enumerate(tables)]
        return [lambda to=to, rows=rows: self.c_w.by(eng.dma_start(to, rows)) for to, rows in loads]

    def pool_program(self, pool):
        pad, n = self.pad, [0]

        def step(instruction):
            self.c_c.by(instruction)
            n[0] += 1
            self.c_c.wait(pool, n[0])

        step(pool.memset(self.raw[:, :], 0.0))
        for i in range(4):
            step(pool.iota(self.row_of[32 * i:32 * i + 32, :], pattern=[[0, 1]], base=0, channel_multiplier=1,
                           allow_small_or_imprecise_dtypes=True))
        step(pool.memset(self.ones[:, :], 1.0))
        step(pool.memset(pad[:, :, :], 0.0))
        step(pool.memset(pad[:, :, D + 2:D + 3], NOWHERE))
        step(pool.memset(self.spare[:, :], 0.0))
        step(pool.memset(self.zero8[:, :], 0.0))
        step(pool.affine_select(out=self.upper[:, :], in_=self.ones[:, :], compare_op=ALU.is_gt, fill=0.0, base=0,
                                pattern=[[1, P]], channel_multiplier=-1))
        for to, pattern, base, down in ((self.rev, [-1, E], E, 0), (self.ramp, [1, NTILE], 0, 0),
                                        (self.steps, [FT, T // FT], 0, 0), (self.tok, [P, GT], -GROUP, 1),
                                        (self.ce, [CAP, E], 0, 0)):
            step(pool.iota(to[:, :], pattern=[pattern], base=base, channel_multiplier=down,
                           allow_small_or_imprecise_dtypes=True))

    def pool_more(self, pool):
        for s in range(2):
            self.c_f.by(pool.dma_start(self.xs_dram[SPARE + s * P:SPARE + (s + 1) * P, :], self.pad[:, s, :]))
        self.c_w.wait(pool, 16 * NBESIDE)
        self.c_c.by(pool.tensor_tensor(self.cbc[:, :, :], self.cbc[:, :, :], self.cbc[:, :, :], ALU.mult))

    def dve_step(self, dve, instruction):
        self.c_v.by(instruction)
        self.nvec += 1
        self.c_v.wait(dve, self.nvec)

    def dve_program(self, dve, part):
        raw, rest, parts = self.raw, self.rest, self.parts
        step = lambda instruction: self.dve_step(dve, instruction)
        if part == 1:
            step(dve.tensor_tensor(rest[:, :], rest[:, :], parts[32:64, :], ALU.subtract))
            step(dve.tensor_copy(parts[64:96, :], rest[:, :]))
        if part == 2:
            step(dve.tensor_reduce(self.c2[:, :], self.cbc[:, :, :], AX, ALU.add))
        if part:
            return
        self.c_w.wait(dve, 16 * NBESIDE)
        self.c_c.wait(dve, 17)
        step(dve.tensor_copy(self.prof[:, :], self.prof_i[:, :]))
        step(dve.tensor_scalar(self.onehot[:, :], self.prof[:, :], self.row_of[:, 0:1], None, ALU.is_equal))
        step(dve.tensor_copy(parts[0:32, :], raw[:, :]))
        step(dve.tensor_tensor(rest[:, :], raw[:, :], parts[0:32, :], ALU.subtract))
        step(dve.tensor_copy(parts[32:64, :], rest[:, :]))

    def pe_end(self, pe, F0, ident):
        self.c_w.wait(pe, 16 * NBESIDE)
        for k in range(KD):
            last = pe.transpose(F0[:, k * E:(k + 1) * E], self.cent[:, k * P:(k + 1) * P], ident[0:E, 0:E])
        self.c_p.by(last)

    def dve_end(self, dve, F0):
        self.c_p.wait(dve, 1)
        self.dve_step(dve, dve.tensor_scalar(
            self.centT[:, :, :], F0[:, 0:KD * E].rearrange("p (k e) -> p k e", k=KD), -2.0, None, ALU.mult))

    def pool_end(self, pool):
        self.c_f.wait(pool, 16 * 2)

    def projections(self, eng, g, j, batches):
        arrived = self.w_in[j]
        for b in batches:
            q = eng.value_load(self.prof_i[0:1, bass.ds(g * (2 * GT) + b, 1)], min_val=0, max_val=NP_ - 1)
            arrived.by(eng.dma_start(self.WD[:, j, b, :, :], self.io["L0_cond2_down_w"][bass.ds(q, 1)].rearrange(
                "o (k p) n -> p (o k) n", p=P)))
            arrived.by(eng.dma_start(self.WU[:, j, b, :], self.io["L0_cond2_up_w"][bass.ds(q, 1)].rearrange(
                "o p n -> p (o n)")))


def dispatch(nc, io, sb, made, dram, ps, ident, const, x1_dram, xs_dram, table_i, table_f, beside_act):
    F0, F1, G, O, Spair, Tpair = (ps[k] for k in ("F0", "F1", "G", "O", "Spair", "Tpair"))
    prof_i, onehot, parts, centT, c2, upper, ones, rev = (
        const.prof_i, const.onehot, const.parts, const.centT, const.c2, const.upper, const.ones, const.rev)
    ramp, steps, tok, ce, pad, spare, zero8, WD, WU, w_in, c_r = (
        const.ramp, const.steps, const.tok, const.ce, const.pad, const.spare, const.zero8, const.WD, const.WU,
        const.w_in, const.c_r)
    ohg = sb("ohg", [3 * 32, 2, 2 * GT, S], BF16)
    ce_i = sb("ce_i", [P, E], I32)
    X1 = sb("X1", [P, 2, GT, D])
    XT = sb("X1T", [P, KD, GROUP])
    ZT = sb("ZT", [BN, GROUP])
    Y = sb("Y", [P, GT, D])
    bst = sb("bst", [P, GT, 6])
    mv = sb("mv", [P, GT, 2])
    std = sb("std", [P, GT])
    rstd = sb("rstd", [P, GT])
    ROW = sb("ROW", [P, 2, GT, RW])
    HT = sb("HT", [P, KD, GROUP])
    sq = sb("sq", [P, D])
    x2 = sb("x2", [P, GT])
    small = [P, GT, E]
    d2, eq, tmp, ohlo, ohhi = (sb(n, small) for n in ("d2", "eq", "tmp", "ohlo", "ohhi"))
    m12 = sb("m12", [P, 2, GT])
    s12 = sb("s12", [P, 2, GT])
    r12 = sb("r12", [P, 2, GT])
    first = sb("first", [P, GT])
    ex = sb("ex", [P, GT])
    w12 = sb("w12", [P, 2, GT])
    oh1 = sb("oh1", small)
    oh2 = sb("oh2", small)
    M = sb("M", small, BF16)
    pos = sb("pos", [P, 2, GT])
    idx = sb("idx", [P, 2, 2, GT], I32)
    nt = sb("nt", [P, E])
    cnt = sb("cnt", [P, E])
    incl = sb("incl", [P, E])
    big = sb("big", [P, NTILE, E])
    big2 = sb("big2", [P, E, T // FT])
    sumt = sb("sumt", [P, NTILE])

    x1_in = [made(f"x1_in{j}", 16) for j in range(2)]
    names = ["xT_ps", "xT", "ohg", "z_ps", "zt", "y_ps", "y", "bst", "mv", "std", "rstd", "veps",
             "gb_ps0", "gb_ps1", "hn", "hg0", "hg1", "hb0", "hb1",
             "hT_ps", "hT", "x2", "dot_ps", "d2a", "d2b", "d2", "m1", "eq1", "eqr1", "r1", "oh1", "d2m",
             "m2", "eq2", "eqr2", "r2", "oh2", "s12", "dif", "ex", "den", "rden", "w2", "first", "wd", "wf", "wlo", "whi",
             "rlo", "M", "ohlo", "ohhi", "rank_ps", "rank", "plo", "phi", "tlo", "idx", "ce", "tok", "tokw", "t2"]
    chains = [("d2b", "d2", "m1", "eq1"), ("eqr1", "r1", "oh1", "d2m"), ("eq2", "eqr2", "r2", "oh2"),
              ("rlo", "ohlo", "den", "rden"), ("tok", "w2", "wd", "wf"), ("wlo", "whi", "tokw", "plo"),
              ("first", "tlo", "t2", "phi"), ("bst", "mv", "rstd", "hn")]
    C = {k: made("c_" + k) for k in names if not any(k in c for c in chains)}
    place = {}
    for c in chains:
        C.update(dict.fromkeys(c, made("c_" + "_".join(c))))
        place.update((k, n) for n, k in enumerate(c))
    carried = made("dispatch_carried")
    rows_out = [made(f"rows_out{j}", 16) for j in range(2)]

    def ge(eng, m, x, mul=1):
        if isinstance(x, int):
            if x > 0:
                eng.wait_ge(m.sem, x * mul)
        else:
            eng.wait_ge(m.sem, x * mul if mul != 1 else x)

    def run(eng, body):
        for g in range(-1, 3):
            body(g, g % 2)
        with eng.Fori(3, NGROUP - 2, 2) as g:
            for j in range(2):
                body(g + j, (1 + j) % 2)
        body(NGROUP - 1, (NGROUP - 1) % 2)
        body(NGROUP, NGROUP % 2)

    def x1_loaded(eng, n, j):
        ge(eng, x1_in[j], n + (1 - j), 8)

    def front(g):
        return not isinstance(g, int) or 0 <= g < NGROUP

    def back(g):
        return not isinstance(g, int) or g > 0

    def ahead(g):
        return not isinstance(g, int) or g + 1 < NGROUP

    def pe_slot(pe, g, j):
        def ranks(x):
            ge(pe, C["M"], x)
            ge(pe, C["d2a"], x)
            at = O[:, 64:64 + GT * E]
            for s in range(GT):
                last = pe.matmul(at[:, s * E:(s + 1) * E], upper[:, :], M[:, s, :], start=True, stop=(s == 0))
                for q in range(s):
                    last = pe.matmul(at[:, s * E:(s + 1) * E], ones[:, :], M[:, q, :], start=False, stop=(q == s - 1))
            for q in range(GT):
                last = pe.matmul(O[:, 128:128 + E], ones[:, :], M[:, q, :], start=(q == 0), stop=(q == GT - 1))
            C["rank_ps"].by(last)

        def turned(rows, done):
            for k in range(KD):
                for s in range(GT):
                    last = pe.transpose((F0, F1)[k][:, s * P:(s + 1) * P], rows[:, s, k * P:(k + 1) * P], ident[:, :])
            C[done].by(last)

        def gains(half):
            ge(pe, C["y" if half else "hb0"], g + half)
            for s in range(2 * half, 2 * half + 2):
                last = pe.matmul((Tpair, Spair)[half][:, (s % 2) * 512:(s % 2) * 512 + 512],
                                 ohg[:, j, 2 * s:2 * s + 2, :].rearrange("r b s -> r (b s)"), parts[:, D:3 * D],
                                 start=True, stop=True)
            C[f"gb_ps{half}"].by(last)

        def down(b0, b1):
            for b in range(b0, b1):
                for k in range(KD):
                    last = pe.matmul(G[:, b * S:(b + 1) * S], WD[:, 1 - j, b, k, :], XT[:, k, b * S:(b + 1) * S],
                                     start=False, stop=(k == KD - 1), skip_group_check=True)
            return last

        if ahead(g):
            x1_loaded(pe, g + 2, 1 - j)
            ge(pe, C["hT"], g - 1)
            turned(X1[:, 1 - j, :, :], "xT_ps")
        if front(g):
            ge(pe, C["zt"], g + 1)
            ge(pe, C["hb1"], g)
            for s in range(GT):
                pe.matmul(Spair[:, s * D:(s + 1) * D], ohg[:, j, 2 * s:2 * s + 2, :].rearrange("r b s -> r (b s)"),
                          parts[:, 0:D], start=True, stop=False, skip_group_check=True)
                for h in range(2):
                    b = 2 * s + h
                    last = pe.matmul(Spair[S * h:S * h + S, s * D:(s + 1) * D], ZT[:, b * S:(b + 1) * S], WU[:, j, b, :],
                                     start=False, stop=True, skip_group_check=True)
            C["y_ps"].by(last)
        if back(g):
            ge(pe, C["hb1"], g)
            ge(pe, C["xT"], min(g + 2, NGROUP) if isinstance(g, int) else g + 2)
            turned(ROW[:, 1 - j, :, :], "hT_ps")
        if front(g):
            gains(0)
        if ahead(g):
            ge(pe, C["ohg"], g + 2)
            ge(pe, C["zt"], g + 1)
            pe.matmul(G[:, :], parts[:, 3 * D:3 * D + BN], ohg[:, 1 - j, :, :].rearrange("r b s -> r (b s)"),
                      start=True, stop=False, skip_group_check=True)
            ge(pe, C["xT"], g + 2)
            ge(pe, w_in[1 - j], g + 2 + j, 8 * 4 * GT)
            down(0, 2)
        if front(g):
            gains(1)
        if back(g):
            ge(pe, C["hT"], g)
            ge(pe, C["ce"], g - 1)
            for s in range(GT):
                for k in range(KD):
                    last = pe.matmul(O[:, s * E:(s + 1) * E], HT[:, k, s * P:(s + 1) * P], centT[:, k, :],
                                     start=(k == 0), stop=(k == KD - 1))
            C["dot_ps"].by(last)
        if ahead(g):
            C["z_ps"].by(down(2, 2 * GT))
        if back(g):
            ranks(g)

    def act_slot(act, g, j):
        if ahead(g):
            ge(act, C["xT_ps"], g + 2)
            act.activation(XT[:, 0, :], F0[:, :], ACT.Copy)
            C["xT"].by(act.activation(XT[:, 1, :], F1[:, :], ACT.Copy))
        if ahead(g):
            ge(act, C["gb_ps1"], g)
            at = 2 * GT * (g + 1) if isinstance(g, int) else g * (2 * GT) + 2 * GT
            C["ohg"].by(act.activation(ohg[:, 1 - j, :, :],
                                       onehot[0:96, bass.ds(at, 2 * GT)].unsqueeze(2).broadcast_to([96, 2 * GT, S]),
                                       ACT.Copy))
        if back(g):
            ge(act, C["hT_ps"], g)
            act.activation(HT[:, 0, :], F0[:, :], ACT.Copy)
            C["hT"].by(act.activation(HT[:, 1, :], F1[:, :], ACT.Copy))
        if front(g):
            ge(act, C["veps"], g + 1)
            C["std"].by(act.activation(std[:, :], std[:, :], ACT.Sqrt))
        if back(g):
            for s in range(GT):
                ge(act, C["x2"], (g - 1) * GT + s)
                C["x2"].by(act.activation(sq[:, :], ROW[:, 1 - j, s, 0:D], ACT.Square, accum_out=x2[:, s:s + 1]))
            ge(act, C["m2"], g)
            C["s12"].by(act.activation(s12[:, :, :], m12[:, :, :], ACT.Sqrt))
            ge(act, C["dif"], g)
            C["ex"].by(act.activation(ex[:, :], ex[:, :], ACT.Exp))
        if ahead(g):
            ge(act, C["z_ps"], g + 2)
            C["zt"].by(act.activation(ZT[:, :], G[:, :], ACT.Relu))

    GB = [banks[:, :].rearrange("p (s c d) -> p s c d", s=2, c=2) for banks in (Tpair, Spair)]

    def dve_slot(dve, g, j):
        bc4 = lambda x: x.unsqueeze(2).broadcast_to(small)
        bce = lambda x: x.unsqueeze(1).broadcast_to(small)

        values = {}

        def after(name, x):
            if name not in place:
                ge(dve, C[name], x)
            elif isinstance(x, int):
                ge(dve, C[name], 4 * (x - 1) + place[name] + 1)
            else:
                n, fore = place[name], name in chains[-1]
                if (n, fore) not in values:
                    values[n, fore] = x * 4 + (n - 3)
                dve.wait_ge(C[name].sem, values[n, fore])

        if front(g):
            front_dve(dve, g, j, after)
        if back(g):
            x = g

            def do(name, instruction, *needs):
                C[name].by(instruction)

            after("dot_ps", x)
            do("d2a", dve.tensor_tensor(d2[:, :, :], O[:, 0:GT * E].rearrange("p (s e) -> p s e", s=GT), bce(c2[:, :]),
                                        ALU.add))
            after("d2a", x)
            ge(dve, C["x2"], x * GT)
            do("d2b", dve.tensor_tensor(d2[:, :, :], d2[:, :, :], bc4(x2[:, :]), ALU.add))
            after("d2b", x)
            do("d2", dve.tensor_scalar(d2[:, :, :], d2[:, :, :], 1e-12, None, ALU.max))
            after("d2", x)
            do("m1", dve.tensor_reduce(m12[:, 0, :], d2[:, :, :], AX, ALU.max))
            after("m1", x)
            do("eq1", dve.tensor_tensor(eq[:, :, :], d2[:, :, :], bc4(m12[:, 0, :]), ALU.is_equal))
            after("eq1", x)
            do("eqr1", dve.tensor_tensor(eq[:, :, :], eq[:, :, :], bce(rev[:, :]), ALU.mult))
            after("eqr1", x)
            do("r1", dve.tensor_reduce(r12[:, 0, :], eq[:, :, :], AX, ALU.max))
            after("r1", x)
            do("oh1", dve.tensor_tensor(oh1[:, :, :], bc4(r12[:, 0, :]), bce(rev[:, :]), ALU.is_equal))
            after("oh1", x)
            do("d2m", dve.scalar_tensor_tensor(out=d2[:, :, :], in0=oh1[:, :, :], scalar=-3.0e38, in1=d2[:, :, :],
                                               op0=ALU.mult, op1=ALU.add))
            after("d2m", x)
            do("m2", dve.tensor_reduce(m12[:, 1, :], d2[:, :, :], AX, ALU.max))
            after("m2", x)
            do("eq2", dve.tensor_tensor(eq[:, :, :], d2[:, :, :], bc4(m12[:, 1, :]), ALU.is_equal))
            after("eq2", x)
            do("eqr2", dve.tensor_tensor(eq[:, :, :], eq[:, :, :], bce(rev[:, :]), ALU.mult))
            after("eqr2", x)
            do("r2", dve.tensor_reduce(r12[:, 1, :], eq[:, :, :], AX, ALU.max))
            after("r2", x)
            do("oh2", dve.tensor_tensor(oh2[:, :, :], bc4(r12[:, 1, :]), bce(rev[:, :]), ALU.is_equal))
            after("oh2", x)
            ge(dve, C["rank_ps"], x - 1)
            do("M", dve.tensor_tensor(M[:, :, :], oh1[:, :, :], oh2[:, :, :], ALU.add))
            after("s12", x)
            do("dif", dve.tensor_tensor(ex[:, :], s12[:, 1, :], s12[:, 0, :], ALU.subtract))
        if front(g):
            gain(dve, g, 1, after)
            ge(dve, rows_out[j], g - j, 16 * GT)
            shift(dve, g, j, 0, after)
            shift(dve, g, j, 1, after)
        if back(g):
            do("first", dve.tensor_tensor(first[:, :], r12[:, 0, :], r12[:, 1, :], ALU.is_gt))
            ge(dve, C["hT_ps"], x)
            rl = ROW[:, 1 - j, :, D + 3]
            do("rlo", dve.tensor_tensor(rl, r12[:, 0, :], r12[:, 1, :], ALU.max))
            after("rlo", x)
            do("ohlo", dve.tensor_tensor(ohlo[:, :, :], bc4(rl), bce(rev[:, :]), ALU.is_equal))
            after("ohlo", x)
            after("M", x)
            do("ohhi", dve.tensor_tensor(ohhi[:, :, :], M[:, :, :], ohlo[:, :, :], ALU.subtract))
            after("ex", x)
            if not front(g):
                do("tok", dve.tensor_scalar(tok[:, :], tok[:, :], float(GROUP), None, ALU.add))
            do("den", dve.tensor_scalar(w12[:, 0, :], ex[:, :], 1.0, None, ALU.add))
            after("den", x)
            do("rden", dve.reciprocal(w12[:, 0, :], w12[:, 0, :]))
            after("rden", x)
            do("w2", dve.tensor_tensor(w12[:, 1, :], w12[:, 0, :], ex[:, :], ALU.mult))
            after("w2", x)
            do("wd", dve.tensor_tensor(ex[:, :], w12[:, 0, :], w12[:, 1, :], ALU.subtract))
            after("wd", x)
            after("first", x)
            do("wf", dve.tensor_tensor(ex[:, :], ex[:, :], first[:, :], ALU.mult))
            after("wf", x)
            do("wlo", dve.tensor_tensor(ROW[:, 1 - j, :, D], w12[:, 1, :], ex[:, :], ALU.add))
            do("whi", dve.tensor_tensor(ROW[:, 1 - j, :, D + 1], w12[:, 0, :], ex[:, :], ALU.subtract))
            after("tok", x)
            do("tokw", dve.tensor_copy(ROW[:, 1 - j, :, D + 2], tok[:, :]))
            after("rank_ps", x)
            do("rank", dve.tensor_tensor(tmp[:, :, :], O[:, 64:64 + GT * E].rearrange("p (s e) -> p s e", s=GT),
                                         bce(ce[:, :]), ALU.add))
            after("rank", x)
            after("ohhi", x)
            do("tlo", dve.tensor_tensor(ohlo[:, :, :], ohlo[:, :, :], tmp[:, :, :], ALU.mult))
            do("t2", dve.tensor_tensor(ohhi[:, :, :], ohhi[:, :, :], tmp[:, :, :], ALU.mult))
            do("ce", dve.tensor_tensor(ce[:, :], ce[:, :], O[:, 128:128 + E], ALU.add))
            after("tlo", x)
            after("t2", x)
            do("plo", dve.tensor_reduce(pos[:, 0, :], ohlo[:, :, :], AX, ALU.add))
            do("phi", dve.tensor_reduce(pos[:, 1, :], ohhi[:, :, :], AX, ALU.add))
            after("plo", x)
            after("phi", x)
            ge(dve, rows_out[1 - j], x - 2 + j, 16 * GT)
            after("whi", x)
            after("wlo", x)
            after("tokw", x)
            do("idx", dve.tensor_copy(idx[:, 1 - j, :, :], pos[:, :, :]))

    def front_dve(dve, g, j, after):
        x = g + 1
        after("hb1", g)
        after("y_ps", x)
        C["y"].by(dve.tensor_tensor(Y[:, :, :], Spair[:, :].rearrange("p (s d) -> p s d", s=GT), X1[:, j, :, :],
                                    ALU.add))
        after("y", x)
        for s in range(GT):
            last = dve.bn_stats(bst[:, s, :], Y[:, s, :])
        C["bst"].by(last)
        after("bst", x)
        if back(g):
            C["tok"].by(dve.tensor_scalar(tok[:, :], tok[:, :], float(GROUP), None, ALU.add))
        for s in range(GT):
            last = dve.bn_aggr(mv[:, s, :], bst[:, s, :])
        C["mv"].by(last)
        after("mv", x)
        C["veps"].by(dve.tensor_scalar(std[:, :], mv[:, :, 1], EPS, None, ALU.add))
        after("std", x)
        C["rstd"].by(dve.reciprocal(rstd[:, :], std[:, :]))
        after("rstd", x)
        for s in range(GT):
            last = dve.tensor_scalar(Y[:, s, :], Y[:, s, :], mv[:, s, 0:1], rstd[:, s:s + 1], ALU.subtract, ALU.mult)
        C["hn"].by(last)
        after("hn", x)
        gain(dve, g, 0, after)

    def gain(dve, g, half, after):
        ss = slice(2 * half, 2 * half + 2)
        after(f"gb_ps{half}", g + 1)
        C[f"hg{half}"].by(dve.tensor_tensor(Y[:, ss, :], Y[:, ss, :], GB[half][:, :, 0, :], ALU.mult))

    def shift(dve, g, j, half, after):
        ss = slice(2 * half, 2 * half + 2)
        after(f"hg{half}", g + 1)
        C[f"hb{half}"].by(dve.tensor_tensor(ROW[:, j, ss, 0:D], Y[:, ss, :], GB[half][:, :, 1, :], ALU.add))

    def pool_slot(pool, g, j):
        if back(g):
            ge(pool, C["idx"], g)
            carry(pool, spare, carried, g - 1)
            for k in range(2):
                for s in range(GT):
                    rows_out[1 - j].by(pool.indirect_dma_start(
                        xs_dram, bass.IndirectOffsetOnAxis(idx[:, 1 - j, k, s:s + 1], 0), ROW[:, 1 - j, s, :], None))

    x1_rows = x1_dram.rearrange("(n p) d -> p n d", p=P)

    def sp_load(sp, g, j):
        ge(sp, C["xT_ps"], g)
        ge(sp, C["y"], min(g, NGROUP - 1) if isinstance(g, int) else g)
        if ahead(g):
            tiles = bass.ds(g * GT + GT, GT)
            x1_in[1 - j].by(sp.dma_start(X1[:, 1 - j, :, :], x1_rows[:, tiles, :]))
        if ahead(g):
            if not isinstance(g, int) or g >= 0:
                ge(sp, C["z_ps"], g)
                ge(sp, C["y_ps"], g)
                const.projections(sp, g + 1, 1 - j, range(2 * GT))

    with nc.Block() as block:
        @block.tensor
        def _(pe):
            run(pe, lambda g, j: pe_slot(pe, g, j))

        @block.scalar
        def _(act):
            run(act, lambda g, j:
                (act_slot(act, g, j), beside_act(act, g)))

        @block.vector
        def _(dve):
            run(dve, lambda g, j: dve_slot(dve, g, j))
            ch = [0]
            done = C["t3"] = made("c_t3")

            def step(instruction):
                done.by(instruction)
                ch[0] += 1
                ge(dve, done, ch[0])

            ge(dve, C["ce"], NGROUP)
            step(dve.tensor_copy(ce_i[:, :], ce[:, :]))
            step(dve.scalar_tensor_tensor(out=cnt[:, :], in0=rev[:, :], scalar=float(CAP), in1=ce[:, :], op0=ALU.mult,
                                          op1=ALU.add))
            step(dve.tensor_scalar(cnt[:, :], cnt[:, :], -float(SPARE), None, ALU.add))
            step(dve.tensor_tensor(big2[:, :, :], cnt[:, :].unsqueeze(2).broadcast_to([P, E, T // FT]),
                                   steps[:, :].unsqueeze(1).broadcast_to([P, E, T // FT]), ALU.is_gt))
            step(dve.tensor_reduce(nt[:, :], big2[:, :, :], AX, ALU.add))
            step(dve.tensor_tensor_scan(incl[:, :], nt[:, :], zero8[:, :], 0.0, ALU.add, ALU.add))
            wide = [P, NTILE, E]
            step(dve.tensor_tensor(big[:, :, :], incl[:, :].unsqueeze(1).broadcast_to(wide),
                                   ramp[:, :].unsqueeze(2).broadcast_to(wide), ALU.is_le))
            step(dve.tensor_reduce(table_f[:, :], big[:, :, :], AX, ALU.add))
            step(dve.tensor_tensor(big[:, :, :], big[:, :, :], nt[:, :].unsqueeze(1).broadcast_to(wide), ALU.mult))
            step(dve.tensor_reduce(sumt[:, :], big[:, :, :], AX, ALU.add))
            step(dve.tensor_tensor(sumt[:, :], ramp[:, :], sumt[:, :], ALU.subtract))
            step(dve.tensor_scalar(sumt[:, :], sumt[:, :], float(FT), None, ALU.mult))
            step(dve.scalar_tensor_tensor(out=sumt[:, :], in0=table_f[:, :], scalar=float(CAP), in1=sumt[:, :],
                                          op0=ALU.mult, op1=ALU.add))
            step(dve.tensor_scalar(sumt[:, :], sumt[:, :], float(SPARE), None, ALU.min))
            step(dve.tensor_copy(table_i[:, 0, :], sumt[:, :]))
            step(dve.tensor_scalar(table_i[:, 1, :], table_f[:, :], float(E - 1), None, ALU.min))
            step(dve.tensor_scalar(table_i[:, 2, 0:2], table_i[:, 1, 0:2], 0.0, None, ALU.not_equal))
            step(dve.tensor_tensor(table_i[:, 2, 2:NTILE], table_i[:, 1, 2:NTILE], table_i[:, 1, 0:NTILE - 2],
                                   ALU.not_equal))
            step(dve.tensor_scalar(table_f[:, :], table_f[:, :], -1.0, float(E), ALU.mult, ALU.add))

        @block.gpsimd
        def _(pool):
            run(pool, lambda g, j: pool_slot(pool, g, j))
            for j in range(2):
                ge(pool, rows_out[j], NGROUP, 16 * GT)

        @block.sync
        def _(sp):
            run(sp, lambda g, j: sp_load(sp, g, j))
            done = C["t3"]
            ge(sp, done, 1)
            for e in range(E):
                r = sp.value_load(ce_i[0:1, e:e + 1], min_val=e * CAP, max_val=e * CAP + T)
                c_r.by(sp.dma_start(xs_dram[bass.ds(r, FT), :].rearrange("(s p) w -> p s w", p=P), pad[:, :, :]))
            c_r.wait(sp, 16 * E)


H = 684
NFULL = H // P
HR = H - NFULL * P
NBLK = 2 * NFULL + 1
NCH = NFULL + 1
UW = 2 * KD * NBLK * P
DW = 2 * NCH * D
LOW = 64
FS = FT // P


class Biases:

    def __init__(self, io, keep, made, arrived):
        self.io = io
        self.bias = keep("bias", [P, E, 2 * NCH])
        self.clear, self.arrived = made("b_clear"), arrived
        self.turned, self.done = made("b_turned"), made("b_done")

    def temporaries(self, sb):
        self.rows = sb("bias_rows", [NCH * E, 2, P])

    def pool_program(self, pool):
        self.clear.by(pool.memset(self.rows[:, :, :], 0.0))

    def loads(self, eng):
        self.clear.wait(eng, 1)
        loads = []
        for i, k in enumerate(("L0_ffn_bg", "L0_ffn_b1")):
            loads.append((self.rows[0:E, i, 0:HR], self.io[k][:, NFULL * P:H]))
            loads += [(self.rows[(c + 1) * E:(c + 2) * E, i, :], self.io[k][:, c * P:(c + 1) * P])
                      for c in range(NFULL)]
        return [lambda to=to, rows=rows: self.arrived.by(eng.dma_start(to, rows)) for to, rows in loads]

    def pe_end(self, pe, at, ident):
        self.arrived.wait(pe, 16 * NBESIDE)
        for i in range(2):
            last = pe.transpose(at[:, i * NCH * E:(i + 1) * NCH * E], self.rows[:, i, :],
                                ident[0:NCH * E, 0:NCH * E])
        self.turned.by(last)

    def act_end(self, act, at):
        self.turned.wait(act, 1)
        for i in range(2):
            self.done.by(act.activation(self.bias[:, :, i * NCH:(i + 1) * NCH],
                                        at[:, i * NCH * E:(i + 1) * NCH * E].rearrange("p (c e) -> p e c", c=NCH),
                                        ACT.Copy))
        self.done.wait(act, 2)


def split_weights(io, sb, made, pool, up_dram, dn_dram, between):
    up = sb("up_stage", [P, 2, KD, NBLK, P])
    dn = sb("dn_stage", [P, 2, NCH, D])
    upb = sb("up_parts", [P, 2, KD, NBLK, P], BF16)
    dnb = sb("dn_parts", [P, 2, NCH, D], BF16)
    spare = sb("split_spare", [P, 2])
    carried = made("split_carried")
    s_in, s_out, s_do = [made(f"split_in{j}", 16) for j in range(2)], made("split_out", 16), made("split_do")
    s_do.by(pool.memset(up[:, :, :, NFULL, :], 0.0))
    s_do.by(pool.memset(dn[:, :, NCH - 1, :], 0.0))
    s_do.by(pool.memset(spare[:, :], 0.0))
    s_do.wait(pool, 3)
    NIN, NDO = 7, 4

    def load_up(e, j, i, name):
        rows = io[name][bass.ds(e, 1)].rearrange("o (k p) n -> p (o k) n", p=P)
        if i == 0:
            s_in[j].by(pool.dma_start(up[:, j, :, :, :].rearrange("p k b n -> p k (b n)")[:, :, 0:H], rows))
        else:
            s_in[j].by(pool.dma_start(up[:, j, :, NFULL + 1:, :].rearrange("p k b n -> p k (b n)"),
                                      rows[:, :, 0:NFULL * P]))
            s_in[j].by(pool.dma_start(up[:, j, :, NFULL, 64:64 + HR], rows[:, :, NFULL * P:H]))

    def load_down(e, j):
        pick = bass.ds(e, 1)
        w2 = io["L0_ffn_W2"][pick]
        s_in[j].by(pool.dma_start(dn[:, j, 0:NFULL, :],
                                  w2[:, 0:NFULL * P, :].rearrange("o (c p) d -> p (o c) d", p=P)))
        for at in (0, LOW):
            s_in[j].by(pool.dma_start(dn[at:at + HR, j, NFULL, :], w2[:, NFULL * P:H, :].rearrange("o p d -> p (o d)")))
        s_in[j].by(pool.dma_start(dn[HR:HR + 1, j, NFULL, :], io["L0_ffn_b2"][pick, :]))

    def split(e, j, ahead=True):
        s_in[j].wait(pool, (e + (2 - j)) * (8 * NIN))
        s_out.wait(pool, e * 32)
        n, e1 = e * NDO, e + 1
        carry(pool, spare, carried, e * 2)
        if ahead:
            load_up(e1, 1 - j, 0, "L0_ffn_Wg")
        s_do.by(pool.tensor_copy(upb[:, 0], up[:, j]))
        if ahead:
            load_up(e1, 1 - j, 1, "L0_ffn_W1")
        s_do.wait(pool, n + 4)
        s_do.by(pool.tensor_tensor(upb[:, 1], up[:, j], upb[:, 0], ALU.subtract))
        s_do.wait(pool, n + 5)
        s_out.by(pool.dma_start(up_dram[bass.ds(e, 1)].rearrange("o p w -> p (o w)"),
                                upb[:, :, :, :, :].rearrange("p a k b n -> p (a k b n)")))
        carry(pool, spare, carried, e * 2 + 1)
        s_do.by(pool.tensor_copy(dnb[:, 0], dn[:, j]))
        if ahead:
            load_down(e1, 1 - j)
        s_do.wait(pool, n + 6)
        s_do.by(pool.tensor_tensor(dnb[:, 1], dn[:, j], dnb[:, 0], ALU.subtract))
        s_do.wait(pool, n + 7)
        s_out.by(pool.dma_start(dn_dram[bass.ds(e, 1)].rearrange("o p w -> p (o w)"),
                                dnb[:, :, :, :].rearrange("p a c d -> p (a c d)")))

    load_up(0, 0, 0, "L0_ffn_Wg")
    load_up(0, 0, 1, "L0_ffn_W1")
    load_down(0, 0)
    for e in range(2):
        split(e, e)
        if e == 1:
            between()
    with pool.Fori(2, E - 3, 2) as e:
        for j in range(2):
            split(e + j if j else e, j)
    split(E - 2, 0)
    split(E - 1, 1, ahead=False)
    s_out.wait(pool, 32 * E)


def load_first(eng, g, UP, DN, up_dram, dn_dram, first_in):
    if not isinstance(g, int):
        return
    if g in (0, 2):
        j = g // 2
        first_in.by(eng.dma_start(DN[:, j, :, :, :].rearrange("p a c d -> p (a c d)"), dn_dram[0]))
    if g in (1, NGROUP - 1):
        j = int(g > 1)
        first_in.by(eng.dma_start(UP[:, j, :, :, :, :].rearrange("p a k b n -> p (a k b n)"), up_dram[0]))


def experts(nc, io, sb, made, ps, ident, bias, UP, DN, first_in, xs_dram, up_dram, dn_dram, table_i, table_f, out):
    Spair, Tpair = ps["Spair"], ps["Tpair"]
    GU = [Spair[:, 0:512], Spair[:, 512:1024], Tpair[:, 0:512], Tpair[:, 512:1024]]
    YP = [ps["F1"], ps["O"]]
    XP = ps["G"]
    XR = sb("rows", [P, 2, FS, RW])
    XT = sb("rowsT", [P, 2, KD, FT], BF16)
    BT = sb("BT", [P, 2, 2 * NCH])
    SIL = sb("SIL", [P, 2, FT])
    H32 = sb("H32", [P, 2, FT])
    UR = sb("UR", [HR, FT])
    HT = sb("innerT", [P, 2, NCH, FT], BF16)
    Z = sb("Z", [P, 2, FS, D])
    idx = sb("row_idx", [P, 2, FS], I32)
    wt = sb("row_wt", [P, 2, FS])
    islo = sb("islo", [P, FS])
    tl = sb("tl", [P, FS])
    spare = sb("expert_spare", [P, 2])

    e_set, spared, carried = made("e_set"), made("spared"), made("carried")
    xr_in, up_in, dn_in, bt_in, z_in, sent = ([made(f"{k}{j}", 16) for j in range(2)]
                                              for k in ("xr_in", "up_in", "dn_in", "bt_in", "z_in", "sent"))
    gu, sil, h32, hhi, hlo = ([made(f"{k}{c}") for c in range(3)] for k in ("gu", "sil", "h32", "hhi", "hlo"))
    ur, xT_ps, xhi, xlo, y_ps, yo, ilo, wl, wh, wdone, idone = (made("e_" + k) for k in (
        "ur", "xT_ps", "xhi", "xlo", "y_ps", "yo", "ilo", "wl", "wh", "wdone", "idone"))

    def ge(eng, m, x, mul=1):
        if isinstance(x, int):
            if x > 0:
                eng.wait_ge(m.sem, x * mul)
        else:
            eng.wait_ge(m.sem, x * mul if mul != 1 else x)

    def run(eng, body):
        for i in range(2):
            body(i, i)
        with eng.Fori(2, NTILE - 2, 2) as i:
            for j in range(2):
                body(i + j if j else i, j)
        body(NTILE - 1, 0)

    def loaded(eng, m, i, j, each=1):
        ge(eng, m[j], i + (2 - j), 8 * each)

    values = {}

    def chunk(eng, m, c, i):
        if isinstance(i, int):
            ge(eng, m[c % 3], 2 * i + c // 3 + 1 if i >= 0 else 0)
        else:
            key = (id(eng), id(i), c // 3)
            if key not in values:
                values[key] = (i, i * 2 + (c // 3 + 1))
            eng.wait_ge(m[c % 3].sem, values[key][1])

    def kr(c):
        return HR if c == 0 else P

    def transposes(pe, i, j):
        loaded(pe, xr_in, i, j)
        ge(pe, xlo, i)
        for k in range(KD):
            for s in range(FS):
                last = pe.transpose(XP[:, k * FT + s * P:k * FT + (s + 1) * P], XR[:, j, s, k * P:(k + 1) * P],
                                    ident[:, :])
        xT_ps.by(last)

    def pe_slot(pe, i, j):
        if isinstance(i, int) and i == 0:
            e_set.wait(pe, 1)
            transposes(pe, 0, 0)
        i1, im = i + 1, i - 1
        ge(pe, xlo, i1)
        loaded(pe, up_in, i, j)
        for c in range(NCH):
            at = GU[(NCH * j + c) % 4]
            if c >= 4:
                chunk(pe, h32, c - 4, i)
            else:
                chunk(pe, h32, c + 2, im)
            blocks = ((NFULL, at[:, 0:FT]),) if c == 0 else ((c - 1, at[:, 0:FT]), (NFULL + c, at[:, FT:2 * FT]))
            for b, to in blocks:
                for k in range(KD):
                    for n, (wp, xp) in enumerate(((0, 0), (0, 1), (1, 0))):
                        last = pe.matmul(to, UP[:, j, wp, k, b, :], XT[:, xp, k, :], start=(k == 0 and n == 0),
                                         stop=(k == KD - 1 and n == 2))
            gu[c % 3].by(last)
        if not (isinstance(i, int) and i == NTILE - 1):
            transposes(pe, i1, 1 - j)
        loaded(pe, dn_in, i, j)
        ge(pe, yo, i)
        for c in range(NCH):
            chunk(pe, hlo, c, i)
            dc = (c - 1) % NCH
            passes = ((0, 0, LOW + HR), (0, 1, HR + 1)) if c == 0 else ((0, 0, P), (0, 1, P), (1, 0, P))
            for s in range(FS):
                for n, (hp, wp, rows) in enumerate(passes):
                    last = pe.matmul(YP[s][:, 0:D], HT[0:rows, hp, c, s * P:(s + 1) * P], DN[0:rows, j, wp, dc, :],
                                     start=(c == 0 and n == 0), stop=(c == NCH - 1 and n == 2))
        y_ps.by(last)

    def act_slot(act, i, j):
        def high(c):
            chunk(act, h32, c, i)
            if c == 0:
                ge(act, y_ps, i)
            hhi[c % 3].by(act.activation(HT[0:kr(c), 0, c, :], H32[0:kr(c), c % 2, :], ACT.Copy))

        def xhigh(i, i1):
            ge(act, xT_ps, i1)
            xhi.by(act.activation(XT[:, 0, :, :], XP[:, :].rearrange("p (k t) -> p k t", k=KD), ACT.Copy))

        if isinstance(i, int) and i == 0:
            xhigh(0, 1)
        i1, im = i + 1, i - 1
        loaded(act, bt_in, i, j)
        for c in range(NCH):
            at = GU[(NCH * j + c) % 4]
            chunk(act, gu, c, i)
            if c >= 2:
                chunk(act, h32, c - 2, i)
            else:
                chunk(act, h32, c + 4, im)
            sil[c % 3].by(act.activation(SIL[0:kr(c), c % 2, :], at[0:kr(c), 0:FT], ACT.Silu,
                                         bias=BT[0:kr(c), j, c:c + 1]))
            if c == 0:
                ur.by(act.activation(UR[:, :], at[64:64 + HR, 0:FT], ACT.Copy))
            else:
                high(c - 1)
        high(NCH - 1)
        if not (isinstance(i, int) and i == NTILE - 1):
            xhigh(i1, i + 2)

    def dve_slot(dve, i, j):
        def low(c):
            chunk(dve, hhi, c, i)
            to = HT[LOW:LOW + HR, 0, c, :] if c == 0 else HT[:, 1, c, :]
            hlo[c % 3].by(dve.tensor_tensor(to, H32[0:kr(c), c % 2, :], HT[0:kr(c), 0, c, :],
                                        ALU.subtract))

        def incoming(i, i1, j):
            ge(dve, xhi, i1)
            xlo.by(dve.tensor_tensor(XT[:, 1, :, :].rearrange("p k t -> p (k t)"), XP[:, :],
                                     XT[:, 0, :, :].rearrange("p k t -> p (k t)"), ALU.subtract))
            if isinstance(i, int):
                tf = table_f[:, i:i + 1]
            else:
                tf = table_f[:, bass.ds(i, 1)]
            loaded(dve, sent, i - 2, j, 2)
            ilo.by(dve.tensor_tensor(islo[:, :], XR[:, j, :, D + 3], tf.broadcast_to([P, FS]), ALU.is_equal))
            idone.by(dve.tensor_copy(idx[:, j, :], XR[:, j, :, D + 2]))
            ge(dve, ilo, i1)
            wl.by(dve.tensor_tensor(tl[:, :], islo[:, :], XR[:, j, :, D], ALU.mult))
            wh.by(dve.scalar_tensor_tensor(out=wt[:, j, :], in0=islo[:, :], scalar=-1.0, in1=XR[:, j, :, D + 1],
                                           op0=ALU.add, op1=ALU.mult))
            ge(dve, wl, i1)
            ge(dve, wh, i1)
            wdone.by(dve.tensor_tensor(wt[:, j, :], tl[:, :], wt[:, j, :], ALU.subtract))

        if isinstance(i, int) and i == 0:
            incoming(0, 1, 0)
            loaded(dve, bt_in, 0, 0)
        else:
            loaded(dve, bt_in, i, j)
        i1, im = i + 1, i - 1
        for c in range(NCH):
            at = GU[(NCH * j + c) % 4]
            lin = UR[:, :] if c == 0 else at[:, FT:2 * FT]
            if c:
                chunk(dve, sil, c, i)
            else:
                ge(dve, ur, i1)
            if c >= 2:
                chunk(dve, hlo, c - 2, i)
            else:
                chunk(dve, hlo, c + 4, im)
            h32[c % 3].by(dve.scalar_tensor_tensor(out=H32[0:kr(c), c % 2, :], in0=lin,
                                                   scalar=BT[0:kr(c), j, NCH + c:NCH + c + 1], in1=SIL[0:kr(c), c % 2, :], op0=ALU.add, op1=ALU.mult))
            if c:
                low(c - 1)
        low(NCH - 1)
        if not (isinstance(i, int) and i == NTILE - 1):
            incoming(i1, i + 2, 1 - j)
        ge(dve, y_ps, i1)
        ge(dve, wdone, i1)
        loaded(dve, z_in, i, j, 2)
        for s in range(FS):
            last = dve.scalar_tensor_tensor(out=Z[:, j, s, :], in0=YP[s][:, 0:D], scalar=wt[:, j, s:s + 1],
                                            in1=Z[:, j, s, :], op0=ALU.mult, op1=ALU.add)
        yo.by(last)

    def pool_slot(pool, i, j):
        i1 = i + 1
        ge(pool, idone, i1)
        loaded(pool, sent, i - 1, 1 - j, 2)
        carry(pool, spare, carried, i * 2)
        for s in range(FS):
            z_in[j].by(pool.indirect_dma_start(Z[:, j, s, :], None, out,
                                               bass.IndirectOffsetOnAxis(idx[:, j, s:s + 1], 0),
                                               bounds_check=T - 1, oob_is_err=False))
        ge(pool, yo, i1)
        carry(pool, spare, carried, i * 2 + 1)
        for s in range(FS):
            sent[j].by(pool.indirect_dma_start(out, bass.IndirectOffsetOnAxis(idx[:, j, s:s + 1], 0),
                                               Z[:, j, s, :], None, bounds_check=T - 1, oob_is_err=False))

    def sp_load(sp, i, j, waits):
        def at(k):
            col = slice(i, i + 1) if isinstance(i, int) else bass.ds(i, 1)
            return table_i[0:1, k, col]

        row = sp.value_load(at(0), min_val=0, max_val=SPARE)
        if waits:
            n = i - 1
            ge(sp, xT_ps, n)
            ge(sp, wdone, n)
        xr_in[j].by(sp.dma_start(XR[:, j, :, :], xs_dram[bass.ds(row, FT), :].rearrange("(s p) w -> p s w", p=P)))
        e = sp.value_load(at(1), min_val=0, max_val=E - 1)
        new = sp.value_load(at(2), min_val=0, max_val=1)
        if waits:
            chunk(sp, gu, NCH - 1, i - 2)
        up_in[j].by(sp.dma_start(UP[:, j, :, :, :, :].rearrange("p a k b n -> p (a k b n)"),
                                 up_dram[bass.ds(e, 1)].rearrange("o p w -> p (o w)"), cond=new))
        if waits:
            chunk(sp, h32, NCH - 1, i - 2)
        bt_in[j].by(sp.dma_start(BT[:, j, :], bias[:, bass.ds(e, 1), :].rearrange("p o c -> p (o c)")))
        if waits:
            ge(sp, y_ps, n)
        dn_in[j].by(sp.dma_start(DN[:, j, :, :, :].rearrange("p a c d -> p (a c d)"),
                                 dn_dram[bass.ds(e, 1)].rearrange("o p w -> p (o w)"), cond=new))

    with nc.Block() as block:
        @block.sync
        def _(sp):
            first_in.wait(sp, 16 * 4)
            sp_load(sp, 0, 0, False)
            sp_load(sp, 1, 1, False)
            with sp.Fori(2, NTILE - 2, 2) as i:
                for j in range(2):
                    sp_load(sp, i + j if j else i, j, True)
            sp_load(sp, NTILE - 1, 0, True)

        @block.tensor
        def _(pe):
            run(pe, lambda i, j: pe_slot(pe, i, j))

        @block.scalar
        def _(act):
            run(act, lambda i, j: act_slot(act, i, j))

        @block.vector
        def _(dve):
            e_set.by(dve.memset(HT[32:64, 0, 0, :], 1.0))
            dve.memset(Z[:, :, :, :], 0.0)
            e_set.wait(dve, 1)
            run(dve, lambda i, j: dve_slot(dve, i, j))

        @block.gpsimd
        def _(pool):
            spared.by(pool.memset(spare[:, :], 0.0))
            spared.wait(pool, 1)
            run(pool, lambda i, j: pool_slot(pool, i, j))
            for i in (NTILE - 2, NTILE - 1):
                loaded(pool, sent, i, i % 2, 2)


class Beside:

    def __init__(self, ps, ident, const, biases, split):
        self.F0, self.F1, self.ident = ps["F0"], ps["F1"], ident
        self.const, self.biases, self.split = const, biases, split

    def act_loads(self, act, part, parts):
        for load in (self.const.loads(act) + self.biases.loads(act))[part::parts]:
            load()

    def pool_program(self, pool):
        self.biases.pool_program(pool)
        self.const.pool_program(pool)
        self.split(pool, lambda: self.const.pool_more(pool))
        self.const.pool_end(pool)

    def dve_program(self, dve, part):
        self.const.dve_program(dve, part)

    def sp_loads(self, sp, b):
        if b == 0:
            self.const.c_w.wait(sp, 16 * NBESIDE)
        if b < 2 * GT:
            self.const.projections(sp, 0, 0, (b,))

    def pe_end(self, pe):
        self.const.pe_end(pe, self.F0, self.ident)
        self.biases.pe_end(pe, self.F1, self.ident)

    def act_end(self, act):
        self.biases.act_end(act, self.F1)

    def dve_end(self, dve):
        self.const.dve_end(dve, self.F0)


def build(nc, io, out):
    with ExitStack() as ctx:
        def made(name, step=1):
            return Made(ctx.enter_context(nc.semaphore(name)), step)

        def dram(name, shape, dt=F32):
            return nc.dram_tensor(name, shape, dt).ap()

        def keep(name, shape, dt=F32):
            return ctx.enter_context(nc.sbuf_tensor(name, shape, dt))

        ps = {k: ctx.enter_context(nc.psum_tensor(k, [P, w], F32)) for k, w in
              (("Spair", 1024), ("Tpair", 1024), ("F0", 512), ("F1", 512), ("G", 512), ("O", 512))}
        xs_dram = dram("xs_dram", [E * CAP + FT, RW])
        up_dram = dram("up_dram", [E, P, UW], BF16)
        dn_dram = dram("dn_dram", [E, P, DW], BF16)
        ident = keep("ident", [P, P])
        table_i = keep("table_i", [P, 3, NTILE], I32)
        table_f = keep("table_f", [P, NTILE])
        const = DispatchConstants(nc, io, keep, made, xs_dram)
        biases = Biases(io, keep, made, const.c_w)
        with ExitStack() as phase:
            sb = lambda name, shape, dt=F32: phase.enter_context(nc.sbuf_tensor(name, shape, dt))
            const.temporaries(sb)
            biases.temporaries(sb)
            beside = Beside(ps, ident, const, biases,
                            lambda pool, between: split_weights(io, sb, made, pool, up_dram,
                                                                 dn_dram, between))
            setup_and_attention(nc, io, sb, made, dram, ps, ident, out, beside)
        UP = keep("UP", [P, 2, 2, KD, NBLK, P], BF16)
        DN = keep("DN", [P, 2, 2, NCH, D], BF16)
        first_in = made("first_in", 16)
        with ExitStack() as phase:
            sb = lambda name, shape, dt=F32: phase.enter_context(nc.sbuf_tensor(name, shape, dt))
            dispatch(nc, io, sb, made, dram, ps, ident, const, out, xs_dram, table_i, table_f,
                     lambda eng, g: load_first(eng, g, UP, DN, up_dram, dn_dram, first_in))
        with ExitStack() as phase:
            sb = lambda name, shape, dt=F32: phase.enter_context(nc.sbuf_tensor(name, shape, dt))
            experts(nc, io, sb, made, ps, ident, biases.bias, UP, DN, first_in, xs_dram, up_dram, dn_dram, table_i,
                    table_f, out)


_INS = ["x", "itok_B_0_2", "itok_B_0_6", "L0_cond_W1", "L0_cond_b1",
        "L0_cond_v", "L0_attn_Wq", "L0_attn_Wk", "L0_attn_Wv", "L0_attn_Wo",
        "L0_attn_W_down_kv", "L0_attn_W_up_k", "L0_attn_W_up_v", "L0_cond2_down_w", "L0_cond2_down_b",
        "L0_cond2_up_w", "L0_cond2_up_b", "L0_cond2_ln_g", "L0_cond2_ln_b", "L0_ffn_centroid",
        "L0_ffn_Wg", "L0_ffn_bg", "L0_ffn_W1", "L0_ffn_b1", "L0_ffn_W2",
        "L0_ffn_b2"]
_OUTS = [((64, 64, 256), "float32")]


def kernel(**inputs):
    import numpy as _np
    import concourse.bacc as _bacc
    from concourse import mybir as _mybir
    from concourse.bass_utils import run_bass_kernel_spmd as _run

    nc = _bacc.Bacc("TRN2", target_bir_lowering=False, num_devices=1)
    arrays, io = {}, {}
    for name in _INS:
        a = _np.ascontiguousarray(inputs[name])
        arrays[f"in_{name}_dram"] = a
        io[name] = nc.dram_tensor(f"in_{name}_dram", a.shape, _mybir.dt.from_np(a.dtype), kind="ExternalInput").ap()
    outs = [nc.dram_tensor(f"out_{i}_dram", shape, _mybir.dt.from_np(_np.dtype(dtype)), kind="ExternalOutput").ap()
            for i, (shape, dtype) in enumerate(_OUTS)]
    build(nc, io, outs[0].rearrange("b s d -> (b s) d"))
    r = _run(nc, [arrays], core_ids=[0])
    return r.results[0]["out_0_dram"]
```
